# Optimizing a Trainium2 kernel written in Bass

```python
import numpy as np
import jax
import jax.numpy as jnp

def _softmax(x, axis=-1):
    return jax.nn.softmax(x, axis=axis)
def _gelu(x):
    return jax.nn.gelu(x, approximate=True)
def _silu(x):
    return jax.nn.silu(x)
def _sigmoid(x):
    return jax.nn.sigmoid(x)
def _layernorm(x, axis=-1, eps=1e-5):
    m = jnp.mean(x, axis=axis, keepdims=True)
    v = jnp.var(x, axis=axis, keepdims=True)
    return (x - m) / jnp.sqrt(v + eps)
def _scatter_add(tgt, idx, src, axis=0):
    return tgt.at[idx].add(src)
def _segment_sum(src, seg, n):
    return jax.ops.segment_sum(src, seg, n)

kernel_name = 'mk_conv_preact_d2_conv_nchw96_8468e6'

def setup_inputs(seed: int = 0):
    np.random.seed(seed)
    _w = jnp.asarray
    def _rec_inputs():
        import jax
        import jax.numpy as jnp
        _gk = jax.random.key(seed)
        x = -0.0002221 + 1 * jax.random.normal(jax.random.fold_in(_gk, 1), (4, 96, 256, 256), jnp.float32)
        return x
    x = _rec_inputs()
    def _L0_conv_setup():
        import jax, jax.numpy as jnp
        import numpy as np
        DIM = 96
        GS = 8
        CS = 64
        TOPK = 3

        def _dwconv3x3(x, w, b):
            y = jax.lax.conv_general_dilated(x, w, window_strides=(1, 1), padding=((1, 1), (1, 1)), feature_group_count=x.shape[1], dimension_numbers=('NCHW', 'OIHW', 'NCHW'))
            return y + b[None, :, None, None]
        key = jax.random.key(seed)
        ks = jax.random.split(key, 12)
        B, C, H, W = (4, DIM, 256, 256)
        s = 0.02
        return {'x': jax.random.normal(ks[0], (B, C, H, W), jnp.float32), 'Wq': jax.random.normal(ks[1], (C, C), jnp.float32) * s, 'bq': jnp.zeros((C,), jnp.float32), 'Wk': jax.random.normal(ks[2], (C, C), jnp.float32) * s, 'bk': jnp.zeros((C,), jnp.float32), 'Wv': jax.random.normal(ks[3], (C, C), jnp.float32) * s, 'bv': jnp.zeros((C,), jnp.float32), 'Wp': jax.random.normal(ks[4], (C, C), jnp.float32) * s, 'bp': jnp.zeros((C,), jnp.float32), 'lepe_w': jax.random.normal(ks[5], (C, 1, 3, 3), jnp.float32) * s, 'lepe_b': jnp.zeros((C,), jnp.float32)}
    _L0_conv_all = _L0_conv_setup()
    _L0_conv_in = {k: v for k, v in _L0_conv_all.items() if k in ('Wq', 'bq', 'Wk', 'bk', 'Wv', 'bv', 'Wp', 'bp', 'lepe_w', 'lepe_b', )}
    del _L0_conv_all

    def _L1_conv_setup():
        import jax, jax.numpy as jnp
        import numpy as np
        key = jax.random.key(seed)
        ks = jax.random.split(key, 8)
        B, C, H, W = (4, 96, 128, 128)
        K, N, R = (2, 1, 6)
        f = jax.random.normal
        return {'x': f(ks[0], (B, C, H, W), jnp.float32), 'in_proj_w': f(ks[1], (2 * C, C), jnp.float32) * 0.05, 'conv_w': f(ks[2], (C, 1, 3, 3), jnp.float32) * 0.1, 'conv_b': f(ks[3], (C,), jnp.float32) * 0.02, 'x_proj_w': f(ks[4], (K, R + 2 * N, C), jnp.float32) * 0.05, 'dt_proj_w': jax.random.uniform(ks[5], (K, C, R), jnp.float32) * 0.1, 'dt_proj_b': jax.random.uniform(ks[6], (K, C), jnp.float32) * 0.1, 'A_logs': jnp.zeros((K * C, N), jnp.float32), 'Ds': jnp.ones((K * C,), jnp.float32), 'out_norm_w': jnp.ones((C,), jnp.float32), 'out_norm_b': jnp.zeros((C,), jnp.float32), 'out_proj_w': f(ks[7], (C, C), jnp.float32) * 0.05, 'scale_w': jnp.ones((1, C, 1, 1), jnp.float32)}
    _L1_conv_all = _L1_conv_setup()
    _L1_conv_in = {k: v for k, v in _L1_conv_all.items() if k in ('in_proj_w', 'conv_w', 'conv_b', 'x_proj_w', 'dt_proj_w', 'dt_proj_b', 'A_logs', 'Ds', 'out_norm_w', 'out_norm_b', 'out_proj_w', 'scale_w', )}
    del _L1_conv_all

    return {
        "x": x,
        "L0_conv_Wq": _L0_conv_in["Wq"],
        "L0_conv_bq": _L0_conv_in["bq"],
        "L0_conv_Wk": _L0_conv_in["Wk"],
        "L0_conv_bk": _L0_conv_in["bk"],
        "L0_conv_Wv": _L0_conv_in["Wv"],
        "L0_conv_bv": _L0_conv_in["bv"],
        "L0_conv_Wp": _L0_conv_in["Wp"],
        "L0_conv_bp": _L0_conv_in["bp"],
        "L0_conv_lepe_w": _L0_conv_in["lepe_w"],
        "L0_conv_lepe_b": _L0_conv_in["lepe_b"],
        "L1_conv_in_proj_w": _L1_conv_in["in_proj_w"],
        "L1_conv_conv_w": _L1_conv_in["conv_w"],
        "L1_conv_conv_b": _L1_conv_in["conv_b"],
        "L1_conv_x_proj_w": _L1_conv_in["x_proj_w"],
        "L1_conv_dt_proj_w": _L1_conv_in["dt_proj_w"],
        "L1_conv_dt_proj_b": _L1_conv_in["dt_proj_b"],
        "L1_conv_A_logs": _L1_conv_in["A_logs"],
        "L1_conv_Ds": _L1_conv_in["Ds"],
        "L1_conv_out_norm_w": _L1_conv_in["out_norm_w"],
        "L1_conv_out_norm_b": _L1_conv_in["out_norm_b"],
        "L1_conv_out_proj_w": _L1_conv_in["out_proj_w"],
        "L1_conv_scale_w": _L1_conv_in["scale_w"],
    }

def reference(x, L0_conv_Wq, L0_conv_bq, L0_conv_Wk, L0_conv_bk, L0_conv_Wv, L0_conv_bv, L0_conv_Wp, L0_conv_bp, L0_conv_lepe_w, L0_conv_lepe_b, L1_conv_in_proj_w, L1_conv_conv_w, L1_conv_conv_b, L1_conv_x_proj_w, L1_conv_dt_proj_w, L1_conv_dt_proj_b, L1_conv_A_logs, L1_conv_Ds, L1_conv_out_norm_w, L1_conv_out_norm_b, L1_conv_out_proj_w, L1_conv_scale_w):
    import jax
    import jax.numpy as jnp
    def _L0_conv_ref(x, Wq, bq, Wk, bk, Wv, bv, Wp, bp, lepe_w, lepe_b):
        import jax, jax.numpy as jnp
        import numpy as np
        DIM = 96
        GS = 8
        CS = 64
        TOPK = 3

        def _dwconv3x3(x, w, b):
            y = jax.lax.conv_general_dilated(x, w, window_strides=(1, 1), padding=((1, 1), (1, 1)), feature_group_count=x.shape[1], dimension_numbers=('NCHW', 'OIHW', 'NCHW'))
            return y + b[None, :, None, None]
        B, C, H, W = x.shape
        gh, gw = (H // GS, W // GS)
        N = B * gh * gw
        itr = N // CS
        P = GS * GS
        scale = C ** (-0.5)
        dsx = x.reshape(B, C, gh, GS, gw, GS).max(axis=(3, 5))
        dsx = dsx.transpose(0, 2, 3, 1).reshape(itr, CS, C)
        sim = jnp.einsum('icd,jed->icje', dsx, dsx)
        blk_s, blk_i = jax.lax.top_k(sim, TOPK)
        blk_gi = blk_i + (jnp.arange(itr) * CS)[None, None, :, None]
        cat_s = blk_s.reshape(itr, CS, itr * TOPK)
        cat_i = blk_gi.reshape(itr, CS, itr * TOPK)
        fin_s, fi = jax.lax.top_k(cat_s, TOPK)
        fin_i = jnp.take_along_axis(cat_i, fi, axis=-1)
        sim_score = fin_s.reshape(N, TOPK)
        sim_index = fin_i.reshape(N, TOPK)
        xw = x.transpose(0, 2, 3, 1).reshape(B, gh, GS, gw, GS, C)
        xw = xw.transpose(0, 1, 3, 2, 4, 5).reshape(N, P, C)
        w = jax.nn.softmax(sim_score, axis=-1)
        neighbors = xw[sim_index]
        context = jnp.einsum('nk,nkpc->npc', w, neighbors)
        q = xw @ Wq + bq
        k = context @ Wk + bk
        v = context @ Wv + bv
        x_img = xw.transpose(0, 2, 1).reshape(N, C, GS, GS)
        lepe = _dwconv3x3(x_img, lepe_w, lepe_b).reshape(N, C, P).transpose(0, 2, 1)
        attn = jax.nn.softmax(jnp.einsum('npc,nqc->npq', q, k) * scale, axis=-1)
        out = jnp.einsum('npq,nqc->npc', attn, v) + lepe
        out = out @ Wp + bp
        out = out.reshape(B, gh, gw, GS, GS, C)
        out = out.transpose(0, 5, 1, 3, 2, 4).reshape(B, C, H, W)
        return out

    def _L1_conv_ref(x, in_proj_w, conv_w, conv_b, x_proj_w, dt_proj_w, dt_proj_b, A_logs, Ds, out_norm_w, out_norm_b, out_proj_w, scale_w):
        import jax, jax.numpy as jnp
        import numpy as np
        B, C, H, W = x.shape
        K, N = (dt_proj_w.shape[0], A_logs.shape[1])
        R = dt_proj_w.shape[2]
        L = H * W
        xz = jnp.einsum('oc,bchw->bohw', in_proj_w, x)
        xc, z = (xz[:, :C], xz[:, C:])
        xc = jax.lax.conv_general_dilated(xc, conv_w, (1, 1), 'SAME', dimension_numbers=('NCHW', 'OIHW', 'NCHW'), feature_group_count=C) + conv_b[None, :, None, None]
        xc = jax.nn.silu(xc)
        u = xc.reshape(B, C, L)
        xs = jnp.stack([u, u[:, :, ::-1]], axis=1)
        x_dbl = jnp.einsum('bkcl,kdc->bkdl', xs, x_proj_w)
        dts, Bs, Cs = (x_dbl[:, :, :R], x_dbl[:, :, R:R + N], x_dbl[:, :, R + N:])
        delta = jax.nn.softplus(jnp.einsum('bkrl,kcr->bkcl', dts, dt_proj_w) + dt_proj_b[None, :, :, None])
        A = -jnp.exp(A_logs).reshape(K, C, N)
        dA = jnp.exp(delta[..., None] * A[None, :, :, None, :])
        dBu = (delta * xs)[..., None] * jnp.swapaxes(Bs, -1, -2)[:, :, None]

        def step(h, inp):
            dA_l, dBu_l, C_l = inp
            h = dA_l * h + dBu_l
            y = jnp.einsum('bkcn,bkn->bkc', h, C_l)
            return (h, y)
        h0 = jnp.zeros((B, K, C, N), x.dtype)
        _, ys = jax.lax.scan(step, h0, (jnp.moveaxis(dA, 3, 0), jnp.moveaxis(dBu, 3, 0), jnp.moveaxis(Cs, 3, 0)))
        ys = jnp.moveaxis(ys, 0, 3) + Ds.reshape(K, C)[None, :, :, None] * xs
        y = (ys[:, 0] + ys[:, 1, :, ::-1]).reshape(B, C, H, W)
        mu = y.mean(1, keepdims=True)
        var = y.var(1, keepdims=True)
        y = (y - mu) * jax.lax.rsqrt(var + 1e-05)
        y = y * out_norm_w[None, :, None, None] + out_norm_b[None, :, None, None]
        y = y * jax.nn.silu(z)
        out = jnp.einsum('oc,bchw->bohw', out_proj_w, y)
        return scale_w * out

    def _gn(v, G=32, eps=1e-5):
        B_, C_, H_, W_ = v.shape
        g = v.reshape(B_, G, C_ // G, H_, W_)
        m = jnp.mean(g, axis=(2, 3, 4), keepdims=True)
        s = jnp.var(g, axis=(2, 3, 4), keepdims=True)
        return ((g - m) / jnp.sqrt(s + eps)).reshape(v.shape)

    def _ln_c(v, eps=1e-6):
        m = jnp.mean(v, axis=1, keepdims=True)
        s = jnp.var(v, axis=1, keepdims=True)
        return (v - m) / jnp.sqrt(s + eps)

    def _ln_t(v, eps=1e-5):
        m = jnp.mean(v, axis=-1, keepdims=True)
        s = jnp.var(v, axis=-1, keepdims=True)
        return (v - m) / jnp.sqrt(s + eps)

    def _to_tokens(v):
        B_, C_, H_, W_ = v.shape
        return v.reshape(B_, C_, H_ * W_).transpose(0, 2, 1)
    def _from_tokens(t, like):
        B_, C_, H_, W_ = like.shape
        return t.transpose(0, 2, 1).reshape(B_, C_, H_, W_)

    x = x + _L0_conv_ref(_gn(x), L0_conv_Wq, L0_conv_bq, L0_conv_Wk, L0_conv_bk, L0_conv_Wv, L0_conv_bv, L0_conv_Wp, L0_conv_bp, L0_conv_lepe_w, L0_conv_lepe_b)
    x = x + _L1_conv_ref(_gn(x), L1_conv_in_proj_w, L1_conv_conv_w, L1_conv_conv_b, L1_conv_x_proj_w, L1_conv_dt_proj_w, L1_conv_dt_proj_b, L1_conv_A_logs, L1_conv_Ds, L1_conv_out_norm_w, L1_conv_out_norm_b, L1_conv_out_proj_w, L1_conv_scale_w)
    return x


_drawn_inputs = setup_inputs


def setup_inputs(seed=0):
    import zlib

    import numpy as np

    out = dict(_drawn_inputs(seed))
    spreads = {'L0_conv_bq': (0.0, 0.8),
     'L0_conv_bk': (0.0, 2.0),
     'L0_conv_bv': (0.0, 0.372),
     'L0_conv_bp': (0.0, 0.1),
     'L0_conv_lepe_b': (0.0, 0.343),
     'L1_conv_A_logs': (0.0, 2.0),
     'L1_conv_Ds': (1.0, 0.6),
     'L1_conv_out_norm_w': (1.0, 0.6),
     'L1_conv_out_norm_b': (0.0, 0.635),
     'L1_conv_scale_w': (1.0, 0.6)}
    factors = {'L0_conv_Wq': 8.0,
     'L0_conv_Wk': 8.0,
     'L0_conv_Wv': 8.0,
     'L0_conv_lepe_w': 5.027,
     'L1_conv_conv_b': 3.102,
     'L1_conv_x_proj_w': 48.285,
     'L1_conv_dt_proj_w': 64.0,
     'L1_conv_dt_proj_b': 64.0}
    for name, (base, spread) in spreads.items():
        noise = np.random.default_rng([zlib.crc32(name.encode()), seed]).standard_normal(out[name].shape)
        drawn = base * np.exp(spread * noise) if base else spread * noise
        out[name] = jnp.asarray(drawn.astype(out[name].dtype))
    for name, factor in factors.items():
        out[name] = (out[name] * factor).astype(out[name].dtype)
    return out
```

```python
from contextlib import ExitStack, contextmanager

import numpy as np

import concourse.bass as bass
from concourse import mybir

F32 = mybir.dt.float32
U32 = mybir.dt.uint32
ALU = mybir.AluOpType
ACT = mybir.ActivationFunctionType
AX = mybir.AxisListType

B, C, H, W = 4, 96, 256, 256
GS = 8
P = GS * GS
GH, GW = H // GS, W // GS
NW = B * GH * GW
NT = B * GH
RT = GS * W
PAIRS = GW // 2
TOPK = 3
L = H * W
R = 6
NX = R + 2
SCALE = float(C) ** -0.5
GEPS = 1e-5


def unit_constants():
    ident = np.eye(128, dtype=np.float32)
    pos = np.arange(P)
    shifts = np.zeros((128, 9, 128), np.float32)
    for t in range(9):
        dy, dx = t // 3 - 1, t % 3 - 1
        r, c = pos // GS + dy, pos % GS + dx
        ok = (r >= 0) & (r < GS) & (c >= 0) & (c < GS)
        for w in range(2):
            shifts[w * P + (r * GS + c)[ok], t, w * P + pos[ok]] = 1.0
    rows = np.zeros((CROWS + 2, 3, CROWS), np.float32)
    for dy in range(3):
        rows[np.arange(CROWS) + dy, dy, np.arange(CROWS)] = 1.0
    group = np.kron(np.eye(C // 3), np.ones((3, 3))).astype(np.float32) / np.float32(3)
    centre = (np.eye(C) - 1.0 / C).astype(np.float32)
    mean = np.full((C, C), 1.0 / C, np.float32)
    return dict(ident=ident, shifts=shifts, rows=rows, group=group, centre=centre, mean=mean)


CROWS = 86
CTILES = 3


class Core:

    def __init__(self, nc, ctx, dram, passed=None):
        self.nc, self.ctx, self.d = nc, ctx, dram
        self.sems = []
        self.passed = passed if passed is not None else ctx.enter_context(nc.semaphore("passed"))

    def sb(self, name, shape, dt=F32):
        return self.ctx.enter_context(self.nc.sbuf_tensor(name, shape, dt))

    def ps(self, name, shape, dt=F32):
        return self.ctx.enter_context(self.nc.psum_tensor(name, shape, dt))

    def sem(self, name):
        self.sems.append(self.nc.alloc_semaphore(name))
        return self.sems[-1]

    def apart(self, eng):
        eng.sem_inc(self.passed, 1)

    @contextmanager
    def stage(self):
        with ExitStack() as ctx:
            stage = Core(self.nc, ctx, self.d, self.passed)
            yield stage
            self.nc.clear_and_free_semaphores(stage.sems)
            self.nc.all_engine_barrier()


def setup_weights(core, w):
    nc, d = core.nc, core.d
    with core.stage() as k:
        wq_t = k.sb("wq_t", [C, C])
        wk_t = k.sb("wk_t", [C, C + 1])
        wv_t = k.sb("wv_t", [C, C])
        bq = k.sb("bq", [C, 1])
        bvl = k.sb("bvl", [C, 2])
        bp = k.sb("bp", [1, C])
        crow = k.sb("crow", [1, C])
        bsum = k.sb("bsum", [C, 1])
        xp = k.sb("xp", [R, 2, C])
        dtw = k.sb("dtw", [R, 2, C])
        xpt = k.sb("xpt", [C, 2 * NX])
        alog = k.sb("alog", [C, 2])
        aexp = k.sb("aexp", [C, 2])
        ds = k.sb("ds", [C, 2])
        p1 = k.ps("setup_p1", [C, 512])
        p2 = k.ps("setup_p2", [C, 512])
        p3 = k.ps("setup_p3", [C + 1, 512])
        loaded, summed, folded, stored, powed, crow_ready, row_in = (
            k.sem(f"setup_{n}") for n in ("loaded", "summed", "folded", "stored", "powed", "crow", "rowin"))
        loads = [
            (wq_t[:], d["wq_t"]), (wk_t[:], d["wk_t_bk"]), (wv_t[:], d["wv_t"]), (bq[:], d["bq"]),
            (bvl[:], d["bv_lb"]), (bp[:], d["bp"]), (w["wp1"][0:C, :], d["wp"]), (w["ident"][:], d["ident"]),
            (w["group"][:], d["group"]), (w["centre"][:], d["centre"]), (w["mean"][:], d["mean"]),
            (xp[:], d["xp_dt"]), (dtw[:], d["dtw_t"]), (xpt[:], d["xp_t"]), (alog[:], d["alog_t"]), (ds[:], d["ds_t"]),
            (w["dtb"][:], d["dtb_t"]), (w["inw"][:], d["in_w_t"]), (w["wo"][:], d["wo_t"]),
            (w["onwb"][:], d["onwb"]), (w["scale"][:], d["scale_w"]),
            (w["lepe"][:], d["lepe_w"].partition_broadcast(128)),
        ]
        with nc.Block() as block:
            @block.sync
            def _(sp):
                for to, src in loads:
                    sp.dma_start(to, src).then_inc(loaded, 16)
                sp.wait_ge(crow_ready, 1)
                sp.dma_start(w["wp1"][C:C + 1, :], crow[:]).then_inc(row_in, 16)
                sp.wait_ge(row_in, 16)

            @block.vector
            def _(dve):
                dve.wait_ge(loaded, 16 * len(loads))
                nc.vector.tensor_tensor(bsum[:], bvl[:, 0:1], bvl[:, 1:2], ALU.add).then_inc(summed, 1)
                nc.vector.tensor_tensor(w["dsum"][:], ds[:, 0:1], ds[:, 1:2], ALU.add)
                for s in range(2):
                    for r in range(2):
                        nc.vector.tensor_copy(w["bc"][:, s, r, :],
                                              xpt[:, s * NX + R + r:s * NX + R + r + 1].to_broadcast([C, C]))
                dve.wait_ge(folded, 1)
                nc.vector.tensor_copy(w["g"][:], p1[:, 0:C + 1])
                nc.vector.tensor_copy(w["wvp"][:], p1[:, 128:128 + C])
                nc.vector.tensor_copy(w["wd"][:, 0, :], p1[:, 256:256 + C])
                nc.vector.tensor_copy(w["wd"][:, 1, :], p1[:, 384:384 + C])
                nc.vector.tensor_copy(w["gb"][:], p3[:, 0:1])
                nc.vector.tensor_tensor(crow[:], p2[0:1, 0:C], bp[:], ALU.add).then_inc(crow_ready, 1)
                dve.wait_ge(powed, 1)
                nc.vector.tensor_scalar(w["nega"][:], aexp[:], -1.0, None, ALU.mult).then_inc(stored, 1)

            @block.scalar
            def _(act):
                act.wait_ge(loaded, 16 * len(loads))
                nc.scalar.activation(aexp[:], alog[:], ACT.Exp).then_inc(powed, 1)

            @block.tensor
            def _(pe):
                pe.wait_ge(loaded, 16 * len(loads))
                mm = lambda o, a, b: nc.tensor.matmul(o, a, b, start=True, stop=True)
                mm(p1[:, 0:C + 1], wq_t[:], wk_t[:])
                mm(p1[:, 128:128 + C], wv_t[:], w["wp1"][0:C, :])
                mm(p1[:, 256:256 + C], xp[:, 0, :], dtw[:, 0, :])
                mm(p1[:, 384:384 + C], xp[:, 1, :], dtw[:, 1, :])
                mm(p3[:, 0:1], wk_t[:], bq[:])
                pe.wait_ge(summed, 1)
                mm(p2[0:1, 0:C], bsum[:], w["wp1"][0:C, :]).then_inc(folded, 1)


def build_window_convs(core, w, wconv):
    nc, d = core.nc, core.d
    GROUP = 8
    with core.stage() as k:
        shifts = k.sb("shifts", [128, 9, 128])
        in_ = k.sem("wc_in")
        built = k.sem("wc_built")
        with nc.Block() as block:
            @block.sync
            def _(sp):
                sp.dma_start(shifts[:], d["shifts"]).then_inc(in_, 16)

            @block.vector
            def _(dve):
                dve.wait_ge(in_, 16)
                with dve.Fori(0, C // GROUP) as g:
                    for t in range(9):
                        for j in range(GROUP):
                            to = wconv[:, bass.ds(g * (GROUP * 128) + j * 128, 128)]
                            tap = w["lepe"][:, bass.ds(g * (GROUP * 9) + (j * 9 + t), 1)]
                            if t == 0:
                                last = nc.vector.tensor_scalar(to, shifts[:, t, :], tap, None, ALU.mult)
                            else:
                                last = nc.vector.scalar_tensor_tensor(to, shifts[:, t, :], tap, to,
                                                                      ALU.mult, ALU.add)
                        last.then_inc(built, 1)
                        dve.wait_ge(built, g * 9 + (t + 1))


def image_stats(core, stats, pooled):
    nc, d = core.nc, core.d
    x = d["x"].rearrange("b c (g r) w -> c b g (r w)", r=GS)
    SLOTS = 4
    with core.stage() as k:
        xin = k.sb("a_x", [C, SLOTS, RT])
        x_in = [k.sem(f"a_x_in{s}") for s in range(SLOTS)]
        x_free = k.sem("a_x_free")
        with nc.Block() as block:
            @block.sync
            def _(sp):
                with sp.Fori(0, B) as b:
                    with sp.Fori(0, GH // SLOTS) as g:
                        for s in range(SLOTS):
                            sp.wait_ge(x_free, b * GH + g * SLOTS + (s + 1))
                            sp.dma_start(xin[:, s, :], x[:, b, g * SLOTS + s, :]).then_inc(x_in[s], 16)

            @block.vector
            def _(dve):
                dve.sem_inc(x_free, SLOTS)
                with dve.Fori(0, NT // SLOTS) as g:
                    for s in range(SLOTS):
                        dve.wait_ge(x_in[s], g * 16 + 16)
                        for q in range(RT // 512):
                            nc.vector.bn_stats(
                                stats[:, bass.ds(g * (SLOTS * 24) + (s * 24 + q * 6), 6)],
                                xin[:, s, q * 512:(q + 1) * 512])
                        nc.vector.tensor_reduce(
                            pooled[:, bass.ds(g * (SLOTS * GW) + s * GW, GW)],
                            xin[:, s, :].rearrange("c (r w k) -> c w r k", r=GS, k=GS),
                            AX.XY, ALU.max).then_inc(x_free, 1)


def group_coefficients(core, w, name, stats, gscale, gbias):
    nc = core.nc
    with core.stage() as k:
        mv = k.sb(name + "mv", [C, B, 2])
        s2 = k.sb(name + "s2", [C, 2, B])
        gs = k.sb(name + "gs", [C, 2, B])
        var = k.sb(name + "var", [C, B])
        std = k.sb(name + "std", [C, B])
        pg = k.ps(name + "pg", [C, 512])
        step, grouped, rooted = k.sem(name + "step"), k.sem(name + "grouped"), k.sem(name + "rooted")
        per = NT // B * 24
        with nc.Block() as block:
            @block.vector
            def _(dve):
                for b in range(B):
                    last = nc.vector.bn_aggr(mv[:, b, :], stats[:, b * per:(b + 1) * per])
                last.then_inc(step, 1)
                dve.wait_ge(step, 1)
                nc.vector.tensor_tensor(var[:], mv[:, :, 0], mv[:, :, 0], ALU.mult)
                nc.vector.tensor_copy(s2[:, 0, :], mv[:, :, 0]).then_inc(step, 1)
                dve.wait_ge(step, 2)
                nc.vector.tensor_tensor(s2[:, 1, :], var[:], mv[:, :, 1], ALU.add).then_inc(step, 1)
                dve.wait_ge(grouped, 1)
                nc.vector.tensor_copy(gs[:], pg[:, 0:2 * B].rearrange("c (a b) -> c a b", a=2)).then_inc(step, 1)
                dve.wait_ge(step, 4)
                nc.vector.tensor_tensor(var[:], gs[:, 0, :], gs[:, 0, :], ALU.mult).then_inc(step, 1)
                dve.wait_ge(step, 5)
                nc.vector.tensor_tensor(std[:], gs[:, 1, :], var[:], ALU.subtract).then_inc(step, 1)
                dve.wait_ge(step, 6)
                nc.vector.tensor_scalar(var[:], std[:], GEPS, None, ALU.add).then_inc(step, 1)
                dve.wait_ge(rooted, 1)
                nc.vector.reciprocal(gscale[:], std[:]).then_inc(step, 1)
                dve.wait_ge(step, 8)
                nc.vector.tensor_tensor(std[:], gscale[:], gscale[:], ALU.mult).then_inc(step, 1)
                dve.wait_ge(step, 9)
                nc.vector.scalar_tensor_tensor(mv[:, :, 0], std[:], -0.5, var[:], ALU.mult, ALU.mult).then_inc(step, 1)
                dve.wait_ge(step, 10)
                nc.vector.scalar_tensor_tensor(gscale[:], mv[:, :, 0], 1.5, gscale[:], ALU.add, ALU.mult
                                               ).then_inc(step, 1)
                dve.wait_ge(step, 11)
                nc.vector.scalar_tensor_tensor(gbias[:], gs[:, 0, :], -1.0, gscale[:], ALU.mult, ALU.mult)

            @block.tensor
            def _(pe):
                pe.wait_ge(step, 3)
                nc.tensor.matmul(pg[:, 0:2 * B], w["group"][:], s2[:].rearrange("c a b -> c (a b)"),
                                 start=True, stop=True).then_inc(grouped, 1)

            @block.scalar
            def _(act):
                act.wait_ge(step, 7)
                nc.scalar.activation(std[:], var[:], ACT.Sqrt).then_inc(rooted, 1)


def top_windows(core, pooled, gscale, gbias, nbr_w, nbr_i):
    nc = core.nc
    T = NW // 128
    HALF = 1024
    with core.stage() as k:
        score = k.sb("score", [128, 2, NW])
        own = k.sb("own", [C, 2, 128])
        top = k.sb("top", [128, 2, 8])
        place = k.sb("place", [128, 2, 8], U32)
        tops = k.sb("tops", [128, T, 8])
        places = k.sb("places", [128, T, 8], U32)
        diff = k.sb("diff", [128, T, TOPK])
        ex = k.sb("ex", [128, T, TOPK])
        tot = k.sb("tot", [128, T])
        rtot = k.sb("rtot", [128, T])
        ps = [k.ps(f"sim{i}", [128, HALF]) for i in range(4)]
        normed, own_ready, sim, copied, step, kept, exped, fin = (
            k.sem("b_" + n) for n in ("normed", "own_ready", "sim", "copied", "step", "kept", "exped", "fin"))
        Q = NW // HALF
        with nc.Block() as block:
            @block.gpsimd
            def _(pool):
                pool.wait_ge(normed, 1)
                with pool.Fori(0, T // 2) as i:
                    for u in range(2):
                        pool.wait_ge(sim, (i * 2 + u) * Q)
                        nc.gpsimd.tensor_copy(own[:, u, :], pooled[:, bass.ds((i * 2 + u) * 128, 128)]
                                              ).then_inc(own_ready, 1)

            @block.tensor
            def _(pe):
                pe.sem_inc(sim, Q)
                pe.wait_ge(normed, 1)
                with pe.Fori(0, T // 2) as i:
                    for u in range(2):
                        pe.wait_ge(own_ready, i * 2 + (u + 1))
                        for q in range(Q):
                            pe.wait_ge(copied, (i * 2 + u) * Q + q)
                            for h in range(2):
                                mm = nc.tensor.matmul(ps[q][:, h * 512:(h + 1) * 512], own[:, u, :],
                                                      pooled[:, q * HALF + h * 512:q * HALF + (h + 1) * 512],
                                                      start=True, stop=True)
                            mm.then_inc(sim, 1)

            @block.scalar
            def _(act):
                act.sem_inc(copied, Q - 1)
                act.sem_inc(kept, 2)
                with act.Fori(0, T // 2) as i:
                    for u in range(2):
                        act.wait_ge(kept, i * 2 + (u + 1))
                        for q in range(Q):
                            act.wait_ge(sim, (i * 2 + u) * Q + (q + 1 + Q))
                            nc.scalar.copy(score[:, u, q * HALF:(q + 1) * HALF], ps[q][:]).then_inc(copied, 1)
                act.wait_ge(step, 1)
                nc.scalar.activation(ex[:], diff[:], ACT.Exp).then_inc(exped, 1)

            @block.vector
            def _(dve):
                for b in range(B):
                    sl = pooled[:, b * GH * GW:(b + 1) * GH * GW]
                    last = nc.vector.tensor_scalar(sl, sl, gscale[:, b:b + 1], gbias[:, b:b + 1],
                                                   ALU.mult, ALU.add)
                last.then_inc(normed, 1)
                with dve.Fori(0, T // 2) as i:
                    for u in range(2):
                        dve.wait_ge(copied, (i * 2 + u) * Q + (2 * Q - 1))
                        core.apart(dve)
                        nc.vector.max(top[:, u, :], score[:, u, :]).then_inc(fin, 1)
                        dve.wait_ge(fin, (i * 2 + u) * 2 + 1)
                        core.apart(dve)
                        nc.vector.max_index(place[:, u, :], top[:, u, :], score[:, u, :]).then_inc(fin, 1)
                        dve.wait_ge(fin, (i * 2 + u) * 2 + 2)
                        nc.vector.tensor_copy(tops[:, i * 2 + u, :], top[:, u, :])
                        nc.vector.tensor_copy(places[:, i * 2 + u, :], place[:, u, :]).then_inc(kept, 1)
                dve.wait_ge(kept, T + 2)
                nc.vector.tensor_tensor(diff[:], tops[:, :, 0:TOPK], tops[:, :, 0:1].to_broadcast([128, T, TOPK]),
                                        ALU.subtract).then_inc(step, 1)
                nc.vector.tensor_copy(nbr_i[:], places[:, :, 0:TOPK])
                dve.wait_ge(exped, 1)
                nc.vector.tensor_reduce(tot[:], ex[:], AX.X, ALU.add).then_inc(step, 1)
                dve.wait_ge(step, 2)
                nc.vector.reciprocal(rtot[:], tot[:]).then_inc(step, 1)
                dve.wait_ge(step, 3)
                nc.vector.tensor_tensor(nbr_w[:], ex[:], rtot[:].unsqueeze(2).to_broadcast([128, T, TOPK]), ALU.mult)


def window_convs(core, w, wconv, gscale, gbias):
    nc, d = core.nc, core.d
    x = d["x"].rearrange("b c (g r) w -> c b g (r w)", r=GS)
    part = d["part"]
    xg = d["xg"].rearrange("(t n) (c s) -> c t n s", n=GW, c=C)
    Q = 4
    M = GH // Q
    TG = Q * PAIRS // 4
    MG = 12
    with core.stage() as k:
        xr = k.sb("l_xr", [C, Q, RT])
        xn = k.sb("l_xn", [C, Q, GW, P])
        xt = k.sb("l_xt", [128, Q * PAIRS, C])
        lt = k.sb("l_lt", [128, Q * PAIRS, C])
        lc = k.sb("l_lc", [C + 1, 2, 512])
        coef = k.sb("l_coef", [C, 2])
        coef_set = k.sem("l_coef_set")
        pt = [k.ps(f"l_pt{i}", [128, 512]) for i in range(2)]
        pm = [k.ps(f"l_pm{i}", [128, 8, Q * PAIRS]) for i in range(2)]
        pb = [k.ps(f"l_pb{i}", [C, 512]) for i in range(2)]
        pw = [k.ps(f"l_pw{i}", [C, 8, GS, GS]) for i in range(2)]
        x_in = [k.sem(f"l_x_in{q}") for q in range(Q)]
        xg_out = [k.sem(f"l_xg_out{q}") for q in range(Q)]
        part_out = [k.sem(f"l_part_out{q}") for q in range(Q)]
        xn_ready, turned, turned_out, conved, conved_dve, conved_act, back, back_out, projected, added, ones = (
            k.sem("l_" + n) for n in ("xn_ready", "turned", "turned_out", "conved", "conved_dve", "conved_act",
                                      "back", "back_out", "projected", "added", "ones"))

        def conv_out(copy, g):
            return copy(lt[:, :, g * 8:(g + 1) * 8].rearrange("p n c -> p c n"), pm[g % 2][:])

        with nc.Block() as block:
            @block.sync
            def _(sp):
                with sp.Fori(0, B) as b:
                    with sp.Fori(0, M) as m:
                        j = b * M + m
                        for q in range(Q):
                            sp.wait_ge(part_out[q], j * 16)
                            sp.dma_start(xr[:, q, :], x[:, b, m * Q + q, :]).then_inc(x_in[q], 16)
                        for q in range(Q):
                            sp.wait_ge(xn_ready, j * Q + (q + 1))
                            sp.dma_start(xg[:, j * Q + q, :, :], xn[:, q, :, :]).then_inc(xg_out[q], 16)
                for q in range(Q):
                    sp.wait_ge(xg_out[q], B * M * 16)

            @block.scalar
            def _(act):
                act.sem_inc(back_out, 2)
                with act.Fori(0, B) as b:
                    nc.scalar.copy(coef[:, 0:1], gscale[:, bass.ds(b, 1)])
                    nc.scalar.copy(coef[:, 1:2], gbias[:, bass.ds(b, 1)]).then_inc(coef_set, 1)
                    act.wait_ge(coef_set, b + 1)
                    with act.Fori(0, M) as m:
                        j = b * M + m
                        for q in range(Q):
                            act.wait_ge(x_in[q], j * 16 + 16)
                            act.wait_ge(xg_out[q], j * 16)
                            nc.scalar.activation(
                                xn[:, q, :, :].rearrange("c n (r k) -> c n r k", r=GS),
                                xr[:, q, :].rearrange("c (r n k) -> c n r k", r=GS, k=GS), ACT.Identity,
                                scale=coef[:, 0:1], bias=coef[:, 1:2]).then_inc(xn_ready, 1)
                        for g in range(1, MG, 2):
                            act.wait_ge(conved, j * MG + (g + 1))
                            conv_out(nc.scalar.copy, g).then_inc(conved_act, 1)
                        for g in range(TG):
                            act.wait_ge(back, j * TG + (g + 1))
                            if g == 0:
                                act.wait_ge(ones, 1)
                            nc.scalar.copy(lc[0:C, g % 2, :], pb[g % 2][:]).then_inc(back_out, 1)

            @block.vector
            def _(dve):
                dve.sem_inc(turned_out, 2)
                dve.sem_inc(added, 2)
                nc.vector.memset(lc[C:C + 1, :, :], 1.0).then_inc(ones, 1)
                with dve.Fori(0, B * M) as j:
                    for g in range(TG):
                        dve.wait_ge(turned, j * TG + (g + 1))
                        nc.vector.tensor_copy(xt[:, g * 4:(g + 1) * 4, :],
                                              pt[g % 2][:, 0:4 * C].rearrange("p (n c) -> p n c", n=4)
                                              ).then_inc(turned_out, 1)
                    for g in range(0, MG, 2):
                        dve.wait_ge(conved, j * MG + (g + 1))
                        conv_out(nc.vector.tensor_copy, g).then_inc(conved_dve, 1)
                    for g in range(TG):
                        q, s = g // 4, g % 4
                        dve.wait_ge(projected, j * TG + (g + 1))
                        res = xr[:, q, :].rearrange("c (r n k) -> c n r k", r=GS, k=GS)[:, s * 8:(s + 1) * 8]
                        nc.vector.tensor_tensor(res, pw[g % 2][:], res, ALU.add).then_inc(added, 1)

            @block.gpsimd
            def _(pool):
                with pool.Fori(0, B) as b:
                    with pool.Fori(0, M) as m:
                        j = b * M + m
                        for q in range(Q):
                            pool.wait_ge(added, j * TG + (4 * q + 6))
                            core.apart(pool)
                            pool.dma_start(part[:, j * Q + q, :], xr[:, q, :]).then_inc(part_out[q], 16)
                for q in range(Q):
                    pool.wait_ge(part_out[q], B * M * 16)

            @block.tensor
            def _(pe):
                def project(j, g):
                    pe.wait_ge(back_out, j * TG + (g + 3))
                    pe.wait_ge(added, j * TG + (g + 1))
                    nc.tensor.matmul(pw[g % 2][:].rearrange("c n r k -> c (n r k)"), w["wp1"][:], lc[:, g % 2, :],
                                     start=True, stop=True).then_inc(projected, 1)

                pe.wait_ge(ones, 1)
                with pe.Fori(0, B * M) as j:
                    for g in range(TG):
                        pe.wait_ge(turned_out, j * TG + (g + 1))
                        if g % 4 == 0:
                            pe.wait_ge(xn_ready, j * Q + (g // 4 + 1))
                        for i in range(4):
                            pair = (g % 4) * 4 + i
                            mm = nc.tensor.transpose(
                                pt[g % 2][:, i * C:(i + 1) * C],
                                xn[:, g // 4, 2 * pair:2 * pair + 2, :].rearrange("c n s -> c (n s)"),
                                w["ident"][0:C, 0:C])
                        mm.then_inc(turned, 1)
                    pe.wait_ge(turned_out, j * TG + (TG + 2))
                    for g in range(MG):
                        pe.wait_ge(conved_act if g % 2 else conved_dve, j * (MG // 2) + g // 2)
                        for i in range(8):
                            c = g * 8 + i
                            mm = nc.tensor.matmul(pm[g % 2][:, i, :], wconv[:, c * 128:(c + 1) * 128], xt[:, :, c],
                                                  start=True, stop=True)
                        mm.then_inc(conved, 1)
                    pe.wait_ge(conved_dve, j * (MG // 2) + MG // 2)
                    pe.wait_ge(conved_act, j * (MG // 2) + MG // 2)
                    for g in range(TG):
                        pe.wait_ge(back_out, j * TG + (g + 1))
                        for i in range(4):
                            mm = nc.tensor.transpose(pb[g % 2][:, i * 128:(i + 1) * 128], lt[:, g * 4 + i, :],
                                                     w["ident"][:])
                        mm.then_inc(back, 1)
                        if g:
                            project(j, g - 1)
                    project(j, TG - 1)


def gather_context(core, nbr_w, nbr_i):
    nc, d = core.nc, core.d
    T = NW // 128
    HALVES = 2
    ROW = C * P // HALVES
    xg = d["xg"].rearrange("n (h v) -> (n h) v", h=HALVES)
    ctx_out = d["ctx"].rearrange("(t n) (h v) -> n t h v", n=128, h=HALVES)
    with core.stage() as k:
        rows = k.sb("c_rows", [128, HALVES, TOPK, ROW])
        every = k.sb("c_every", [128, T, HALVES, TOPK], U32)
        idx = k.sb("c_idx", [128, HALVES, TOPK], U32)
        got = [k.sem(f"c_got{h}") for h in range(HALVES)]
        out = [k.sem(f"c_out{h}") for h in range(HALVES)]
        every_set, idx_set, summed = k.sem("c_every_set"), k.sem("c_idx_set"), k.sem("c_summed")
        with nc.Block() as block:
            @block.gpsimd
            def _(pool):
                pool.wait_ge(every_set, 1)
                with pool.Fori(0, T) as t:
                    for h in range(HALVES):
                        pool.wait_ge(out[h], t * 16)
                        nc.gpsimd.tensor_copy(idx[:, h, :], every[:, t, h, :]).then_inc(idx_set, 1)
                        pool.wait_ge(idx_set, t * HALVES + (h + 1))
                        core.apart(pool)
                        for j in range(TOPK):
                            pool.indirect_dma_start(rows[:, h, j, :], None, xg[:],
                                                    bass.IndirectOffsetOnAxis(idx[:, h, j:j + 1], 0)
                                                    ).then_inc(got[h], 16)

            @block.vector
            def _(dve):
                for h in range(HALVES):
                    last = nc.vector.tensor_scalar(every[:, :, h, :], nbr_i[:], float(HALVES), float(h),
                                                   ALU.mult, ALU.add)
                last.then_inc(every_set, 1)
                with dve.Fori(0, T) as t:
                    for h in range(HALVES):
                        dve.wait_ge(got[h], t * (16 * TOPK) + 16 * TOPK)
                        for j in range(TOPK):
                            wj = nbr_w[:, t, j:j + 1]
                            if j == 0:
                                ins = nc.vector.tensor_scalar(rows[:, h, 0, :], rows[:, h, 0, :], wj, None, ALU.mult)
                            else:
                                dve.wait_ge(summed, (t * HALVES + h) * TOPK + j)
                                ins = nc.vector.scalar_tensor_tensor(rows[:, h, 0, :], rows[:, h, j, :], wj,
                                                                     rows[:, h, 0, :], ALU.mult, ALU.add)
                            ins.then_inc(summed, 1)

            @block.sync
            def _(sp):
                with sp.Fori(0, T) as t:
                    for h in range(HALVES):
                        sp.wait_ge(summed, (t * HALVES + h) * TOPK + TOPK)
                        sp.dma_start(ctx_out[:, t, h, :], rows[:, h, 0, :]).then_inc(out[h], 16)
                for h in range(HALVES):
                    sp.wait_ge(out[h], T * 16)


def attend(core, w, stats):
    nc, d = core.nc, core.d
    UW = 16
    UT = UW * P
    N = NW // UW
    UPR = GW // UW
    BODY = 2 * UPR
    xg = d["xg"].rearrange("(t n) (c s) -> c t n s", n=GW, c=C)
    cg = d["ctx"].rearrange("(t n) (c s) -> c t n s", n=GW, c=C)
    part, x1 = d["part"], d["x1"]
    with core.stage() as k:
        xw = k.sb("d_xw", [C, 2, GW, P])
        cx = k.sb("d_cx", [C + 1, 2, GW, P])
        pr = k.sb("d_pr", [C, 2, RT])
        tq = k.sb("d_tq", [C + 1, 2, UT])
        mx = k.sb("d_mx", [128, 2, 8])
        sm = k.sb("d_sm", [128, 2, 8])
        rs = k.sb("d_rs", [128, 2, 8])
        ex = k.sb("d_ex", [128, 2, 8, P])
        pn = k.sb("d_pn", [128, 2, 8, P])
        vt = k.sb("d_vt", [128, 2, 8, C])
        at = k.sb("d_at", [128, 2, 4, 128])
        p_t = k.ps("d_p_t", [C + 1, UT])
        p_s = [k.ps(f"d_p_s{i}", [128, 8, P]) for i in range(2)]
        p_v = k.ps("d_p_v", [128, 512])
        p_a = k.ps("d_p_a", [128, 4, 128])
        p_o = k.ps("d_p_o", [C, 2, 8, GS, GS])
        xw_in, cx_in, pr_in, x1_out = ([k.sem(f"d_{n}{s}") for s in range(2)]
                                       for n in ("xw_in", "cx_in", "pr_in", "x1_out"))
        (ones, queries, queries_out, scores, maxed, centred, exped, softmaxed, p_ready, values, values_out,
         turned, turned_out, attended, added, x1_ready) = (
            k.sem("d_" + n) for n in ("ones", "queries", "queries_out", "scores", "maxed", "centred", "exped",
                                      "softmaxed", "p_ready", "values", "values_out", "turned", "turned_out",
                                      "attended", "added", "x1_ready"))

        def wait(eng, sem, value):
            if not isinstance(value, int) or value > 0:
                eng.wait_ge(sem, value)

        def units(step):
            def over(eng):
                for j in range(-2, BODY):
                    step(j, j % BODY, j // BODY, lambda m: m >= 0)
                with eng.Fori(1, N // BODY - 1) as i:
                    for k in range(BODY):
                        step(i * BODY + k, k, i, lambda m: True)
                for j in range(N - BODY, N + 3):
                    step(j, j % BODY, j // BODY, lambda m: m < N)
            return over

        def landed(i, k):
            return (i + k // BODY) * 16 + 16

        def slot(k):
            return k % BODY // UPR

        with nc.Block() as block:
            @block.sync
            def _(sp):
                def load_x(r, s):
                    sp.dma_start(xw[:, s, :, :], xg[:, r, :, :]).then_inc(xw_in[s], 16)

                def load_ctx(r, s):
                    sp.dma_start(cx[0:C, s, :, :], cg[:, r, :, :]).then_inc(cx_in[s], 16)

                def load_part(r, s):
                    sp.dma_start(pr[:, s, :], part[:, r, :]).then_inc(pr_in[s], 16)

                def store(i, s):
                    r = i * 2 + s
                    sp.wait_ge(x1_ready, r * UPR + UPR)
                    sp.dma_start(x1[:, r, :], pr[:, s, :]).then_inc(x1_out[s], 16)

                for s in range(2):
                    load_x(s, s)
                    load_ctx(s, s)
                    load_part(s, s)
                with sp.Fori(0, NT // 2 - 1) as i:
                    for s in range(2):
                        r = i * 2 + s
                        sp.wait_ge(queries, r * UPR + UPR)
                        load_x(r + 2, s)
                        sp.wait_ge(values, r * (2 * UPR) + 2 * UPR)
                        load_ctx(r + 2, s)
                        store(i, s)
                        sp.wait_ge(x1_out[s], i * 16 + 16)
                        load_part(r + 2, s)
                for s in range(2):
                    store(NT // 2 - 1, s)
                for s in range(2):
                    sp.wait_ge(x1_out[s], NT // 2 * 16)

            @block.tensor
            def _(pe):
                def make_queries(n, k, i):
                    if k % UPR == 0:
                        pe.wait_ge(xw_in[slot(k)], landed(i, k))
                    wait(pe, queries_out, n)
                    for h in range(2):
                        lo = (k % UPR) * UW + h * 8
                        mm = nc.tensor.matmul(p_t[:, h * 512:(h + 1) * 512], w["g"][:],
                                              xw[:, slot(k), lo:lo + 8, :].rearrange("c n s -> c (n s)"),
                                              start=True, stop=True)
                    mm.then_inc(queries, 1)

                def make_values(n, k, h):
                    wait(pe, values_out, n * 2 + h)
                    for j in range(4):
                        lo = (k % UPR) * UW + (h * 4 + j) * 2
                        mm = nc.tensor.matmul(p_v[:, j * C:(j + 1) * C],
                                              cx[0:C, slot(k), lo:lo + 2, :].rearrange("c n s -> c (n s)"),
                                              w["wvp"][:], start=True, stop=True)
                    mm.then_inc(values, 1)

                def score(n, k, i):
                    if k % UPR == 0:
                        pe.wait_ge(cx_in[slot(k)], landed(i, k))
                    pe.wait_ge(queries_out, n + 1)
                    wait(pe, centred, n - 1)
                    for v in range(UW):
                        half, col = v // 2 % 2, 2 * (v // 4) + v % 2
                        mm = nc.tensor.matmul(p_s[k % 2][half * P:(half + 1) * P, col, :],
                                              tq[:, k % 2, v * P:(v + 1) * P],
                                              cx[:, slot(k), (k % UPR) * UW + v, :], start=True, stop=True)
                    mm.then_inc(scores, 1)

                def turn(n, k):
                    pe.wait_ge(p_ready, n + 1)
                    wait(pe, turned_out, n)
                    for j in range(4):
                        mm = nc.tensor.transpose(p_a[:, j, :],
                                                 pn[:, k % 2, 2 * j:2 * j + 2, :].rearrange("p n s -> p (n s)"),
                                                 w["ident"][:])
                    mm.then_inc(turned, 1)

                def apply(n, k):
                    pe.wait_ge(turned_out, n + 1)
                    pe.wait_ge(values_out, n * 2 + 2)
                    wait(pe, added, n)
                    for v in range(UW):
                        h, j, half = v % 2, v // 4, v // 2 % 2
                        mm = nc.tensor.matmul(p_o[:, h, v // 2, :, :].rearrange("c r k -> c (r k)"),
                                              vt[h * P:(h + 1) * P, k % 2, v // 2, :],
                                              at[h * P:(h + 1) * P, k % 2, j, half * P:(half + 1) * P],
                                              start=True, stop=True)
                    mm.then_inc(attended, 1)

                def step(n, k, i, live):
                    if live(n + 2):
                        make_queries(n + 2, k + 2, i)
                    if live(n):
                        make_values(n, k, 0)
                    if live(n + 1):
                        score(n + 1, k + 1, i)
                    if live(n):
                        make_values(n, k, 1)
                        turn(n, k)
                    if live(n - 1):
                        apply(n - 1, k - 1)

                pe.wait_ge(ones, 1)
                units(step)(pe)

            @block.scalar
            def _(act):
                def step(n, k, i, live):
                    if live(n + 2):
                        act.wait_ge(queries, n + 3)
                        nc.scalar.activation(tq[:, k % 2, :], p_t[:], ACT.Identity, bias=w["gb"][:, 0:1]
                                             ).then_inc(queries_out, 1)
                    for h in range(2):
                        if live(n):
                            act.wait_ge(values, n * 2 + (h + 1))
                            nc.scalar.copy(vt[:, k % 2, h * 4:(h + 1) * 4, :],
                                           p_v[:, 0:4 * C].rearrange("p (n c) -> p n c", n=4)).then_inc(values_out, 1)
                    if live(n):
                        act.wait_ge(turned, n + 1)
                        nc.scalar.copy(at[:, k % 2, :, :], p_a[:]).then_inc(turned_out, 1)
                    if live(n + 1):
                        act.wait_ge(centred, n + 2)
                        e = ex[:, (k + 1) % 2, :, :]
                        nc.scalar.activation(e, e, ACT.Exp, scale=SCALE).then_inc(exped, 1)

                units(step)(act)

            @block.vector
            def _(dve):
                nc.vector.memset(cx[C:C + 1, :, :, :], 1.0).then_inc(ones, 1)

                def step(n, k, i, live):
                    m, s = n + 1, (k + 1) % 2
                    if live(m):
                        dve.wait_ge(scores, m + 1)
                        nc.vector.tensor_reduce(mx[:, s, :], p_s[s][:], AX.X, ALU.max).then_inc(maxed, 1)
                        dve.wait_ge(maxed, m + 1)
                        nc.vector.tensor_tensor(ex[:, s, :, :], p_s[s][:],
                                                mx[:, s, :].unsqueeze(2).to_broadcast([128, 8, P]),
                                                ALU.subtract).then_inc(centred, 1)
                    if live(n - 2):
                        o, q = n - 2, k - 2
                        half = q % UPR
                        if half == 0:
                            dve.wait_ge(pr_in[slot(q)], landed(i, q))
                        dve.wait_ge(attended, o + 1)
                        rows = pr[:, slot(q), :].rearrange("c (r w) -> c r w", r=GS)
                        for h in range(2):
                            cols = rows[:, :, half * 128:half * 128 + 128]
                            res = cols.rearrange("c r (n h k) -> c h n r k", h=2, k=GS)[:, h]
                            ins = nc.vector.tensor_tensor(res, p_o[:, h, :, :, :], res, ALU.add)
                        ins.then_inc(added, 1)
                        dve.wait_ge(added, o + 1)
                        for h in range(2):
                            st = stats[:, bass.ds(o * 12 + h * 6, 6)] if not isinstance(o, int) else \
                                stats[:, o * 12 + h * 6:o * 12 + h * 6 + 6]
                            ins = nc.vector.bn_stats(st, rows[:, h * 4:h * 4 + 4, half * 128:half * 128 + 128])
                        ins.then_inc(x1_ready, 1)
                    if live(m):
                        dve.wait_ge(exped, m + 1)
                        nc.vector.tensor_reduce(sm[:, s, :], ex[:, s, :, :], AX.X, ALU.add).then_inc(softmaxed, 1)
                        dve.wait_ge(softmaxed, m * 2 + 1)
                        nc.vector.reciprocal(rs[:, s, :], sm[:, s, :]).then_inc(softmaxed, 1)
                        dve.wait_ge(softmaxed, m * 2 + 2)
                        nc.vector.tensor_tensor(pn[:, s, :, :], ex[:, s, :, :],
                                                rs[:, s, :].unsqueeze(2).to_broadcast([128, 8, P]),
                                                ALU.mult).then_inc(p_ready, 1)

                units(step)(dve)


HALF = 1024
TILE = 2 * HALF
NTILE = B * L // TILE


def tokens(ap):
    if len(ap.shape) == 3:
        ap = ap.rearrange("c a b -> c (a b)")
    return ap.rearrange("c (t n) -> c t n", n=TILE)


def image_units(n, body, step, start=lambda b: None):
    def over(eng):
        with eng.Fori(0, B) as b:
            start(b)
            for j in range(-2, body):
                step(b * n + j, j % body, b, j // body, lambda o, j=j: j + o >= 0)
            with eng.Fori(1, n // body - 1) as i:
                for j in range(body):
                    step(b * n + i * body + j, j, b, i, lambda o: True)
            for j in range(n - body, n):
                step(b * n + j, j % body, b, j // body, lambda o, j=j: j + o < n)
    return over


def project_in(core, w, gscale, gbias):
    nc, d = core.nc, core.d
    x1, xc, zs = tokens(d["x1"]), tokens(d["xc"]), tokens(d["zs"])
    PER = NTILE // B
    with core.stage() as k:
        xi = k.sb("p_xi", [C, 4, TILE])
        xo = k.sb("p_xo", [C, 2, TILE])
        zo = k.sb("p_zo", [C, 2, TILE])
        wcur = k.sb("p_wcur", [C, 2 * C])
        bias = k.sb("p_bias", [C, 2, B])
        bcur = k.sb("p_bcur", [C, 2])
        px = [k.ps(f"p_px{i}", [C, HALF]) for i in range(2)]
        pz = [k.ps(f"p_pz{i}", [C, HALF]) for i in range(2)]
        x_in = [k.sem(f"p_x_in{s}") for s in range(4)]
        xc_out, zs_out = ([k.sem(f"p_{n}{s}") for s in range(2)] for n in ("xc_out", "zs_out"))
        biased, bias_set, w_set, b_set, made, xc_ready, zs_ready = (
            k.sem("p_" + n) for n in ("biased", "bias_set", "w_set", "b_set", "made", "xc_ready", "zs_ready"))
        with nc.Block() as block:
            @block.sync
            def _(sp):
                with sp.Fori(0, NTILE // 4) as i:
                    for s in range(4):
                        sp.wait_ge(made, i * 8 + (2 * s + 2))
                        sp.dma_start(xi[:, s, :], x1[:, i * 4 + s, :]).then_inc(x_in[s], 16)

            @block.tensor
            def _(pe):
                pe.sem_inc(made, 8)
                for h in range(2):
                    mm = nc.tensor.matmul(px[0][:, h * B:(h + 1) * B], w["inw"][:, h * C:(h + 1) * C], gbias[:],
                                          start=True, stop=True)
                mm.then_inc(biased, 1)
                pe.wait_ge(bias_set, 1)
                with pe.Fori(0, B) as b:
                    pe.wait_ge(w_set, b + 1)
                    core.apart(pe)
                    with pe.Fori(0, PER // 4) as i:
                        for s in range(4):
                            pe.wait_ge(x_in[s], b * (PER // 4 * 16) + i * 16 + 16)
                            for h in range(2):
                                n = b * (2 * PER) + i * 8 + (2 * s + h)
                                pe.wait_ge(xc_ready, n + 1)
                                pe.wait_ge(zs_ready, n + 1)
                                for p, lo in ((px, 0), (pz, C)):
                                    for q in range(2):
                                        mm = nc.tensor.matmul(
                                            p[h][:, q * 512:(q + 1) * 512], wcur[:, lo:lo + C],
                                            xi[:, s, h * HALF + q * 512:h * HALF + (q + 1) * 512],
                                            start=True, stop=True)
                                mm.then_inc(made, 1)

            @block.vector
            def _(dve):
                dve.sem_inc(xc_ready, 2)
                dve.wait_ge(biased, 1)
                nc.vector.tensor_copy(bias[:], px[0][:, 0:2 * B].rearrange("c (h b) -> c h b", h=2)
                                      ).then_inc(bias_set, 1)
                dve.wait_ge(bias_set, 1)
                with dve.Fori(0, B) as b:
                    dve.wait_ge(made, b * (2 * PER) + 8)
                    nc.vector.tensor_scalar(wcur[:], w["inw"][:], gscale[:, bass.ds(b, 1)], None, ALU.mult
                                            ).then_inc(w_set, 1)
                    dve.wait_ge(zs_ready, b * (2 * PER) + 2)
                    dve.wait_ge(xc_ready, b * (2 * PER) + 2)
                    nc.vector.tensor_copy(bcur[:], bias[:, :, b]).then_inc(b_set, 1)
                    dve.wait_ge(b_set, b + 1)
                    core.apart(dve)
                    with dve.Fori(0, PER // 2) as i:
                        for s in range(2):
                            dve.wait_ge(xc_out[s], b * (PER // 2 * 16) + i * 16)
                            for h in range(2):
                                dve.wait_ge(made, b * (2 * PER) + i * 4 + (2 * s + h + 9))
                                nc.vector.tensor_scalar(xo[:, s, h * HALF:(h + 1) * HALF], px[h][:],
                                                        bcur[:, 0:1], None, ALU.add).then_inc(xc_ready, 1)

            @block.scalar
            def _(act):
                act.sem_inc(zs_ready, 2)
                with act.Fori(0, B) as b:
                    act.wait_ge(b_set, b + 1)
                    with act.Fori(0, PER // 2) as i:
                        for s in range(2):
                            act.wait_ge(zs_out[s], b * (PER // 2 * 16) + i * 16)
                            for h in range(2):
                                act.wait_ge(made, b * (2 * PER) + i * 4 + (2 * s + h + 9))
                                nc.scalar.activation(zo[:, s, h * HALF:(h + 1) * HALF], pz[h][:], ACT.Silu,
                                                     bias=bcur[:, 1:2]).then_inc(zs_ready, 1)

            @block.gpsimd
            def _(pool):
                with pool.Fori(0, NTILE // 2) as i:
                    for s in range(2):
                        for ready, outs, to, src in ((xc_ready, xc_out, xc, xo), (zs_ready, zs_out, zs, zo)):
                            pool.wait_ge(ready, i * 4 + (2 * s + 4))
                            core.apart(pool)
                            pool.dma_start(to[:, i * 2 + s, :], src[:, s, :]).then_inc(outs[s], 16)
                for s in range(2):
                    pool.wait_ge(xc_out[s], NTILE // 2 * 16)
                    pool.wait_ge(zs_out[s], NTILE // 2 * 16)


def image_convs(core, w):
    nc, d = core.nc, core.d
    xc = d["xc"].rearrange("c (b h) w -> c h b w", b=B)
    u = d["u"].rearrange("c (b h) w -> c h b w", b=B)
    spans = [(0, 1, CROWS + 1, 0, CROWS), (CROWS - 1, 0, CROWS + 2, CROWS, H - CROWS - 85),
             (H - CROWS, 0, CROWS, H - 85, 85)]
    GROUPS = CTILES * B // 2
    with core.stage() as k:
        rows = k.sb("v_rows", [CROWS + 2, 3, CROWS])
        taps = k.sb("v_taps", [128, C * 9])
        cb = k.sb("v_cb", [128, C])
        xi = k.sb("v_xi", [CROWS + 2, 2, CTILES, B, W + 2])
        band = k.sb("v_band", [CROWS + 2, 2, 3, CROWS])
        cbc = k.sb("v_cbc", [CROWS, 2])
        uo = k.sb("v_uo", [CROWS, 2, CTILES, B, W])
        pc = [k.ps(f"v_pc{i}", [CROWS, 2, W]) for i in range(GROUPS)]
        consts, zeroed, built, banded, made, acted = (
            k.sem("v_" + n) for n in ("consts", "zeroed", "built", "banded", "made", "acted"))
        x_in, u_out = ([k.sem(f"v_{n}{s}") for s in range(2)] for n in ("x_in", "u_out"))
        with nc.Block() as block:
            @block.sync
            def _(sp):
                sp.dma_start(rows[:], d["rows"]).then_inc(consts, 16)
                sp.dma_start(taps[:], d["conv_w"].partition_broadcast(128)).then_inc(consts, 16)
                sp.dma_start(cb[:], d["conv_b"].partition_broadcast(128)).then_inc(consts, 16)
                sp.wait_ge(zeroed, 1)
                with sp.Fori(0, C // 2) as i:
                    for s in range(2):
                        sp.wait_ge(made, i * (2 * GROUPS) + (s + 1) * GROUPS)
                        for t, (row, p, n, _, _) in enumerate(spans):
                            sp.dma_start(xi[p:p + n, s, t, :, 1:W + 1], xc[i * 2 + s, row:row + n, :, :]
                                         ).then_inc(x_in[s], 16)

            @block.vector
            def _(dve):
                nc.vector.memset(xi[:], 0.0).then_inc(zeroed, 1)
                dve.wait_ge(consts, 48)
                with dve.Fori(0, C // 2) as i:
                    for s in range(2):
                        dve.wait_ge(made, i * (2 * GROUPS) + (s + 1) * GROUPS)
                        dve.wait_ge(acted, i * (2 * GROUPS) + (s + 1) * GROUPS)
                        nc.vector.tensor_copy(cbc[:, s:s + 1], cb[0:CROWS, bass.ds(i * 2 + s, 1)])
                        for dy in range(3):
                            if dy:
                                dve.wait_ge(built, (i * 2 + s) * 2 + dy)
                            for dx in range(3):
                                tap = taps[0:CROWS + 2, bass.ds(i * 18 + (s * 9 + dy * 3 + dx), 1)]
                                to = band[:, s, dx, :]
                                if dy == 0:
                                    ins = nc.vector.tensor_scalar(to, rows[:, dy, :], tap, None, ALU.mult)
                                else:
                                    ins = nc.vector.scalar_tensor_tensor(to, rows[:, dy, :], tap, to,
                                                                         ALU.mult, ALU.add)
                            ins.then_inc(banded if dy == 2 else built, 1)

            @block.tensor
            def _(pe):
                pe.sem_inc(made, 2 * GROUPS)
                with pe.Fori(0, C // 2) as i:
                    for s in range(2):
                        pe.wait_ge(banded, i * 2 + (s + 1))
                        pe.wait_ge(x_in[s], i * (16 * CTILES) + 16 * CTILES)
                        for g in range(GROUPS):
                            pe.wait_ge(acted, i * (2 * GROUPS) + ((s + 1) * GROUPS + g + 1))
                            t, b = g // 2, g % 2 * 2
                            for dx in range(3):
                                mm = nc.tensor.matmul(pc[g][:], band[:, s, dx, :], xi[:, s, t, b:b + 2, dx:dx + W],
                                                      start=(dx == 0), stop=(dx == 2))
                            mm.then_inc(made, 1)

            @block.scalar
            def _(act):
                act.sem_inc(acted, 2 * GROUPS)
                with act.Fori(0, C // 2) as i:
                    for s in range(2):
                        act.wait_ge(u_out[s], i * (16 * CTILES))
                        for g in range(GROUPS):
                            act.wait_ge(made, i * (2 * GROUPS) + ((s + 2) * GROUPS + g + 1))
                            nc.scalar.activation(uo[:, s, g // 2, g % 2 * 2:g % 2 * 2 + 2, :], pc[g][:],
                                                 ACT.Silu, bias=cbc[:, s:s + 1]).then_inc(acted, 1)

            @block.gpsimd
            def _(pool):
                with pool.Fori(0, C // 2) as i:
                    for s in range(2):
                        pool.wait_ge(acted, i * (2 * GROUPS) + (s + 3) * GROUPS)
                        for t, (_, _, _, row, n) in enumerate(spans):
                            pool.dma_start(u[i * 2 + s, row:row + n, :, :], uo[0:n, s, t, :, :]
                                           ).then_inc(u_out[s], 16)
                for s in range(2):
                    pool.wait_ge(u_out[s], C // 2 * 16 * CTILES)


def scan_pass(core, w, way):
    nc, d = core.nc, core.d
    u, yf, y = tokens(d["u"]), tokens(d["yf"]), tokens(d["y"])
    PER = NTILE // B
    N = 2 * PER
    BODY = 4
    CAP = 40.0
    n_ = f"s{way}_"
    with core.stage() as k:
        ui = k.sb(n_ + "ui", [C, 2, TILE])
        fi = k.sb(n_ + "fi", [C, 2, TILE]) if way else None
        yo = k.sb(n_ + "yo", [C, 2, TILE])
        ex = k.sb(n_ + "ex", [C, 2, HALF])
        dl = k.sb(n_ + "dl", [C, 2, HALF])
        da = k.sb(n_ + "da", [C, 2, HALF])
        db = k.sb(n_ + "db", [C, 2, HALF])
        hs = k.sb(n_ + "hs", [C, 2, HALF])
        us = k.sb(n_ + "us", [C, 2, HALF]) if way else None
        p_d = [k.ps(f"{n_}p_d{i}", [C, HALF]) for i in range(2)]
        p_b = k.ps(n_ + "p_b", [C, HALF])
        p_c = k.ps(n_ + "p_c", [C, HALF])
        u_in, f_in, y_out = ([k.sem(f"{n_}{n}{s}") for s in range(2)] for n in ("u_in", "f_in", "y_out"))
        (raw, b_made, c_made, capped, logged, delta, decays, gained, bu, scanned, y_ready, skip, skipped,
         cleared, seen) = (
            k.sem(n_ + n) for n in ("raw", "b_made", "c_made", "capped", "logged", "delta", "decays", "gained",
                                    "bu", "scanned", "y_ready", "skip", "skipped", "cleared", "seen"))

        def units(step, start=lambda b: None):
            return image_units(N, BODY, step, start)

        def landed(b, i, k):
            return b * (PER // 2 * 16) + (i + k // BODY) * 16 + 16

        def half(k, n=HALF):
            h = k % 2 if way == 0 else 1 - k % 2
            return slice(h * n, (h + 1) * n)

        def slot(k):
            return k % BODY // 2

        with nc.Block() as block:
            @block.sync
            def _(sp):
                with sp.Fori(0, B) as b:
                    with sp.Fori(0, PER // 2) as i:
                        for s in range(2):
                            t = b * PER + i * 2 + s if way == 0 else b * PER + (PER - 1 - s) - i * 2
                            tiles = b * PER + i * 2 + s
                            sp.wait_ge(y_ready, tiles * 2)
                            sp.dma_start(ui[:, s, :], u[:, t, :]).then_inc(u_in[s], 16)
                            if way:
                                sp.dma_start(fi[:, s, :], yf[:, t, :]).then_inc(f_in[s], 16)

            @block.tensor
            def _(pe):
                def step(m, k, b, i, live):
                    if live(2):
                        kk = k + 2
                        if kk % 2 == 0:
                            pe.wait_ge(u_in[slot(kk)], landed(b, i, kk))
                        pe.wait_ge(delta, m + 3)
                        for q in range(2):
                            lo = half(kk).start + q * 512
                            mm = nc.tensor.matmul(p_d[kk % 2][:, q * 512:(q + 1) * 512], w["wd"][:, way, :],
                                                  ui[:, slot(kk), lo:lo + 512], start=True, stop=True)
                        mm.then_inc(raw, 1)
                    if live(0):
                        for r, p, done, used in ((0, p_b, b_made, bu), (1, p_c, c_made, y_ready)):
                            pe.wait_ge(used, m + (2 if used is y_ready else 0))
                            for q in range(2):
                                lo = half(k).start + q * 512
                                mm = nc.tensor.matmul(p[:, q * 512:(q + 1) * 512], w["bc"][:, way, r, :],
                                                      ui[:, slot(k), lo:lo + 512], start=True, stop=True)
                            mm.then_inc(done, 1)

                units(step)(pe)

            @block.scalar
            def _(act):
                def step(m, k, b, i, live):
                    if live(2):
                        e = ex[:, k % 2, :]
                        act.wait_ge(capped, m + 3)
                        nc.scalar.activation(e, e, ACT.Exp).then_inc(logged, 1)
                        act.wait_ge(logged, m * 2 + 5)
                        nc.scalar.activation(e, e, ACT.Ln, bias=1.0).then_inc(logged, 1)
                    if live(1):
                        act.wait_ge(delta, m + 4)
                        nc.scalar.activation(da[:, (k + 1) % 2, :], dl[:, (k + 1) % 2, :], ACT.Exp,
                                             scale=w["nega"][:, way:way + 1]).then_inc(decays, 1)
                        if way:
                            kk = k + 1
                            act.wait_ge(u_in[slot(kk)], landed(b, i, kk))
                            nc.scalar.activation(us[:, kk % 2, :], ui[:, slot(kk), half(kk)], ACT.Identity,
                                                 scale=w["dsum"][:, 0:1]).then_inc(skip, 1)

                units(step)(act)

            @block.gpsimd
            def _(pool):
                def step(m, k, b, i, live):
                    if live(1):
                        kk = k + 1
                        pool.wait_ge(decays, m + 2)
                        dd = dl[:, kk % 2, :]
                        nc.gpsimd.tensor_tensor(dd, dd, ui[:, slot(kk), half(kk)], ALU.mult).then_inc(gained, 1)
                        if way:
                            pool.wait_ge(skip, m + 2)
                            pool.wait_ge(f_in[slot(kk)], landed(b, i, kk))
                            us_ = us[:, kk % 2, :]
                            nc.gpsimd.tensor_tensor(us_, us_, fi[:, slot(kk), half(kk)], ALU.add
                                                    ).then_inc(skipped, 1)
                    if live(0) and k % 2 == 1:
                        s = slot(k)
                        t = b * PER + i * 2 + s if way == 0 else b * PER + (PER - 1 - s) - i * 2
                        pool.wait_ge(y_ready, m + 3)
                        core.apart(pool)
                        pool.dma_start((yf if way == 0 else y)[:, t, :], yo[:, s, :]).then_inc(y_out[s], 16)

                units(step)(pool)
                for s in range(2):
                    pool.wait_ge(y_out[s], NTILE // 2 * 16)

            @block.vector
            def _(dve):
                dve.sem_inc(delta, 2)
                dve.sem_inc(y_ready, 2)

                def start(b):
                    last = HALF - 1 if way == 0 else 0
                    dve.wait_ge(y_ready, b * N + 2)
                    nc.vector.memset(hs[:, 1, last:last + 1], 0.0).then_inc(cleared, 1)
                    dve.wait_ge(cleared, b + 1)

                def step(m, k, b, i, live):
                    if live(2):
                        dve.wait_ge(raw, m + 3)
                        nc.vector.tensor_scalar(ex[:, k % 2, :], p_d[k % 2][:], w["dtb"][:, way:way + 1], CAP,
                                                ALU.add, ALU.min).then_inc(capped, 1)
                    if live(0):
                        dve.wait_ge(gained, m + 1)
                        dve.wait_ge(b_made, m + 1)
                        nc.vector.tensor_tensor(db[:, k % 2, :], dl[:, k % 2, :], p_b[:], ALU.mult).then_inc(bu, 1)
                        dve.wait_ge(bu, m + 1)
                        dve.wait_ge(decays, m + 1)
                        r = slice(None) if way == 0 else slice(None, None, -1)
                        before = hs[:, (k + 1) % 2, HALF - 1:HALF] if way == 0 else hs[:, (k + 1) % 2, 0:1]
                        nc.vector.tensor_tensor_scan(hs[:, k % 2, r], da[:, k % 2, r], db[:, k % 2, r], before,
                                                     ALU.mult, ALU.add).then_inc(scanned, 1)
                    if live(1):
                        dve.wait_ge(logged, m * 2 + 4)
                        nc.vector.scalar_tensor_tensor(dl[:, (k + 1) % 2, :], p_d[(k + 1) % 2][:],
                                                       w["dtb"][:, way:way + 1], ex[:, (k + 1) % 2, :],
                                                       ALU.add, ALU.max).then_inc(delta, 1)
                    if live(0):
                        dve.wait_ge(scanned, m + 1)
                        dve.wait_ge(c_made, m + 1)
                        if k % 2 == 0:
                            dve.wait_ge(y_out[slot(k)], landed(b, i, k) - 16)
                        to = yo[:, slot(k), half(k)]
                        ins = nc.vector.tensor_tensor(to, hs[:, k % 2, :], p_c[:], ALU.mult)
                        if way:
                            ins.then_inc(seen, 1)
                            dve.wait_ge(seen, m + 1)
                            dve.wait_ge(skipped, m + 1)
                            ins = nc.vector.tensor_tensor(to, to, us[:, k % 2, :], ALU.add)
                        ins.then_inc(y_ready, 1)

                units(step, start)(dve)


def norm_gate_out(core, w):
    nc, d = core.nc, core.d
    x1, y, zs = tokens(d["x1"]), tokens(d["y"]), tokens(d["zs"])
    out = d["out"].rearrange("b c h w -> c b (h w)").rearrange("c b (t n) -> c b t n", n=TILE)
    PER = NTILE // B
    SLOTS = 4
    BODY = 2 * SLOTS
    N = 2 * PER
    with core.stage() as k:
        yi, xi, zi = (k.sb("o_" + n, [C, SLOTS, TILE]) for n in ("yi", "xi", "zi"))
        sq, rs, tn, gt = (k.sb("o_" + n, [C, 2, HALF]) for n in ("sq", "rs", "tn", "gt"))
        eps = k.sb("o_eps", [C, 1])
        p_y = [k.ps(f"o_p_y{i}", [C, HALF]) for i in range(2)]
        p_v = k.ps("o_p_v", [C, HALF])
        p_o = k.ps("o_p_o", [C, HALF])
        y_in, x_in, z_in, out_done = ([k.sem(f"o_{n}{s}") for s in range(SLOTS)]
                                      for n in ("y_in", "x_in", "z_in", "out_done"))
        (eps_set, centred, squared, vared, logged, rooted, normed, affine, gated, projected, finished) = (
            k.sem("o_" + n) for n in ("eps_set", "centred", "squared", "vared", "logged", "rooted", "normed",
                                      "affine", "gated", "projected", "finished"))

        def landed(b, i, k):
            return b * (PER // SLOTS * 16) + (i + k // BODY) * 16 + 16

        def slot(k):
            return k % BODY // 2

        def half(k):
            return slice(k % 2 * HALF, (k % 2 + 1) * HALF)

        with nc.Block() as block:
            @block.sync
            def _(sp):
                with sp.Fori(0, B) as b:
                    with sp.Fori(0, PER // SLOTS) as i:
                        for s in range(SLOTS):
                            t = b * PER + i * SLOTS + s
                            sp.wait_ge(out_done[s], b * (PER // SLOTS * 16) + i * 16)
                            sp.dma_start(yi[:, s, :], y[:, t, :]).then_inc(y_in[s], 16)
                            sp.dma_start(zi[:, s, :], zs[:, t, :]).then_inc(z_in[s], 16)
                            sp.dma_start(xi[:, s, :], x1[:, t, :]).then_inc(x_in[s], 16)

            @block.tensor
            def _(pe):
                pe.sem_inc(projected, 1)

                def product(p, lhs, rhs, done):
                    for q in range(2):
                        mm = nc.tensor.matmul(p[:, q * 512:(q + 1) * 512], lhs, rhs[:, q * 512:(q + 1) * 512],
                                              start=True, stop=True)
                    mm.then_inc(done, 1)

                def step(m, k, b, i, live):
                    if live(2):
                        kk = k + 2
                        if kk % 2 == 0:
                            pe.wait_ge(y_in[slot(kk)], landed(b, i, kk))
                        pe.wait_ge(normed, m + 3)
                        product(p_y[kk % 2], w["centre"][:], yi[:, slot(kk), half(kk)], centred)
                    if live(0):
                        pe.wait_ge(gated, m + 2)
                        pe.wait_ge(finished, m)
                        product(p_o, w["wo"][:], gt[:, k % 2, :], projected)
                    if live(2):
                        pe.wait_ge(squared, m + 3)
                        pe.wait_ge(logged, m + 2)
                        product(p_v, w["mean"][:], sq[:, k % 2, :], vared)

                image_units(N, BODY, step)(pe)

            @block.scalar
            def _(act):
                act.wait_ge(eps_set, 1)

                def step(m, k, b, i, live):
                    r = rs[:, (k + 1) % 2, :]
                    if live(1):
                        act.wait_ge(vared, m + 2)
                        nc.scalar.activation(r, p_v[:], ACT.Ln, bias=eps[:, 0:1]).then_inc(logged, 1)
                    if live(2):
                        act.wait_ge(centred, m + 3)
                        nc.scalar.activation(sq[:, k % 2, :], p_y[k % 2][:], ACT.Square).then_inc(squared, 1)
                    if live(1):
                        act.wait_ge(logged, m + 2)
                        nc.scalar.activation(r, r, ACT.Exp, scale=-0.5).then_inc(rooted, 1)

                image_units(N, BODY, step)(act)

            @block.vector
            def _(dve):
                dve.sem_inc(normed, 2)
                nc.vector.memset(eps[:], GEPS).then_inc(eps_set, 1)

                def step(m, k, b, i, live):
                    if live(0):
                        if k % 2 == 0:
                            dve.wait_ge(x_in[slot(k)], landed(b, i, k))
                        dve.wait_ge(projected, m + 2)
                        x = xi[:, slot(k), half(k)]
                        nc.vector.scalar_tensor_tensor(x, p_o[:], w["scale"][:, 0:1], x, ALU.mult, ALU.add
                                                       ).then_inc(finished, 1)
                    if live(1):
                        kk = (k + 1) % 2
                        dve.wait_ge(rooted, m + 2)
                        dve.wait_ge(gated, m + 1)
                        nc.vector.tensor_tensor(tn[:, kk, :], p_y[kk][:], rs[:, kk, :], ALU.mult).then_inc(normed, 1)
                        dve.wait_ge(normed, m + 4)
                        nc.vector.tensor_scalar(tn[:, kk, :], tn[:, kk, :], w["onwb"][:, 0:1], w["onwb"][:, 1:2],
                                                ALU.mult, ALU.add).then_inc(affine, 1)

                image_units(N, BODY, step)(dve)

            @block.gpsimd
            def _(pool):
                pool.sem_inc(gated, 1)

                def step(m, k, b, i, live):
                    if live(1):
                        kk = k + 1
                        if kk % 2 == 0:
                            pool.wait_ge(z_in[slot(kk)], landed(b, i, kk))
                        pool.wait_ge(affine, m + 2)
                        pool.wait_ge(projected, m + 1)
                        nc.gpsimd.tensor_tensor(gt[:, kk % 2, :], tn[:, kk % 2, :], zi[:, slot(kk), half(kk)],
                                                ALU.mult).then_inc(gated, 1)
                    if live(0) and k % 2 == 1:
                        pool.wait_ge(finished, m + 1)
                        core.apart(pool)
                        pool.dma_start(out[:, b, i * SLOTS + slot(k), :], xi[:, slot(k), :]
                                       ).then_inc(out_done[slot(k)], 16)

                image_units(N, BODY, step)(pool)
                for s in range(SLOTS):
                    pool.wait_ge(out_done[s], NTILE // SLOTS * 16)


def program(nc, dram, upto=99):
    with ExitStack() as ctx:
        core = Core(nc, ctx, dram)
        w = {n: core.sb("w_" + n, s) for n, s in dict(
            ident=[128, 128], group=[C, C], centre=[C, C], mean=[C, C], g=[C, C + 1], gb=[C + 1, 1],
            wvp=[C, C], wp1=[C + 1, C], lepe=[128, C * 9], wd=[C, 2, C], bc=[C, 2, 2, C], dtb=[C, 2],
            nega=[C, 2], dsum=[C, 1], inw=[C, 2 * C], wo=[C, C], onwb=[C, 2], scale=[C, 1]).items()}
        gscale, gbias = core.sb("gscale", [C, B]), core.sb("gbias", [C, B])
        nbr_w = core.sb("nbr_w", [128, NW // 128, TOPK])
        nbr_i = core.sb("nbr_i", [128, NW // 128, TOPK], U32)
        setup_weights(core, w)
        with ExitStack() as early:
            wconv = early.enter_context(nc.sbuf_tensor("wconv", [128, C * 128], F32))
            build_window_convs(core, w, wconv)
            with ExitStack() as pool:
                stats = pool.enter_context(nc.sbuf_tensor("stats", [C, NT * 24], F32))
                pooled = pool.enter_context(nc.sbuf_tensor("pooled", [C, NW], F32))
                image_stats(core, stats, pooled)
                group_coefficients(core, w, "g0", stats, gscale, gbias)
                top_windows(core, pooled, gscale, gbias, nbr_w, nbr_i)
            if upto < 2:
                return
            window_convs(core, w, wconv, gscale, gbias)
        gather_context(core, nbr_w, nbr_i)
        if upto < 3:
            return
        with ExitStack() as pool:
            stats = pool.enter_context(nc.sbuf_tensor("stats1", [C, NT * 24], F32))
            attend(core, w, stats)
            group_coefficients(core, w, "g1", stats, gscale, gbias)
        if upto < 4:
            return
        project_in(core, w, gscale, gbias)
        if upto < 5:
            return
        image_convs(core, w)
        if upto < 6:
            return
        scan_pass(core, w, 0)
        if upto < 7:
            return
        scan_pass(core, w, 1)
        if upto < 8:
            return
        norm_gate_out(core, w)


def declare(nc, d):
    for name, shape in dict(xg=(NW, C * P), ctx=(NW, C * P), part=(C, NT, RT), x1=(C, NT, RT), xc=(C, B * H, W),
                            u=(C, B * H, W), yf=(C, B * L), y=(C, B * L), zs=(C, B * L)).items():
        d[name] = nc.dram_tensor("mid_" + name, shape, F32, kind="Internal").ap()


def arrays(i):
    f = lambda a: np.ascontiguousarray(a)
    col = lambda a: f(np.asarray(a).reshape(-1, 1))
    a = {k: np.asarray(v) for k, v in i.items()}
    xp = a["L1_conv_x_proj_w"]
    out = dict(
        x=f(a["x"]), wq_t=f(a["L0_conv_Wq"].T),
        wk_t_bk=f(np.concatenate([a["L0_conv_Wk"].T, a["L0_conv_bk"][:, None]], axis=1)),
        bq=col(a["L0_conv_bq"]), wv_t=f(a["L0_conv_Wv"].T),
        bv_lb=f(np.stack([a["L0_conv_bv"], a["L0_conv_lepe_b"]], axis=1)),
        wp=f(a["L0_conv_Wp"]), bp=f(a["L0_conv_bp"].reshape(1, C)), lepe_w=f(a["L0_conv_lepe_w"].reshape(C * 9)),
        xp_dt=f(xp[:, 0:R].transpose(1, 0, 2)), dtw_t=f(a["L1_conv_dt_proj_w"].transpose(2, 0, 1)),
        xp_t=f(xp.transpose(2, 0, 1).reshape(C, 2 * NX)), alog_t=f(a["L1_conv_A_logs"].reshape(2, C).T),
        ds_t=f(a["L1_conv_Ds"].reshape(2, C).T), dtb_t=f(a["L1_conv_dt_proj_b"].T),
        in_w_t=f(a["L1_conv_in_proj_w"].T), wo_t=f(a["L1_conv_out_proj_w"].T),
        onwb=f(np.stack([a["L1_conv_out_norm_w"], a["L1_conv_out_norm_b"]], axis=1)),
        scale_w=col(a["L1_conv_scale_w"]), conv_w=f(a["L1_conv_conv_w"].reshape(C * 9)), conv_b=f(a["L1_conv_conv_b"]))
    out.update(unit_constants())
    return {"in_" + n: v for n, v in out.items()}


def kernel(**inputs):
    import concourse.bacc as bacc
    from concourse.bass_utils import run_bass_kernel_spmd

    nc = bacc.Bacc("TRN2", target_bir_lowering=False, num_devices=1)
    sent = arrays(inputs)
    dram = {n[3:]: nc.dram_tensor(n, a.shape, mybir.dt.from_np(a.dtype), kind="ExternalInput").ap()
            for n, a in sent.items()}
    dram["out"] = nc.dram_tensor("out", (B, C, H, W), F32, kind="ExternalOutput").ap()
    declare(nc, dram)
    program(nc, dram)
    return run_bass_kernel_spmd(nc, [sent], core_ids=[0]).results[0]["out"]
```

```python
from contextlib import ExitStack, contextmanager

import numpy as np

import concourse.bass as bass
from concourse import mybir

F32 = mybir.dt.float32
U32 = mybir.dt.uint32
ALU = mybir.AluOpType
ACT = mybir.ActivationFunctionType
AX = mybir.AxisListType

B, C, H, W = 4, 96, 256, 256
GS = 8
P = GS * GS
GH, GW = H // GS, W // GS
NW = B * GH * GW
NT = B * GH
RT = GS * W
PAIRS = GW // 2
TOPK = 3
L = H * W
R = 6
NX = R + 2
SCALE = float(C) ** -0.5
GEPS = 1e-5


def unit_constants():
    ident = np.eye(128, dtype=np.float32)
    pos = np.arange(P)
    shifts = np.zeros((128, 9, 128), np.float32)
    for t in range(9):
        dy, dx = t // 3 - 1, t % 3 - 1
        r, c = pos // GS + dy, pos % GS + dx
        ok = (r >= 0) & (r < GS) & (c >= 0) & (c < GS)
        for w in range(2):
            shifts[w * P + (r * GS + c)[ok], t, w * P + pos[ok]] = 1.0
    rows = np.stack([np.eye(128, k=1 - dy) for dy in range(3)], axis=1).astype(np.float32)
    seams = np.stack([np.kron(np.eye(SEAM * B), np.eye(4, k=1 - dy)[:, 1:3]) for dy in range(3)],
                     axis=1).astype(np.float32)
    group = np.kron(np.eye(C // 3), np.ones((3, 3))).astype(np.float32) / np.float32(3)
    centre = (np.eye(C) - 1.0 / C).astype(np.float32)
    mean = np.full((C, C), 1.0 / C, np.float32)
    return dict(ident=ident, shifts=shifts, rows=rows, group=group, centre=centre, mean=mean,
                seams=seams)


SEAM = 6


class Core:

    def __init__(self, nc, ctx, dram, passed=None):
        self.nc, self.ctx, self.d = nc, ctx, dram
        self.sems = []
        self.passed = passed if passed is not None else ctx.enter_context(nc.semaphore("passed"))

    def sb(self, name, shape, dt=F32):
        return self.ctx.enter_context(self.nc.sbuf_tensor(name, shape, dt))

    def ps(self, name, shape, dt=F32):
        return self.ctx.enter_context(self.nc.psum_tensor(name, shape, dt))

    def sem(self, name):
        self.sems.append(self.nc.alloc_semaphore(name))
        return self.sems[-1]

    def apart(self, eng):
        eng.sem_inc(self.passed, 1)

    @contextmanager
    def stage(self):
        with ExitStack() as ctx:
            stage = Core(self.nc, ctx, self.d, self.passed)
            yield stage
            self.nc.clear_and_free_semaphores(stage.sems)
            self.nc.all_engine_barrier()


def setup_weights(core, w):
    nc, d = core.nc, core.d
    with core.stage() as k:
        wq_t = k.sb("wq_t", [C, C])
        wk_t = k.sb("wk_t", [C, C + 1])
        wv_t = k.sb("wv_t", [C, C])
        bq = k.sb("bq", [C, 1])
        bvl = k.sb("bvl", [C, 2])
        bp = k.sb("bp", [1, C])
        crow = k.sb("crow", [1, C])
        bsum = k.sb("bsum", [C, 1])
        xp = k.sb("xp", [R, 2, C])
        dtw = k.sb("dtw", [R, 2, C])
        xpt = k.sb("xpt", [C, 2 * NX])
        alog = k.sb("alog", [C, 2])
        aexp = k.sb("aexp", [C, 2])
        ds = k.sb("ds", [C, 2])
        p1 = k.ps("setup_p1", [C, 512])
        p2 = k.ps("setup_p2", [C, 512])
        p3 = k.ps("setup_p3", [C + 1, 512])
        loaded, summed, folded, stored, powed, crow_ready, row_in = (
            k.sem(f"setup_{n}") for n in ("loaded", "summed", "folded", "stored", "powed", "crow", "rowin"))
        loads = [
            (wq_t[:], d["wq_t"]), (wk_t[:], d["wk_t_bk"]), (wv_t[:], d["wv_t"]), (bq[:], d["bq"]),
            (bvl[:], d["bv_lb"]), (bp[:], d["bp"]), (w["wp1"][0:C, :], d["wp"]), (w["ident"][:], d["ident"]),
            (w["group"][:], d["group"]), (w["centre"][:], d["centre"]), (w["mean"][:], d["mean"]),
            (xp[:], d["xp_dt"]), (dtw[:], d["dtw_t"]), (xpt[:], d["xp_t"]), (alog[:], d["alog_t"]), (ds[:], d["ds_t"]),
            (w["wd"][C:C + 1, :, :], d["dtb"]), (w["inw"][:], d["in_w_t"]), (w["wo"][:], d["wo_t"]),
            (w["onwb"][:], d["onwb"]), (w["scale"][:], d["scale_w"]),
            (w["lepe"][:], d["lepe_w"].partition_broadcast(128)),
        ]
        with nc.Block() as block:
            @block.sync
            def _(sp):
                for to, src in loads:
                    sp.dma_start(to, src).then_inc(loaded, 16)
                sp.wait_ge(crow_ready, 1)
                sp.dma_start(w["wp1"][C:C + 1, :], crow[:]).then_inc(row_in, 16)
                sp.wait_ge(row_in, 16)

            @block.vector
            def _(dve):
                dve.wait_ge(loaded, 16 * len(loads))
                nc.vector.tensor_tensor(bsum[:], bvl[:, 0:1], bvl[:, 1:2], ALU.add).then_inc(summed, 1)
                nc.vector.tensor_tensor(w["dsum"][:], ds[:, 0:1], ds[:, 1:2], ALU.add)
                for s in range(2):
                    for r in range(2):
                        nc.vector.tensor_copy(w["bc"][:, s, r, :],
                                              xpt[:, s * NX + R + r:s * NX + R + r + 1].to_broadcast([C, C]))
                dve.wait_ge(folded, 1)
                nc.vector.tensor_copy(w["g"][:], p1[:, 0:C + 1])
                nc.vector.tensor_copy(w["wvp"][:], p1[:, 128:128 + C])
                nc.vector.tensor_copy(w["wd"][0:C, 0, :], p1[:, 256:256 + C])
                nc.vector.tensor_copy(w["wd"][0:C, 1, :], p1[:, 384:384 + C])
                nc.vector.tensor_copy(w["gb"][:], p3[:, 0:1])
                nc.vector.tensor_tensor(crow[:], p2[0:1, 0:C], bp[:], ALU.add).then_inc(crow_ready, 1)
                dve.wait_ge(powed, 1)
                nc.vector.tensor_scalar(w["nega"][:], aexp[:], -1.0, None, ALU.mult).then_inc(stored, 1)

            @block.scalar
            def _(act):
                act.wait_ge(loaded, 16 * len(loads))
                nc.scalar.activation(aexp[:], alog[:], ACT.Exp).then_inc(powed, 1)

            @block.tensor
            def _(pe):
                pe.wait_ge(loaded, 16 * len(loads))
                mm = lambda o, a, b: nc.tensor.matmul(o, a, b, start=True, stop=True)
                mm(p1[:, 0:C + 1], wq_t[:], wk_t[:])
                mm(p1[:, 128:128 + C], wv_t[:], w["wp1"][0:C, :])
                mm(p1[:, 256:256 + C], xp[:, 0, :], dtw[:, 0, :])
                mm(p1[:, 384:384 + C], xp[:, 1, :], dtw[:, 1, :])
                mm(p3[:, 0:1], wk_t[:], bq[:])
                pe.wait_ge(summed, 1)
                mm(p2[0:1, 0:C], bsum[:], w["wp1"][0:C, :]).then_inc(folded, 1)


def build_window_convs(core, w, wconv):
    nc, d = core.nc, core.d
    GROUP = 8
    with core.stage() as k:
        shifts = k.sb("shifts", [128, 9, 128])
        in_ = k.sem("wc_in")
        built = k.sem("wc_built")
        with nc.Block() as block:
            @block.sync
            def _(sp):
                sp.dma_start(shifts[:], d["shifts"]).then_inc(in_, 16)

            @block.vector
            def _(dve):
                dve.wait_ge(in_, 16)
                with dve.Fori(0, C // GROUP) as g:
                    for t in range(9):
                        for j in range(GROUP):
                            to = wconv[:, bass.ds(g * (GROUP * 128) + j * 128, 128)]
                            tap = w["lepe"][:, bass.ds(g * (GROUP * 9) + (j * 9 + t), 1)]
                            if t == 0:
                                last = nc.vector.tensor_scalar(to, shifts[:, t, :], tap, None, ALU.mult)
                            else:
                                last = nc.vector.scalar_tensor_tensor(to, shifts[:, t, :], tap, to,
                                                                      ALU.mult, ALU.add)
                        last.then_inc(built, 1)
                        dve.wait_ge(built, g * 9 + (t + 1))


def image_stats(core, stats, pooled):
    nc, d = core.nc, core.d
    x = d["x"].rearrange("b c (g r) w -> c b g (r w)", r=GS)
    SLOTS = 4
    with core.stage() as k:
        xin = k.sb("a_x", [C, SLOTS, RT])
        x_in = [k.sem(f"a_x_in{s}") for s in range(SLOTS)]
        x_free = k.sem("a_x_free")
        with nc.Block() as block:
            @block.sync
            def _(sp):
                with sp.Fori(0, B) as b:
                    with sp.Fori(0, GH // SLOTS) as g:
                        for s in range(SLOTS):
                            sp.wait_ge(x_free, b * GH + g * SLOTS + (s + 1))
                            sp.dma_start(xin[:, s, :], x[:, b, g * SLOTS + s, :]).then_inc(x_in[s], 16)

            @block.vector
            def _(dve):
                dve.sem_inc(x_free, SLOTS)
                with dve.Fori(0, NT // SLOTS) as g:
                    for s in range(SLOTS):
                        dve.wait_ge(x_in[s], g * 16 + 16)
                        for q in range(RT // 512):
                            nc.vector.bn_stats(
                                stats[:, bass.ds(g * (SLOTS * 24) + (s * 24 + q * 6), 6)],
                                xin[:, s, q * 512:(q + 1) * 512])
                        nc.vector.tensor_reduce(
                            pooled[:, bass.ds(g * (SLOTS * GW) + s * GW, GW)],
                            xin[:, s, :].rearrange("c (r w k) -> c w r k", r=GS, k=GS),
                            AX.XY, ALU.max).then_inc(x_free, 1)


def group_coefficients(core, w, name, stats, gscale, gbias):
    nc = core.nc
    with core.stage() as k:
        mv = k.sb(name + "mv", [C, B, 2])
        s2 = k.sb(name + "s2", [C, 2, B])
        gs = k.sb(name + "gs", [C, 2, B])
        var = k.sb(name + "var", [C, B])
        std = k.sb(name + "std", [C, B])
        pg = k.ps(name + "pg", [C, 512])
        step, grouped, rooted = k.sem(name + "step"), k.sem(name + "grouped"), k.sem(name + "rooted")
        per = NT // B * 24
        with nc.Block() as block:
            @block.vector
            def _(dve):
                for b in range(B):
                    last = nc.vector.bn_aggr(mv[:, b, :], stats[:, b * per:(b + 1) * per])
                last.then_inc(step, 1)
                dve.wait_ge(step, 1)
                nc.vector.tensor_tensor(var[:], mv[:, :, 0], mv[:, :, 0], ALU.mult)
                nc.vector.tensor_copy(s2[:, 0, :], mv[:, :, 0]).then_inc(step, 1)
                dve.wait_ge(step, 2)
                nc.vector.tensor_tensor(s2[:, 1, :], var[:], mv[:, :, 1], ALU.add).then_inc(step, 1)
                dve.wait_ge(grouped, 1)
                nc.vector.tensor_copy(gs[:], pg[:, 0:2 * B].rearrange("c (a b) -> c a b", a=2)).then_inc(step, 1)
                dve.wait_ge(step, 4)
                nc.vector.tensor_tensor(var[:], gs[:, 0, :], gs[:, 0, :], ALU.mult).then_inc(step, 1)
                dve.wait_ge(step, 5)
                nc.vector.tensor_tensor(std[:], gs[:, 1, :], var[:], ALU.subtract).then_inc(step, 1)
                dve.wait_ge(step, 6)
                nc.vector.tensor_scalar(var[:], std[:], GEPS, None, ALU.add).then_inc(step, 1)
                dve.wait_ge(rooted, 1)
                nc.vector.reciprocal(gscale[:], std[:]).then_inc(step, 1)
                dve.wait_ge(step, 8)
                nc.vector.tensor_tensor(std[:], gscale[:], gscale[:], ALU.mult).then_inc(step, 1)
                dve.wait_ge(step, 9)
                nc.vector.scalar_tensor_tensor(mv[:, :, 0], std[:], -0.5, var[:], ALU.mult, ALU.mult).then_inc(step, 1)
                dve.wait_ge(step, 10)
                nc.vector.scalar_tensor_tensor(gscale[:], mv[:, :, 0], 1.5, gscale[:], ALU.add, ALU.mult
                                               ).then_inc(step, 1)
                dve.wait_ge(step, 11)
                nc.vector.scalar_tensor_tensor(gbias[:], gs[:, 0, :], -1.0, gscale[:], ALU.mult, ALU.mult)

            @block.tensor
            def _(pe):
                pe.wait_ge(step, 3)
                nc.tensor.matmul(pg[:, 0:2 * B], w["group"][:], s2[:].rearrange("c a b -> c (a b)"),
                                 start=True, stop=True).then_inc(grouped, 1)

            @block.scalar
            def _(act):
                act.wait_ge(step, 7)
                nc.scalar.activation(std[:], var[:], ACT.Sqrt).then_inc(rooted, 1)


def top_windows(core, pooled, gscale, gbias, nbr_w, nbr_i):
    nc = core.nc
    T = NW // 128
    HALF = 1024
    with core.stage() as k:
        score = k.sb("score", [128, 2, NW])
        own = k.sb("own", [C, 2, 128])
        top = k.sb("top", [128, 2, 8])
        place = k.sb("place", [128, 2, 8], U32)
        tops = k.sb("tops", [128, T, 8])
        places = k.sb("places", [128, T, 8], U32)
        diff = k.sb("diff", [128, T, TOPK])
        ex = k.sb("ex", [128, T, TOPK])
        tot = k.sb("tot", [128, T])
        rtot = k.sb("rtot", [128, T])
        ps = [k.ps(f"sim{i}", [128, HALF]) for i in range(4)]
        normed, own_ready, sim, copied, step, kept, exped, fin = (
            k.sem("b_" + n) for n in ("normed", "own_ready", "sim", "copied", "step", "kept", "exped", "fin"))
        Q = NW // HALF
        with nc.Block() as block:
            @block.gpsimd
            def _(pool):
                pool.wait_ge(normed, 1)
                with pool.Fori(0, T // 2) as i:
                    for u in range(2):
                        pool.wait_ge(sim, (i * 2 + u) * Q)
                        nc.gpsimd.tensor_copy(own[:, u, :], pooled[:, bass.ds((i * 2 + u) * 128, 128)]
                                              ).then_inc(own_ready, 1)

            @block.tensor
            def _(pe):
                pe.sem_inc(sim, Q)
                pe.wait_ge(normed, 1)
                with pe.Fori(0, T // 2) as i:
                    for u in range(2):
                        pe.wait_ge(own_ready, i * 2 + (u + 1))
                        for q in range(Q):
                            pe.wait_ge(copied, (i * 2 + u) * Q + q)
                            for h in range(2):
                                mm = nc.tensor.matmul(ps[q][:, h * 512:(h + 1) * 512], own[:, u, :],
                                                      pooled[:, q * HALF + h * 512:q * HALF + (h + 1) * 512],
                                                      start=True, stop=True)
                            mm.then_inc(sim, 1)

            @block.scalar
            def _(act):
                act.sem_inc(copied, Q - 1)
                act.sem_inc(kept, 2)
                with act.Fori(0, T // 2) as i:
                    for u in range(2):
                        act.wait_ge(kept, i * 2 + (u + 1))
                        for q in range(Q):
                            act.wait_ge(sim, (i * 2 + u) * Q + (q + 1 + Q))
                            nc.scalar.copy(score[:, u, q * HALF:(q + 1) * HALF], ps[q][:]).then_inc(copied, 1)
                act.wait_ge(step, 1)
                nc.scalar.activation(ex[:], diff[:], ACT.Exp).then_inc(exped, 1)

            @block.vector
            def _(dve):
                for b in range(B):
                    sl = pooled[:, b * GH * GW:(b + 1) * GH * GW]
                    last = nc.vector.tensor_scalar(sl, sl, gscale[:, b:b + 1], gbias[:, b:b + 1],
                                                   ALU.mult, ALU.add)
                last.then_inc(normed, 1)
                with dve.Fori(0, T // 2) as i:
                    for u in range(2):
                        dve.wait_ge(copied, (i * 2 + u) * Q + (2 * Q - 1))
                        core.apart(dve)
                        nc.vector.max(top[:, u, :], score[:, u, :]).then_inc(fin, 1)
                        dve.wait_ge(fin, (i * 2 + u) * 2 + 1)
                        core.apart(dve)
                        nc.vector.max_index(place[:, u, :], top[:, u, :], score[:, u, :]).then_inc(fin, 1)
                        dve.wait_ge(fin, (i * 2 + u) * 2 + 2)
                        nc.vector.tensor_copy(tops[:, i * 2 + u, :], top[:, u, :])
                        nc.vector.tensor_copy(places[:, i * 2 + u, :], place[:, u, :]).then_inc(kept, 1)
                dve.wait_ge(kept, T + 2)
                nc.vector.tensor_tensor(diff[:], tops[:, :, 0:TOPK], tops[:, :, 0:1].to_broadcast([128, T, TOPK]),
                                        ALU.subtract).then_inc(step, 1)
                nc.vector.tensor_copy(nbr_i[:], places[:, :, 0:TOPK])
                dve.wait_ge(exped, 1)
                nc.vector.tensor_reduce(tot[:], ex[:], AX.X, ALU.add).then_inc(step, 1)
                dve.wait_ge(step, 2)
                nc.vector.reciprocal(rtot[:], tot[:]).then_inc(step, 1)
                dve.wait_ge(step, 3)
                nc.vector.tensor_tensor(nbr_w[:], ex[:], rtot[:].unsqueeze(2).to_broadcast([128, T, TOPK]), ALU.mult)


def window_convs(core, w, wconv, gscale, gbias):
    nc, d = core.nc, core.d
    x = d["x"].rearrange("b c (g r) w -> c b g (r w)", r=GS)
    part = d["part"]
    xg = d["xg"].rearrange("(t n) (c s) -> c t n s", n=GW, c=C)
    Q = 8
    M = GH // Q
    NS = 4
    TG = Q * PAIRS // 4
    GPR = TG // Q
    MG = C // 8
    with core.stage() as k:
        xr = k.sb("l_xr", [C, Q, RT])
        xn = k.sb("l_xn", [C, NS, GW, P])
        xt = k.sb("l_xt", [128, Q * PAIRS, C])
        lc = k.sb("l_lc", [C + 1, 2, 512])
        coef = k.sb("l_coef", [C, 2])
        pt = [k.ps(f"l_pt{i}", [128, 512]) for i in range(2)]
        pm = [k.ps(f"l_pm{i}", [128, 8, Q * PAIRS]) for i in range(2)]
        pw = [k.ps(f"l_pw{i}", [C, 8, GS, GS]) for i in range(2)]
        x_in = [k.sem(f"l_x_in{q}") for q in range(Q)]
        part_out = [k.sem(f"l_part_out{q}") for q in range(Q)]
        xg_out = [k.sem(f"l_xg_out{s}") for s in range(NS)]
        (coef_set, xn_ready, turned, turned_dve, turned_act, conved, conved_dve, conved_act, back, back_out,
         projected, added, ones, freed) = (
            k.sem("l_" + n) for n in ("coef_set", "xn_ready", "turned", "turned_dve", "turned_act", "conved",
                                      "conved_dve", "conved_act", "back", "back_out", "projected", "added",
                                      "ones", "freed"))

        def turn_out(copy, g):
            return copy(xt[:, g * 4:(g + 1) * 4, :], pt[g % 2][:, 0:4 * C].rearrange("p (n c) -> p n c", n=4))

        def conv_out(copy, g):
            return copy(xt[:, :, g * 8:(g + 1) * 8].rearrange("p n c -> p c n"), pm[g % 2][:])

        with nc.Block() as block:
            @block.sync
            def _(sp):
                with sp.Fori(0, B) as b:
                    with sp.Fori(0, M) as m:
                        for q in range(Q):
                            sp.wait_ge(freed, (b * M + m) * Q + (q + 1))
                            sp.dma_start(xr[:, q, :], x[:, b, m * Q + q, :]).then_inc(x_in[q], 16)

            @block.scalar
            def _(act):
                act.sem_inc(back_out, 2)
                act.sem_inc(conved_act, 1)
                for s in range(NS):
                    act.sem_inc(xg_out[s], 16)
                with act.Fori(0, B) as b:
                    nc.scalar.copy(coef[:, 0:1], gscale[:, bass.ds(b, 1)])
                    nc.scalar.copy(coef[:, 1:2], gbias[:, bass.ds(b, 1)]).then_inc(coef_set, 1)
                    act.wait_ge(coef_set, b + 1)
                    with act.Fori(0, M) as m:
                        j = b * M + m
                        for q in range(Q + 1):
                            if q < Q:
                                act.wait_ge(x_in[q], j * 16 + 16)
                                act.wait_ge(xg_out[q % NS], j * (Q // NS * 16) + (q // NS * 16 + 16))
                                if q >= NS:
                                    act.wait_ge(turned, j * TG + (q - NS + 1) * GPR)
                                nc.scalar.activation(
                                    xn[:, q % NS, :, :].rearrange("c n (r k) -> c n r k", r=GS),
                                    xr[:, q, :].rearrange("c (r n k) -> c n r k", r=GS, k=GS), ACT.Identity,
                                    scale=coef[:, 0:1], bias=coef[:, 1:2]).then_inc(xn_ready, 1)
                            if q:
                                act.wait_ge(xn_ready, j * Q + q)
                                nc.scalar.dma_start(xg[:, j * Q + (q - 1), :, :], xn[:, (q - 1) % NS, :, :]
                                                    ).then_inc(xg_out[(q - 1) % NS], 16)
                                for g in range((q - 1) * GPR + 1, q * GPR, 2):
                                    act.wait_ge(turned, j * TG + (g + 1))
                                    turn_out(nc.scalar.copy, g).then_inc(turned_act, 1)
                        for g in range(1, MG, 2):
                            act.wait_ge(conved, j * MG + (g + 1))
                            conv_out(nc.scalar.copy, g).then_inc(conved_act, 1)
                        for g in range(TG):
                            act.wait_ge(back, j * TG + (g + 1))
                            if g == 0:
                                act.wait_ge(ones, 1)
                            nc.scalar.copy(lc[0:C, g % 2, :], pt[g % 2][0:C, :]).then_inc(back_out, 1)
                for s in range(NS):
                    act.wait_ge(xg_out[s], B * M * (Q // NS) * 16 + 16)

            @block.vector
            def _(dve):
                dve.sem_inc(conved_dve, 1)
                dve.sem_inc(added, 2)
                nc.vector.memset(lc[C:C + 1, :, :], 1.0).then_inc(ones, 1)
                with dve.Fori(0, B * M) as j:
                    for g in range(0, TG, 2):
                        dve.wait_ge(turned, j * TG + (g + 1))
                        turn_out(nc.vector.tensor_copy, g).then_inc(turned_dve, 1)
                    for g in range(0, MG, 2):
                        dve.wait_ge(conved, j * MG + (g + 1))
                        conv_out(nc.vector.tensor_copy, g).then_inc(conved_dve, 1)
                    for g in range(TG):
                        q, s = g // GPR, g % GPR
                        dve.wait_ge(projected, j * TG + (g + 1))
                        res = xr[:, q, :].rearrange("c (r n k) -> c n r k", r=GS, k=GS)[:, s * 8:(s + 1) * 8]
                        nc.vector.tensor_tensor(res, pw[g % 2][:], res, ALU.add).then_inc(added, 1)

            @block.gpsimd
            def _(pool):
                pool.sem_inc(freed, Q)
                with pool.Fori(0, B * M) as j:
                    for q in range(Q + 1):
                        if q < Q:
                            pool.wait_ge(added, j * TG + ((q + 1) * GPR + 2))
                            core.apart(pool)
                            pool.dma_start(part[:, j * Q + q, :], xr[:, q, :]).then_inc(part_out[q], 16)
                        if q:
                            pool.wait_ge(part_out[q - 1], j * 16 + 16)
                            pool.sem_inc(freed, 1)

            @block.tensor
            def _(pe):
                def project(j, g):
                    pe.wait_ge(back_out, j * TG + (g + 3))
                    pe.wait_ge(added, j * TG + (g + 1))
                    nc.tensor.matmul(pw[g % 2][:].rearrange("c n r k -> c (n r k)"), w["wp1"][:], lc[:, g % 2, :],
                                     start=True, stop=True).then_inc(projected, 1)

                pe.wait_ge(ones, 1)
                with pe.Fori(0, B * M) as j:
                    for g in range(TG):
                        if g < 2:
                            pe.wait_ge(back_out, j * TG + (g + 1))
                        else:
                            pe.wait_ge(turned_act if g % 2 else turned_dve, j * (TG // 2) + g // 2)
                        if g % GPR == 0:
                            pe.wait_ge(xn_ready, j * Q + (g // GPR + 1))
                        for i in range(4):
                            pair = (g % GPR) * 4 + i
                            mm = nc.tensor.transpose(
                                pt[g % 2][:, i * C:(i + 1) * C],
                                xn[:, g // GPR % NS, 2 * pair:2 * pair + 2, :].rearrange("c n s -> c (n s)"),
                                w["ident"][0:C, 0:C])
                        mm.then_inc(turned, 1)
                    pe.wait_ge(turned_dve, j * (TG // 2) + TG // 2)
                    pe.wait_ge(turned_act, j * (TG // 2) + TG // 2)
                    for g in range(MG):
                        pe.wait_ge(conved_act if g % 2 else conved_dve, j * (MG // 2) + (g // 2 + 1))
                        for i in range(8):
                            c = g * 8 + i
                            mm = nc.tensor.matmul(pm[g % 2][:, i, :], wconv[:, c * 128:(c + 1) * 128], xt[:, :, c],
                                                  start=True, stop=True)
                        mm.then_inc(conved, 1)
                    pe.wait_ge(conved_dve, j * (MG // 2) + (MG // 2 + 1))
                    pe.wait_ge(conved_act, j * (MG // 2) + (MG // 2 + 1))
                    for g in range(TG):
                        pe.wait_ge(back_out, j * TG + (g + 1))
                        for i in range(4):
                            mm = nc.tensor.transpose(pt[g % 2][0:C, i * 128:(i + 1) * 128], xt[:, g * 4 + i, :],
                                                     w["ident"][:])
                        mm.then_inc(back, 1)
                        if g:
                            project(j, g - 1)
                    project(j, TG - 1)


def gather_context(core, nbr_w, nbr_i):
    nc, d = core.nc, core.d
    T = NW // 128
    HALVES = 2
    ROW = C * P // HALVES
    xg = d["xg"].rearrange("n (h v) -> (n h) v", h=HALVES)
    ctx_out = d["ctx"].rearrange("(t n) (h v) -> n t h v", n=128, h=HALVES)
    with core.stage() as k:
        rows = k.sb("c_rows", [128, HALVES, TOPK, ROW])
        every = k.sb("c_every", [128, T, HALVES, TOPK], U32)
        idx = k.sb("c_idx", [128, HALVES, TOPK], U32)
        got = [k.sem(f"c_got{h}") for h in range(HALVES)]
        out = [k.sem(f"c_out{h}") for h in range(HALVES)]
        every_set, idx_set, summed = k.sem("c_every_set"), k.sem("c_idx_set"), k.sem("c_summed")
        with nc.Block() as block:
            @block.gpsimd
            def _(pool):
                pool.wait_ge(every_set, 1)
                with pool.Fori(0, T) as t:
                    for h in range(HALVES):
                        pool.wait_ge(out[h], t * 16)
                        nc.gpsimd.tensor_copy(idx[:, h, :], every[:, t, h, :]).then_inc(idx_set, 1)
                        pool.wait_ge(idx_set, t * HALVES + (h + 1))
                        core.apart(pool)
                        for j in range(TOPK):
                            pool.indirect_dma_start(rows[:, h, j, :], None, xg[:],
                                                    bass.IndirectOffsetOnAxis(idx[:, h, j:j + 1], 0)
                                                    ).then_inc(got[h], 16)

            @block.vector
            def _(dve):
                for h in range(HALVES):
                    last = nc.vector.tensor_scalar(every[:, :, h, :], nbr_i[:], float(HALVES), float(h),
                                                   ALU.mult, ALU.add)
                last.then_inc(every_set, 1)
                with dve.Fori(0, T) as t:
                    for h in range(HALVES):
                        dve.wait_ge(got[h], t * (16 * TOPK) + 16 * TOPK)
                        for j in range(TOPK):
                            wj = nbr_w[:, t, j:j + 1]
                            if j == 0:
                                ins = nc.vector.tensor_scalar(rows[:, h, 0, :], rows[:, h, 0, :], wj, None, ALU.mult)
                            else:
                                dve.wait_ge(summed, (t * HALVES + h) * TOPK + j)
                                ins = nc.vector.scalar_tensor_tensor(rows[:, h, 0, :], rows[:, h, j, :], wj,
                                                                     rows[:, h, 0, :], ALU.mult, ALU.add)
                            ins.then_inc(summed, 1)

            @block.sync
            def _(sp):
                with sp.Fori(0, T) as t:
                    for h in range(HALVES):
                        sp.wait_ge(summed, (t * HALVES + h) * TOPK + TOPK)
                        sp.dma_start(ctx_out[:, t, h, :], rows[:, h, 0, :]).then_inc(out[h], 16)
                for h in range(HALVES):
                    sp.wait_ge(out[h], T * 16)


def attend(core, w, stats):
    nc, d = core.nc, core.d
    UW = 16
    UT = UW * P
    N = NW // UW
    UPR = GW // UW
    SLOTS = 4
    BODY = SLOTS * UPR
    xg = d["xg"].rearrange("(t n) (c s) -> c t n s", n=GW, c=C)
    cg = d["ctx"].rearrange("(t n) (c s) -> c t n s", n=GW, c=C)
    part, x1 = d["part"], d["x1"]
    with core.stage() as k:
        xw = k.sb("d_xw", [C, SLOTS, GW, P])
        cx = k.sb("d_cx", [C + 1, SLOTS, GW, P])
        pr = k.sb("d_pr", [C, SLOTS, RT])
        tq = k.sb("d_tq", [C + 1, 2, UT])
        mx = k.sb("d_mx", [128, 2, 8])
        sm = k.sb("d_sm", [128, 2, 8])
        rs = k.sb("d_rs", [128, 2, 8])
        ex = k.sb("d_ex", [128, 2, 8, P])
        pn = k.sb("d_pn", [128, 2, 8, P])
        vt = k.sb("d_vt", [128, 2, 8, C])
        at = k.sb("d_at", [128, 2, UW, P])
        p_t = k.ps("d_p_t", [C + 1, UT])
        p_s = [k.ps(f"d_p_s{i}", [128, 8, P]) for i in range(2)]
        p_v = k.ps("d_p_v", [128, 512])
        p_a = k.ps("d_p_a", [128, 4, 128])
        p_o = k.ps("d_p_o", [C, UW, GS, GS])
        xw_in, cx_in, pr_in, x1_out = ([k.sem(f"d_{n}{s}") for s in range(SLOTS)]
                                       for n in ("xw_in", "cx_in", "pr_in", "x1_out"))
        (ones, queries, queries_out, scores, maxed, centred, exped, softmaxed, p_ready, values, values_out,
         turned, turned_out, attended, added, x1_ready) = (
            k.sem("d_" + n) for n in ("ones", "queries", "queries_out", "scores", "maxed", "centred", "exped",
                                      "softmaxed", "p_ready", "values", "values_out", "turned", "turned_out",
                                      "attended", "added", "x1_ready"))

        def wait(eng, sem, value):
            if not isinstance(value, int) or value > 0:
                eng.wait_ge(sem, value)

        def units(step):
            def over(eng):
                for j in range(-2, BODY):
                    step(j, j % BODY, j // BODY, lambda m: m >= 0)
                with eng.Fori(1, N // BODY - 1) as i:
                    for k in range(BODY):
                        step(i * BODY + k, k, i, lambda m: True)
                for j in range(N - BODY, N + 3):
                    step(j, j % BODY, j // BODY, lambda m: m < N)
            return over

        def landed(i, k):
            return (i + k // BODY) * 16 + 16

        def slot(k):
            return k % BODY // UPR

        with nc.Block() as block:
            @block.sync
            def _(sp):
                def load_x(r, s):
                    sp.dma_start(xw[:, s, :, :], xg[:, r, :, :]).then_inc(xw_in[s], 16)

                def load_ctx(r, s):
                    sp.dma_start(cx[0:C, s, :, :], cg[:, r, :, :]).then_inc(cx_in[s], 16)

                def load_part(r, s):
                    sp.dma_start(pr[:, s, :], part[:, r, :]).then_inc(pr_in[s], 16)

                def store(i, s):
                    r = i * SLOTS + s
                    sp.wait_ge(x1_ready, r * UPR + UPR)
                    sp.dma_start(x1[:, r, :], pr[:, s, :]).then_inc(x1_out[s], 16)

                for s in range(SLOTS):
                    load_x(s, s)
                    load_ctx(s, s)
                    load_part(s, s)
                with sp.Fori(0, NT // SLOTS - 1) as i:
                    for s in range(SLOTS):
                        r = i * SLOTS + s
                        sp.wait_ge(queries, r * UPR + UPR)
                        load_x(r + SLOTS, s)
                        sp.wait_ge(values, r * (2 * UPR) + 2 * UPR)
                        load_ctx(r + SLOTS, s)
                        store(i, s)
                        sp.wait_ge(x1_out[s], i * 16 + 16)
                        load_part(r + SLOTS, s)
                for s in range(SLOTS):
                    store(NT // SLOTS - 1, s)
                for s in range(SLOTS):
                    sp.wait_ge(x1_out[s], NT // SLOTS * 16)

            @block.tensor
            def _(pe):
                def make_queries(n, k, i):
                    if k % UPR == 0:
                        pe.wait_ge(xw_in[slot(k)], landed(i, k))
                    wait(pe, queries_out, n)
                    for h in range(2):
                        lo = (k % UPR) * UW + h * 8
                        mm = nc.tensor.matmul(p_t[:, h * 512:(h + 1) * 512], w["g"][:],
                                              xw[:, slot(k), lo:lo + 8, :].rearrange("c n s -> c (n s)"),
                                              start=True, stop=True)
                    mm.then_inc(queries, 1)

                def make_values(n, k, h):
                    wait(pe, values_out, n * 2 + h)
                    for j in range(4):
                        lo = (k % UPR) * UW + (h * 4 + j) * 2
                        mm = nc.tensor.matmul(p_v[:, j * C:(j + 1) * C],
                                              cx[0:C, slot(k), lo:lo + 2, :].rearrange("c n s -> c (n s)"),
                                              w["wvp"][:], start=True, stop=True)
                    mm.then_inc(values, 1)

                def score(n, k, i):
                    if k % UPR == 0:
                        pe.wait_ge(cx_in[slot(k)], landed(i, k))
                    pe.wait_ge(queries_out, n + 1)
                    wait(pe, centred, n - 1)
                    for v in range(UW):
                        half, col = v // 2 % 2, 2 * (v // 4) + v % 2
                        mm = nc.tensor.matmul(p_s[k % 2][half * P:(half + 1) * P, col, :],
                                              tq[:, k % 2, v * P:(v + 1) * P],
                                              cx[:, slot(k), (k % UPR) * UW + v, :], start=True, stop=True)
                    mm.then_inc(scores, 1)

                def turn(n, k):
                    pe.wait_ge(p_ready, n + 1)
                    wait(pe, turned_out, n)
                    for j in range(4):
                        mm = nc.tensor.transpose(p_a[:, j, :],
                                                 pn[:, k % 2, 2 * j:2 * j + 2, :].rearrange("p n s -> p (n s)"),
                                                 w["ident"][:])
                    mm.then_inc(turned, 1)

                def apply(n, k):
                    pe.wait_ge(turned_out, n + 1)
                    pe.wait_ge(values_out, n * 2 + 2)
                    wait(pe, added, n)
                    for j in range(UW // 2):
                        mm = nc.tensor.matmul(
                            p_o[:, 2 * j:2 * j + 2, :, :].rearrange("c n r k -> c (n r k)"), vt[:, k % 2, j, :],
                            at[:, k % 2, 2 * j:2 * j + 2, :].rearrange("p n s -> p (n s)"), start=True, stop=True)
                    mm.then_inc(attended, 1)

                def step(n, k, i, live):
                    if live(n + 2):
                        make_queries(n + 2, k + 2, i)
                    if live(n):
                        make_values(n, k, 0)
                    if live(n + 1):
                        score(n + 1, k + 1, i)
                    if live(n):
                        make_values(n, k, 1)
                        turn(n, k)
                    if live(n - 1):
                        apply(n - 1, k - 1)

                pe.wait_ge(ones, 1)
                units(step)(pe)

            @block.scalar
            def _(act):
                nc.scalar.preload_act_table(ACT.Exp)
                act.wait_ge(ones, 1)

                def step(n, k, i, live):
                    if live(n + 2):
                        act.wait_ge(queries, n + 3)
                        nc.scalar.activation(tq[:, k % 2, :], p_t[:], ACT.Identity, bias=w["gb"][:, 0:1]
                                             ).then_inc(queries_out, 1)
                    for h in range(2):
                        if live(n):
                            act.wait_ge(values, n * 2 + (h + 1))
                            nc.scalar.copy(vt[:, k % 2, h * 4:(h + 1) * 4, :],
                                           p_v[:, 0:4 * C].rearrange("p (n c) -> p n c", n=4)).then_inc(values_out, 1)
                    if live(n):
                        act.wait_ge(turned, n + 1)
                        for h in range(2):
                            ins = nc.scalar.copy(at[h * P:(h + 1) * P, k % 2, h::2, :],
                                                 p_a[h * P:(h + 1) * P, :, :].rearrange("p i (n s) -> p (i n) s", n=2))
                        ins.then_inc(turned_out, 1)
                    if live(n + 1):
                        act.wait_ge(centred, n + 2)
                        e = ex[:, (k + 1) % 2, :, :]
                        nc.scalar.activation(e, e, ACT.Exp, scale=SCALE).then_inc(exped, 1)

                units(step)(act)

            @block.vector
            def _(dve):
                nc.vector.memset(at[:], 0.0)
                nc.vector.memset(cx[C:C + 1, :, :, :], 1.0).then_inc(ones, 1)

                def step(n, k, i, live):
                    m, s = n + 1, (k + 1) % 2
                    if live(m):
                        dve.wait_ge(scores, m + 1)
                        nc.vector.tensor_reduce(mx[:, s, :], p_s[s][:], AX.X, ALU.max).then_inc(maxed, 1)
                        dve.wait_ge(maxed, m + 1)
                        nc.vector.tensor_tensor(ex[:, s, :, :], p_s[s][:],
                                                mx[:, s, :].unsqueeze(2).to_broadcast([128, 8, P]),
                                                ALU.subtract).then_inc(centred, 1)
                    if live(n - 2):
                        o, q = n - 2, k - 2
                        half = q % UPR
                        if half == 0:
                            dve.wait_ge(pr_in[slot(q)], landed(i, q))
                        dve.wait_ge(attended, o + 1)
                        rows = pr[:, slot(q), :].rearrange("c (r w) -> c r w", r=GS)
                        res = rows[:, :, half * 128:half * 128 + 128].rearrange("c r (n k) -> c n r k", k=GS)
                        nc.vector.tensor_tensor(res, p_o[:], res, ALU.add).then_inc(added, 1)
                        dve.wait_ge(added, o + 1)
                        for h in range(2):
                            st = stats[:, bass.ds(o * 12 + h * 6, 6)] if not isinstance(o, int) else \
                                stats[:, o * 12 + h * 6:o * 12 + h * 6 + 6]
                            ins = nc.vector.bn_stats(st, rows[:, h * 4:h * 4 + 4, half * 128:half * 128 + 128])
                        ins.then_inc(x1_ready, 1)
                    if live(m):
                        dve.wait_ge(exped, m + 1)
                        nc.vector.tensor_reduce(sm[:, s, :], ex[:, s, :, :], AX.X, ALU.add).then_inc(softmaxed, 1)
                        dve.wait_ge(softmaxed, m * 2 + 1)
                        nc.vector.reciprocal(rs[:, s, :], sm[:, s, :]).then_inc(softmaxed, 1)
                        dve.wait_ge(softmaxed, m * 2 + 2)
                        nc.vector.tensor_tensor(pn[:, s, :, :], ex[:, s, :, :],
                                                rs[:, s, :].unsqueeze(2).to_broadcast([128, 8, P]),
                                                ALU.mult).then_inc(p_ready, 1)

                units(step)(dve)


HALF = 1024
TILE = 2 * HALF
NTILE = B * L // TILE


def tokens(ap):
    if len(ap.shape) == 3:
        ap = ap.rearrange("c a b -> c (a b)")
    return ap.rearrange("c (t n) -> c t n", n=TILE)


def image_units(n, body, step, start=lambda b: None, ahead=2):
    def over(eng):
        with eng.Fori(0, B) as b:
            start(b)
            for j in range(-ahead, body):
                step(b * n + j, j % body, b, j // body, lambda o, j=j: j + o >= 0)
            with eng.Fori(1, n // body - 1) as i:
                for j in range(body):
                    step(b * n + i * body + j, j, b, i, lambda o: True)
            for j in range(n - body, n):
                step(b * n + j, j % body, b, j // body, lambda o, j=j: j + o < n)
    return over


def project_in(core, w, gscale, gbias):
    nc, d = core.nc, core.d
    x1, xc, zs = tokens(d["x1"]), tokens(d["xc"]), tokens(d["zs"])
    PER = NTILE // B
    with core.stage() as k:
        xi = k.sb("p_xi", [C, 4, TILE])
        xo = k.sb("p_xo", [C, 2, TILE])
        zo = k.sb("p_zo", [C, 2, TILE])
        wcur = k.sb("p_wcur", [C, 2 * C])
        bias = k.sb("p_bias", [C, 2, B])
        bcur = k.sb("p_bcur", [C, 2])
        px = [k.ps(f"p_px{i}", [C, HALF]) for i in range(2)]
        pz = [k.ps(f"p_pz{i}", [C, HALF]) for i in range(2)]
        x_in = [k.sem(f"p_x_in{s}") for s in range(4)]
        xc_out, zs_out = ([k.sem(f"p_{n}{s}") for s in range(2)] for n in ("xc_out", "zs_out"))
        biased, bias_set, w_set, b_set, made, xc_ready, zs_ready = (
            k.sem("p_" + n) for n in ("biased", "bias_set", "w_set", "b_set", "made", "xc_ready", "zs_ready"))
        with nc.Block() as block:
            @block.sync
            def _(sp):
                with sp.Fori(0, NTILE // 4) as i:
                    for s in range(4):
                        sp.wait_ge(made, i * 8 + (2 * s + 2))
                        sp.dma_start(xi[:, s, :], x1[:, i * 4 + s, :]).then_inc(x_in[s], 16)

            @block.tensor
            def _(pe):
                pe.sem_inc(made, 8)
                for h in range(2):
                    mm = nc.tensor.matmul(px[0][:, h * B:(h + 1) * B], w["inw"][:, h * C:(h + 1) * C], gbias[:],
                                          start=True, stop=True)
                mm.then_inc(biased, 1)
                pe.wait_ge(bias_set, 1)
                with pe.Fori(0, B) as b:
                    pe.wait_ge(w_set, b + 1)
                    core.apart(pe)
                    with pe.Fori(0, PER // 4) as i:
                        for s in range(4):
                            pe.wait_ge(x_in[s], b * (PER // 4 * 16) + i * 16 + 16)
                            for h in range(2):
                                n = b * (2 * PER) + i * 8 + (2 * s + h)
                                pe.wait_ge(xc_ready, n + 1)
                                pe.wait_ge(zs_ready, n + 1)
                                for p, lo in ((px, 0), (pz, C)):
                                    for q in range(2):
                                        mm = nc.tensor.matmul(
                                            p[h][:, q * 512:(q + 1) * 512], wcur[:, lo:lo + C],
                                            xi[:, s, h * HALF + q * 512:h * HALF + (q + 1) * 512],
                                            start=True, stop=True)
                                mm.then_inc(made, 1)

            @block.vector
            def _(dve):
                dve.sem_inc(xc_ready, 2)
                dve.wait_ge(biased, 1)
                nc.vector.tensor_copy(bias[:], px[0][:, 0:2 * B].rearrange("c (h b) -> c h b", h=2)
                                      ).then_inc(bias_set, 1)
                dve.wait_ge(bias_set, 1)
                with dve.Fori(0, B) as b:
                    dve.wait_ge(made, b * (2 * PER) + 8)
                    nc.vector.tensor_scalar(wcur[:], w["inw"][:], gscale[:, bass.ds(b, 1)], None, ALU.mult
                                            ).then_inc(w_set, 1)
                    dve.wait_ge(zs_ready, b * (2 * PER) + 2)
                    dve.wait_ge(xc_ready, b * (2 * PER) + 2)
                    nc.vector.tensor_copy(bcur[:], bias[:, :, b]).then_inc(b_set, 1)
                    dve.wait_ge(b_set, b + 1)
                    core.apart(dve)
                    with dve.Fori(0, PER // 2) as i:
                        for s in range(2):
                            dve.wait_ge(xc_out[s], b * (PER // 2 * 16) + i * 16)
                            for h in range(2):
                                dve.wait_ge(made, b * (2 * PER) + i * 4 + (2 * s + h + 9))
                                nc.vector.tensor_scalar(xo[:, s, h * HALF:(h + 1) * HALF], px[h][:],
                                                        bcur[:, 0:1], None, ALU.add).then_inc(xc_ready, 1)

            @block.scalar
            def _(act):
                nc.scalar.preload_act_table(ACT.Silu)
                act.sem_inc(zs_ready, 2)
                with act.Fori(0, B) as b:
                    act.wait_ge(b_set, b + 1)
                    with act.Fori(0, PER // 2) as i:
                        for s in range(2):
                            act.wait_ge(zs_out[s], b * (PER // 2 * 16) + i * 16)
                            for h in range(2):
                                act.wait_ge(made, b * (2 * PER) + i * 4 + (2 * s + h + 9))
                                nc.scalar.activation(zo[:, s, h * HALF:(h + 1) * HALF], pz[h][:], ACT.Silu,
                                                     bias=bcur[:, 1:2]).then_inc(zs_ready, 1)

            @block.gpsimd
            def _(pool):
                with pool.Fori(0, NTILE // 2) as i:
                    for s in range(2):
                        for ready, outs, to, src in ((xc_ready, xc_out, xc, xo), (zs_ready, zs_out, zs, zo)):
                            pool.wait_ge(ready, i * 4 + (2 * s + 4))
                            core.apart(pool)
                            pool.dma_start(to[:, i * 2 + s, :], src[:, s, :]).then_inc(outs[s], 16)
                for s in range(2):
                    pool.wait_ge(xc_out[s], NTILE // 2 * 16)
                    pool.wait_ge(zs_out[s], NTILE // 2 * 16)


def image_convs(core, w):
    nc, d = core.nc, core.d
    halves = d["xc"].rearrange("c (b t p) w -> c p t b w", b=B, p=128)
    xc = d["xc"].rearrange("c (b h) w -> c b h w", b=B)
    u = d["u"].rearrange("c (b h) w -> c b h w", b=B)
    T = H // 128
    GROUPS = T * B // 2
    NS = C // SEAM
    KS, MS = SEAM * B * 4, SEAM * B * 2
    with core.stage() as k:
        rows = k.sb("v_rows", [128, 3, 128])
        taps = k.sb("v_taps", [128, C * 9])
        cb = k.sb("v_cb", [128, C])
        xi = k.sb("v_xi", [128, 3, T, B, W + 2])
        band = k.sb("v_band", [128, 2, 3, 128])
        cbc = k.sb("v_cbc", [128, 2])
        uo = k.sb("v_uo", [128, 2, T, B, W])
        seams = k.sb("v_seams", [KS, 3, MS])
        seam_taps = k.sb("v_seam_taps", [KS, NS, 9])
        seam_cb = k.sb("v_seam_cb", [MS, NS])
        seam_band = k.sb("v_seam_band", [KS, NS, 3, MS])
        seam_x = k.sb("v_seam_x", [KS, NS, W + 2])
        seam_u = k.sb("v_seam_u", [MS, NS, W])
        pc = [k.ps(f"v_pc{i}", [128, 2, W]) for i in range(2 * GROUPS)]
        consts, zeroed, built, banded, made, acted, seam_in, seam_built, seam_made, seam_acted, seam_out = (
            k.sem("v_" + n) for n in ("consts", "zeroed", "built", "banded", "made", "acted", "seam_in",
                                      "seam_built", "seam_made", "seam_acted", "seam_out"))
        freed = k.sem("v_freed")
        x_in = [k.sem(f"v_x_in{s}") for s in range(3)]
        u_out = [k.sem(f"v_u_out{s}") for s in range(2)]
        STEPS = 6
        with nc.Block() as block:
            @block.sync
            def _(sp):
                loads = [(rows[:], d["rows"]), (taps[:], d["conv_w"].partition_broadcast(128)),
                         (cb[:], d["conv_b"].partition_broadcast(128)), (seams[:], d["seams"]),
                         (seam_taps[:], d["seam_taps"]), (seam_cb[:], d["seam_cb"])]
                for to, src in loads:
                    sp.dma_start(to, src).then_inc(consts, 16)
                sp.wait_ge(zeroed, 1)
                with sp.Fori(0, C // STEPS) as i:
                    for j in range(STEPS):
                        sp.wait_ge(made, i * (STEPS * GROUPS) + (j + 1) * GROUPS)
                        for t in range(T):
                            sp.dma_start(xi[:, j % 3, t, :, 1:W + 1], halves[i * STEPS + j, :, t, :, :]
                                         ).then_inc(x_in[j % 3], 16)
                for g in range(NS):
                    for c in range(SEAM):
                        sp.dma_start(seam_x[c * B * 4:(c + 1) * B * 4, g, 1:W + 1],
                                     xc[g * SEAM + c, :, H // 2 - 2:H // 2 + 2, :]).then_inc(seam_in, 16)
                for g in range(NS):
                    sp.wait_ge(seam_acted, g + 1)
                    for c in range(SEAM):
                        sp.dma_start(u[g * SEAM + c, :, H // 2 - 1:H // 2 + 1, :],
                                     seam_u[c * B * 2:(c + 1) * B * 2, g, :]).then_inc(seam_out, 16)
                sp.wait_ge(seam_out, 16 * C)

            @block.vector
            def _(dve):
                nc.vector.memset(seam_x[:], 0.0)
                nc.vector.memset(xi[:], 0.0).then_inc(zeroed, 1)
                dve.wait_ge(consts, 96)
                with dve.Fori(0, C // 2) as i:
                    for s in range(2):
                        dve.wait_ge(made, i * (2 * GROUPS) + (s + 2) * GROUPS)
                        dve.wait_ge(acted, i * (2 * GROUPS) + (s + 1) * GROUPS)
                        nc.vector.tensor_copy(cbc[:, s:s + 1], cb[:, bass.ds(i * 2 + s, 1)])
                        for dy in range(3):
                            if dy:
                                dve.wait_ge(built, (i * 2 + s) * 2 + dy)
                            for dx in range(3):
                                tap = taps[:, bass.ds(i * 18 + (s * 9 + dy * 3 + dx), 1)]
                                to = band[:, s, dx, :]
                                if dy == 0:
                                    ins = nc.vector.tensor_scalar(to, rows[:, dy, :], tap, None, ALU.mult)
                                else:
                                    ins = nc.vector.scalar_tensor_tensor(to, rows[:, dy, :], tap, to,
                                                                         ALU.mult, ALU.add)
                            ins.then_inc(banded if dy == 2 else built, 1)
                for dy in range(3):
                    if dy:
                        dve.wait_ge(seam_built, dy)
                    for g in range(NS):
                        for dx in range(3):
                            tap = seam_taps[:, g, dy * 3 + dx:dy * 3 + dx + 1]
                            to = seam_band[:, g, dx, :]
                            if dy == 0:
                                ins = nc.vector.tensor_scalar(to, seams[:, dy, :], tap, None, ALU.mult)
                            else:
                                ins = nc.vector.scalar_tensor_tensor(to, seams[:, dy, :], tap, to,
                                                                     ALU.mult, ALU.add)
                    ins.then_inc(seam_built, 1)

            @block.tensor
            def _(pe):
                pe.sem_inc(made, 3 * GROUPS)
                with pe.Fori(0, C // STEPS) as i:
                    for j in range(STEPS):
                        pe.wait_ge(banded, i * STEPS + (j + 1))
                        pe.wait_ge(x_in[j % 3], (i * 2 + (j // 3 + 1)) * (16 * T))
                        for g in range(GROUPS):
                            pe.wait_ge(acted, i * (STEPS * GROUPS) + (j * GROUPS + g + 1))
                            t, b = g // 2, g % 2 * 2
                            for dx in range(3):
                                mm = nc.tensor.matmul(pc[j % 2 * GROUPS + g][:], band[:, j % 2, dx, :],
                                                      xi[:, j % 3, t, b:b + 2, dx:dx + W],
                                                      start=(dx == 0), stop=(dx == 2))
                            mm.then_inc(made, 1)
                pe.wait_ge(seam_built, 3)
                pe.wait_ge(seam_in, 16 * C)
                pe.wait_ge(acted, (C + 2) * GROUPS)
                for g in range(NS):
                    if g >= 2 * GROUPS:
                        pe.wait_ge(seam_acted, g - 2 * GROUPS + 1)
                    for dx in range(3):
                        mm = nc.tensor.matmul(pc[g % (2 * GROUPS)][0:MS, 0, :], seam_band[:, g, dx, :],
                                              seam_x[:, g, dx:dx + W], start=(dx == 0), stop=(dx == 2))
                    mm.then_inc(seam_made, 1)

            @block.scalar
            def _(act):
                nc.scalar.preload_act_table(ACT.Silu)
                act.sem_inc(acted, 2 * GROUPS)
                with act.Fori(0, C // 2) as i:
                    for s in range(2):
                        act.wait_ge(freed, i * 2 + (s + 1))
                        for g in range(GROUPS):
                            act.wait_ge(made, i * (2 * GROUPS) + ((s + 3) * GROUPS + g + 1))
                            nc.scalar.activation(uo[:, s, g // 2, g % 2 * 2:g % 2 * 2 + 2, :],
                                                 pc[s * GROUPS + g][:],
                                                 ACT.Silu, bias=cbc[:, s:s + 1]).then_inc(acted, 1)
                for g in range(NS):
                    act.wait_ge(seam_made, g + 1)
                    nc.scalar.activation(seam_u[:, g, :], pc[g % (2 * GROUPS)][0:MS, 0, :], ACT.Silu,
                                         bias=seam_cb[:, g:g + 1]).then_inc(seam_acted, 1)

            @block.gpsimd
            def _(pool):
                pool.sem_inc(freed, 2)
                with pool.Fori(0, C // 2) as i:
                    for s in range(2):
                        pool.wait_ge(acted, i * (2 * GROUPS) + (s + 3) * GROUPS)
                        for t in range(T):
                            row = t * 128 + t
                            pool.dma_start(u[i * 2 + s, :, row:row + 127, :].rearrange("b p w -> p b w"),
                                           uo[t:t + 127, s, t, :, :]).then_inc(u_out[s], 16)
                        pool.wait_ge(u_out[s], i * (16 * T) + 16 * T)
                        pool.sem_inc(freed, 1)
                for s in range(2):
                    pool.wait_ge(u_out[s], C // 2 * 16 * T)


def scan_pass(core, w, way):
    nc, d = core.nc, core.d
    u, yf, y = tokens(d["u"]), tokens(d["yf"]), tokens(d["y"])
    PER = NTILE // B
    N = 2 * PER
    SLOTS = 4
    BODY = 2 * SLOTS
    DEEP = 4
    n_ = f"s{way}_"
    with core.stage() as k:
        ui = k.sb(n_ + "ui", [C + 1, SLOTS, TILE])
        fi = k.sb(n_ + "fi", [C, SLOTS, TILE]) if way else None
        yo = k.sb(n_ + "yo", [C, 2, TILE])
        ex = k.sb(n_ + "ex", [C, 2, HALF])
        dl = k.sb(n_ + "dl", [C, 2, HALF])
        da = k.sb(n_ + "da", [C, DEEP, HALF])
        db = k.sb(n_ + "db", [C, DEEP, HALF])
        hs = k.sb(n_ + "hs", [C, 2, HALF])
        us = k.sb(n_ + "us", [C, DEEP, HALF]) if way else None
        p_d = [k.ps(f"{n_}p_d{i}", [C, HALF]) for i in range(2)]
        p_b = k.ps(n_ + "p_b", [C, HALF])
        p_c = k.ps(n_ + "p_c", [C, HALF])
        u_in, f_in = ([k.sem(f"{n_}{n}{s}") for s in range(SLOTS)] for n in ("u_in", "f_in"))
        y_out = [k.sem(f"{n_}y_out{s}") for s in range(2)]
        (ones, raw, b_made, c_made, sized, exped, logged, delta, decays, gained, bu, scanned, y_ready, skip, skipped,
         cleared, seen) = (
            k.sem(n_ + n) for n in ("ones", "raw", "b_made", "c_made", "sized", "exped", "logged", "delta", "decays", "gained",
                                    "bu", "scanned", "y_ready", "skip", "skipped", "cleared", "seen"))

        def units(step, start=lambda b: None):
            return image_units(N, BODY, step, start, ahead=3)

        def landed(b, i, k):
            return b * (PER // SLOTS * 16) + (i + k // BODY) * 16 + 16

        def half(k, n=HALF):
            h = k % 2 if way == 0 else 1 - k % 2
            return slice(h * n, (h + 1) * n)

        def slot(k):
            return k % BODY // 2

        def place(t):
            return t if way == 0 else NTILE - 1 - t

        with nc.Block() as block:
            @block.sync
            def _(sp):
                def load(t, s):
                    sp.dma_start(ui[0:C, s, :], u[:, place(t), :]).then_inc(u_in[s], 16)
                    if way:
                        sp.dma_start(fi[:, s, :], yf[:, place(t), :]).then_inc(f_in[s], 16)

                def store(t, s):
                    sp.wait_ge(y_ready, t * 2 + 3)
                    core.apart(sp)
                    sp.dma_start((yf if way == 0 else y)[:, place(t), :], yo[:, s % 2, :]).then_inc(y_out[s % 2], 16)

                for s in range(2):
                    sp.sem_inc(y_out[s], 16)
                for s in range(SLOTS):
                    load(s, s)
                with sp.Fori(0, NTILE // SLOTS - 1) as i:
                    for s in range(SLOTS):
                        t = i * SLOTS + s
                        store(t, s)
                        load(t + SLOTS, s)
                for s in range(SLOTS):
                    store(NTILE - SLOTS + s, s)
                for s in range(2):
                    sp.wait_ge(y_out[s], NTILE // 2 * 16 + 16)

            @block.tensor
            def _(pe):
                def product(p, lhs, k, rows):
                    for q in range(2):
                        lo = half(k).start + q * 512
                        mm = nc.tensor.matmul(p[:, q * 512:(q + 1) * 512], lhs, ui[0:rows, slot(k), lo:lo + 512],
                                              start=True, stop=True)
                    return mm

                def step(m, k, b, i, live):
                    if live(3):
                        kk = k + 3
                        if kk % 2 == 0:
                            pe.wait_ge(u_in[slot(kk)], landed(b, i, kk))
                        pe.wait_ge(delta, m + 4)
                        product(p_d[kk % 2], w["wd"][:, way, :], kk, C + 1).then_inc(raw, 1)
                    if live(0):
                        pe.wait_ge(bu, m + 1)
                        product(p_b, w["bc"][:, way, 0, :], k, C).then_inc(b_made, 1)
                        if way:
                            pe.wait_ge(seen, m + 1)
                        else:
                            pe.wait_ge(y_ready, m + 1)
                        product(p_c, w["bc"][:, way, 1, :], k, C).then_inc(c_made, 1)

                pe.wait_ge(ones, 1)
                units(step)(pe)

            @block.scalar
            def _(act):
                nc.scalar.preload_act_table_set("natural_log_exp_and_others")

                def step(m, k, b, i, live):
                    kk = k + 2
                    e = ex[:, (k + 3) % 2, :]
                    if live(3):
                        act.wait_ge(raw, m + 4)
                        nc.scalar.activation(e, p_d[(k + 3) % 2][:], ACT.Abs).then_inc(sized, 1)
                    if live(2):
                        act.wait_ge(delta, m + 5)
                        nc.scalar.activation(da[:, kk % DEEP, :], dl[:, kk % 2, :], ACT.Exp,
                                             scale=w["nega"][:, way:way + 1]).then_inc(decays, 1)
                    if live(3):
                        act.wait_ge(sized, m + 4)
                        nc.scalar.activation(e, e, ACT.Exp, scale=-1.0).then_inc(exped, 1)
                    if live(2) and way:
                        nc.scalar.activation(us[:, kk % DEEP, :], ui[0:C, slot(kk), half(kk)], ACT.Identity,
                                             scale=w["dsum"][:, 0:1]).then_inc(skip, 1)
                    if live(3):
                        act.wait_ge(exped, m + 4)
                        nc.scalar.activation(e, e, ACT.Ln, bias=1.0).then_inc(logged, 1)

                units(step)(act)

            @block.gpsimd
            def _(pool):
                def step(m, k, b, i, live):
                    if live(2):
                        kk = k + 2
                        pool.wait_ge(delta, m + 5)
                        nc.gpsimd.tensor_tensor(db[:, kk % DEEP, :], dl[:, kk % 2, :], ui[0:C, slot(kk), half(kk)],
                                                ALU.mult).then_inc(gained, 1)
                        if way:
                            pool.wait_ge(skip, m + 3)
                            if kk % 2 == 0:
                                pool.wait_ge(f_in[slot(kk)], landed(b, i, kk))
                            us_ = us[:, kk % DEEP, :]
                            nc.gpsimd.tensor_tensor(us_, us_, fi[:, slot(kk), half(kk)], ALU.add
                                                    ).then_inc(skipped, 1)

                units(step)(pool)

            @block.vector
            def _(dve):
                dve.sem_inc(delta, 2)
                dve.sem_inc(y_ready, 1)
                dve.sem_inc(bu, 1)
                dve.sem_inc(seen, 1)
                nc.vector.memset(ui[C:C + 1, :, :], 1.0).then_inc(ones, 1)

                def start(b):
                    last = HALF - 1 if way == 0 else 0
                    dve.wait_ge(y_ready, b * N + 1)
                    nc.vector.memset(hs[:, 1, last:last + 1], 0.0).then_inc(cleared, 1)
                    dve.wait_ge(cleared, b + 1)

                def step(m, k, b, i, live):
                    if live(0):
                        d = db[:, k % DEEP, :]
                        dve.wait_ge(gained, m + 1)
                        dve.wait_ge(b_made, m + 1)
                        nc.vector.tensor_tensor(d, d, p_b[:], ALU.mult).then_inc(bu, 1)
                        dve.wait_ge(decays, m + 1)
                    if live(2):
                        kk = k % 2
                        dve.wait_ge(logged, m + 3)
                        nc.vector.scalar_tensor_tensor(dl[:, kk, :], p_d[kk][:], 0.0, ex[:, kk, :],
                                                       ALU.max, ALU.add).then_inc(delta, 1)
                    if live(0):
                        dve.wait_ge(bu, m + 2)
                        r = slice(None) if way == 0 else slice(None, None, -1)
                        before = hs[:, (k + 1) % 2, HALF - 1:HALF] if way == 0 else hs[:, (k + 1) % 2, 0:1]
                        nc.vector.tensor_tensor_scan(hs[:, k % 2, r], da[:, k % DEEP, r], db[:, k % DEEP, r], before,
                                                     ALU.mult, ALU.add).then_inc(scanned, 1)
                        dve.wait_ge(scanned, m + 1)
                        dve.wait_ge(c_made, m + 1)
                        if k % 2 == 0:
                            dve.wait_ge(y_out[k // 2 % 2], b * (PER // 2 * 16) + i * (SLOTS // 2 * 16)
                                        + (k // 4 * 16 + 16))
                        to = yo[:, k // 2 % 2, half(k)]
                        nc.vector.tensor_tensor(to, hs[:, k % 2, :], p_c[:], ALU.mult).then_inc(
                            seen if way else y_ready, 1)
                        if way:
                            dve.wait_ge(seen, m + 2)
                            dve.wait_ge(skipped, m + 1)
                            nc.vector.tensor_tensor(to, to, us[:, k % DEEP, :], ALU.add).then_inc(y_ready, 1)

                units(step, start)(dve)


def norm_gate_out(core, w):
    nc, d = core.nc, core.d
    x1, y, zs = tokens(d["x1"]), tokens(d["y"]), tokens(d["zs"])
    out = d["out"].rearrange("b c h w -> c b (h w)").rearrange("c b (t n) -> c b t n", n=TILE)
    PER = NTILE // B
    SLOTS = 4
    BODY = 2 * SLOTS
    N = 2 * PER
    with core.stage() as k:
        yi, xi, zi = (k.sb("o_" + n, [C, SLOTS, TILE]) for n in ("yi", "xi", "zi"))
        sq, rs, tn, gt = (k.sb("o_" + n, [C, 2, HALF]) for n in ("sq", "rs", "tn", "gt"))
        eps = k.sb("o_eps", [C, 1])
        p_y = [k.ps(f"o_p_y{i}", [C, HALF]) for i in range(2)]
        p_v = k.ps("o_p_v", [C, HALF])
        p_o = k.ps("o_p_o", [C, HALF])
        y_in, x_in, z_in, out_done = ([k.sem(f"o_{n}{s}") for s in range(SLOTS)]
                                      for n in ("y_in", "x_in", "z_in", "out_done"))
        (eps_set, centred, squared, vared, logged, rooted, normed, affine, gated, projected, finished) = (
            k.sem("o_" + n) for n in ("eps_set", "centred", "squared", "vared", "logged", "rooted", "normed",
                                      "affine", "gated", "projected", "finished"))

        def landed(b, i, k):
            return b * (PER // SLOTS * 16) + (i + k // BODY) * 16 + 16

        def slot(k):
            return k % BODY // 2

        def half(k):
            return slice(k % 2 * HALF, (k % 2 + 1) * HALF)

        with nc.Block() as block:
            @block.sync
            def _(sp):
                with sp.Fori(0, B) as b:
                    with sp.Fori(0, PER // SLOTS) as i:
                        for s in range(SLOTS):
                            t = b * PER + i * SLOTS + s
                            sp.wait_ge(out_done[s], b * (PER // SLOTS * 16) + i * 16)
                            sp.dma_start(yi[:, s, :], y[:, t, :]).then_inc(y_in[s], 16)
                            sp.dma_start(zi[:, s, :], zs[:, t, :]).then_inc(z_in[s], 16)
                            sp.dma_start(xi[:, s, :], x1[:, t, :]).then_inc(x_in[s], 16)

            @block.tensor
            def _(pe):
                pe.sem_inc(projected, 1)

                def product(p, lhs, rhs, done):
                    for q in range(2):
                        mm = nc.tensor.matmul(p[:, q * 512:(q + 1) * 512], lhs, rhs[:, q * 512:(q + 1) * 512],
                                              start=True, stop=True)
                    mm.then_inc(done, 1)

                def step(m, k, b, i, live):
                    if live(2):
                        kk = k + 2
                        if kk % 2 == 0:
                            pe.wait_ge(y_in[slot(kk)], landed(b, i, kk))
                        pe.wait_ge(normed, m + 3)
                        product(p_y[kk % 2], w["centre"][:], yi[:, slot(kk), half(kk)], centred)
                    if live(0):
                        pe.wait_ge(gated, m + 2)
                        pe.wait_ge(finished, m)
                        product(p_o, w["wo"][:], gt[:, k % 2, :], projected)
                    if live(2):
                        pe.wait_ge(squared, m + 3)
                        pe.wait_ge(logged, m + 2)
                        product(p_v, w["mean"][:], sq[:, k % 2, :], vared)

                image_units(N, BODY, step)(pe)

            @block.scalar
            def _(act):
                nc.scalar.preload_act_table_set("natural_log_exp_and_others")
                act.wait_ge(eps_set, 1)

                def step(m, k, b, i, live):
                    r = rs[:, (k + 1) % 2, :]
                    if live(1):
                        act.wait_ge(vared, m + 2)
                        nc.scalar.activation(r, p_v[:], ACT.Ln, bias=eps[:, 0:1]).then_inc(logged, 1)
                    if live(2):
                        act.wait_ge(centred, m + 3)
                        nc.scalar.activation(sq[:, k % 2, :], p_y[k % 2][:], ACT.Square).then_inc(squared, 1)
                    if live(1):
                        act.wait_ge(logged, m + 2)
                        nc.scalar.activation(r, r, ACT.Exp, scale=-0.5).then_inc(rooted, 1)

                image_units(N, BODY, step)(act)

            @block.vector
            def _(dve):
                dve.sem_inc(normed, 2)
                nc.vector.memset(eps[:], GEPS).then_inc(eps_set, 1)

                def step(m, k, b, i, live):
                    if live(0):
                        if k % 2 == 0:
                            dve.wait_ge(x_in[slot(k)], landed(b, i, k))
                        dve.wait_ge(projected, m + 2)
                        x = xi[:, slot(k), half(k)]
                        nc.vector.scalar_tensor_tensor(x, p_o[:], w["scale"][:, 0:1], x, ALU.mult, ALU.add
                                                       ).then_inc(finished, 1)
                    if live(1):
                        kk = (k + 1) % 2
                        dve.wait_ge(rooted, m + 2)
                        dve.wait_ge(gated, m + 1)
                        nc.vector.tensor_tensor(tn[:, kk, :], p_y[kk][:], rs[:, kk, :], ALU.mult).then_inc(normed, 1)
                        dve.wait_ge(normed, m + 4)
                        nc.vector.tensor_scalar(tn[:, kk, :], tn[:, kk, :], w["onwb"][:, 0:1], w["onwb"][:, 1:2],
                                                ALU.mult, ALU.add).then_inc(affine, 1)

                image_units(N, BODY, step)(dve)

            @block.gpsimd
            def _(pool):
                pool.sem_inc(gated, 1)

                def step(m, k, b, i, live):
                    if live(1):
                        kk = k + 1
                        if kk % 2 == 0:
                            pool.wait_ge(z_in[slot(kk)], landed(b, i, kk))
                        pool.wait_ge(affine, m + 2)
                        pool.wait_ge(projected, m + 1)
                        nc.gpsimd.tensor_tensor(gt[:, kk % 2, :], tn[:, kk % 2, :], zi[:, slot(kk), half(kk)],
                                                ALU.mult).then_inc(gated, 1)
                    if live(0) and k % 2 == 1:
                        pool.wait_ge(finished, m + 1)
                        core.apart(pool)
                        pool.dma_start(out[:, b, i * SLOTS + slot(k), :], xi[:, slot(k), :]
                                       ).then_inc(out_done[slot(k)], 16)

                image_units(N, BODY, step)(pool)
                for s in range(SLOTS):
                    pool.wait_ge(out_done[s], NTILE // SLOTS * 16)


def program(nc, dram, upto=99):
    with ExitStack() as ctx:
        core = Core(nc, ctx, dram)
        w = {n: core.sb("w_" + n, s) for n, s in dict(
            ident=[128, 128], group=[C, C], centre=[C, C], mean=[C, C], g=[C, C + 1], gb=[C + 1, 1],
            wvp=[C, C], wp1=[C + 1, C], lepe=[128, C * 9], wd=[C + 1, 2, C], bc=[C, 2, 2, C],
            nega=[C, 2], dsum=[C, 1], inw=[C, 2 * C], wo=[C, C], onwb=[C, 2], scale=[C, 1]).items()}
        gscale, gbias = core.sb("gscale", [C, B]), core.sb("gbias", [C, B])
        nbr_w = core.sb("nbr_w", [128, NW // 128, TOPK])
        nbr_i = core.sb("nbr_i", [128, NW // 128, TOPK], U32)
        setup_weights(core, w)
        with ExitStack() as early:
            wconv = early.enter_context(nc.sbuf_tensor("wconv", [128, C * 128], F32))
            build_window_convs(core, w, wconv)
            with ExitStack() as pool:
                stats = pool.enter_context(nc.sbuf_tensor("stats", [C, NT * 24], F32))
                pooled = pool.enter_context(nc.sbuf_tensor("pooled", [C, NW], F32))
                image_stats(core, stats, pooled)
                group_coefficients(core, w, "g0", stats, gscale, gbias)
                top_windows(core, pooled, gscale, gbias, nbr_w, nbr_i)
            if upto < 2:
                return
            window_convs(core, w, wconv, gscale, gbias)
        gather_context(core, nbr_w, nbr_i)
        if upto < 3:
            return
        with ExitStack() as pool:
            stats = pool.enter_context(nc.sbuf_tensor("stats1", [C, NT * 24], F32))
            attend(core, w, stats)
            group_coefficients(core, w, "g1", stats, gscale, gbias)
        if upto < 4:
            return
        project_in(core, w, gscale, gbias)
        if upto < 5:
            return
        image_convs(core, w)
        if upto < 6:
            return
        scan_pass(core, w, 0)
        if upto < 7:
            return
        scan_pass(core, w, 1)
        if upto < 8:
            return
        norm_gate_out(core, w)


def declare(nc, d):
    for name, shape in dict(xg=(NW, C * P), ctx=(NW, C * P), part=(C, NT, RT), x1=(C, NT, RT), xc=(C, B * H, W),
                            u=(C, B * H, W), yf=(C, B * L), y=(C, B * L), zs=(C, B * L)).items():
        d[name] = nc.dram_tensor("mid_" + name, shape, F32, kind="Internal").ap()


def arrays(i):
    f = lambda a: np.ascontiguousarray(a)
    col = lambda a: f(np.asarray(a).reshape(-1, 1))
    a = {k: np.asarray(v) for k, v in i.items()}
    xp = a["L1_conv_x_proj_w"]
    out = dict(
        x=f(a["x"]), wq_t=f(a["L0_conv_Wq"].T),
        wk_t_bk=f(np.concatenate([a["L0_conv_Wk"].T, a["L0_conv_bk"][:, None]], axis=1)),
        bq=col(a["L0_conv_bq"]), wv_t=f(a["L0_conv_Wv"].T),
        bv_lb=f(np.stack([a["L0_conv_bv"], a["L0_conv_lepe_b"]], axis=1)),
        wp=f(a["L0_conv_Wp"]), bp=f(a["L0_conv_bp"].reshape(1, C)), lepe_w=f(a["L0_conv_lepe_w"].reshape(C * 9)),
        xp_dt=f(xp[:, 0:R].transpose(1, 0, 2)), dtw_t=f(a["L1_conv_dt_proj_w"].transpose(2, 0, 1)),
        xp_t=f(xp.transpose(2, 0, 1).reshape(C, 2 * NX)), alog_t=f(a["L1_conv_A_logs"].reshape(2, C).T),
        ds_t=f(a["L1_conv_Ds"].reshape(2, C).T), dtb=f(a["L1_conv_dt_proj_b"].reshape(1, 2, C)),
        in_w_t=f(a["L1_conv_in_proj_w"].T), wo_t=f(a["L1_conv_out_proj_w"].T),
        onwb=f(np.stack([a["L1_conv_out_norm_w"], a["L1_conv_out_norm_b"]], axis=1)),
        scale_w=col(a["L1_conv_scale_w"]), conv_w=f(a["L1_conv_conv_w"].reshape(C * 9)), conv_b=f(a["L1_conv_conv_b"]))
    cw, cbias = a["L1_conv_conv_w"].reshape(C // SEAM, SEAM, 9), a["L1_conv_conv_b"].reshape(C // SEAM, SEAM)
    out.update(seam_taps=f(np.repeat(cw.transpose(1, 0, 2), B * 4, axis=0)),
               seam_cb=f(np.repeat(cbias.T, B * 2, axis=0)))
    out.update(unit_constants())
    return {"in_" + n: v for n, v in out.items()}


def kernel(**inputs):
    import concourse.bacc as bacc
    from concourse.bass_utils import run_bass_kernel_spmd

    nc = bacc.Bacc("TRN2", target_bir_lowering=False, num_devices=1)
    sent = arrays(inputs)
    dram = {n[3:]: nc.dram_tensor(n, a.shape, mybir.dt.from_np(a.dtype), kind="ExternalInput").ap()
            for n, a in sent.items()}
    dram["out"] = nc.dram_tensor("out", (B, C, H, W), F32, kind="ExternalOutput").ap()
    declare(nc, dram)
    program(nc, dram)
    return run_bass_kernel_spmd(nc, [sent], core_ids=[0]).results[0]["out"]
```

```python
from contextlib import ExitStack, contextmanager

import numpy as np

import concourse.bass as bass
from concourse import mybir

F32 = mybir.dt.float32
U32 = mybir.dt.uint32
ALU = mybir.AluOpType
ACT = mybir.ActivationFunctionType
AX = mybir.AxisListType

B, C, H, W = 4, 96, 256, 256
GS = 8
P = GS * GS
GH, GW = H // GS, W // GS
NW = B * GH * GW
NT = B * GH
RT = GS * W
PAIRS = GW // 2
TOPK = 3
L = H * W
R = 6
NX = R + 2
SCALE = float(C) ** -0.5
GEPS = 1e-5


def unit_constants():
    ident = np.eye(128, dtype=np.float32)
    pos = np.arange(P)
    shifts = np.zeros((128, 9, 128), np.float32)
    for t in range(9):
        dy, dx = t // 3 - 1, t % 3 - 1
        r, c = pos // GS + dy, pos % GS + dx
        ok = (r >= 0) & (r < GS) & (c >= 0) & (c < GS)
        for w in range(2):
            shifts[w * P + (r * GS + c)[ok], t, w * P + pos[ok]] = 1.0
    rows = np.stack([np.eye(128, k=1 - dy) for dy in range(3)], axis=1).astype(np.float32)
    seams = np.stack([np.kron(np.eye(SEAM * B), np.eye(4, k=1 - dy)[:, 1:3]) for dy in range(3)],
                     axis=1).astype(np.float32)
    group = np.kron(np.eye(C // 3), np.ones((3, 3))).astype(np.float32) / np.float32(3)
    centre = (np.eye(C) - 1.0 / C).astype(np.float32)
    mean = np.full((C, C), 1.0 / C, np.float32)
    return dict(ident=ident, shifts=shifts, rows=rows, group=group, centre=centre, mean=mean,
                seams=seams)


SEAM = 6


class Core:

    def __init__(self, nc, ctx, dram, passed=None):
        self.nc, self.ctx, self.d = nc, ctx, dram
        self.sems = []
        self.passed = passed if passed is not None else ctx.enter_context(nc.semaphore("passed"))

    def sb(self, name, shape, dt=F32):
        return self.ctx.enter_context(self.nc.sbuf_tensor(name, shape, dt))

    def ps(self, name, shape, dt=F32):
        return self.ctx.enter_context(self.nc.psum_tensor(name, shape, dt))

    def sem(self, name):
        self.sems.append(self.nc.alloc_semaphore(name))
        return self.sems[-1]

    def apart(self, eng):
        eng.sem_inc(self.passed, 1)

    @contextmanager
    def stage(self):
        with ExitStack() as ctx:
            stage = Core(self.nc, ctx, self.d, self.passed)
            yield stage
            self.nc.clear_and_free_semaphores(stage.sems)
            self.nc.all_engine_barrier()


def setup_weights(core, w):
    nc, d = core.nc, core.d
    with core.stage() as k:
        wq_t = k.sb("wq_t", [C, C])
        wk_t = k.sb("wk_t", [C, C + 1])
        wv_t = k.sb("wv_t", [C, C])
        bq = k.sb("bq", [C, 1])
        bvl = k.sb("bvl", [C, 2])
        bp = k.sb("bp", [1, C])
        crow = k.sb("crow", [1, C])
        bsum = k.sb("bsum", [C, 1])
        xp = k.sb("xp", [R, 2, C])
        dtw = k.sb("dtw", [R, 2, C])
        xpt = k.sb("xpt", [C, 2 * NX])
        alog = k.sb("alog", [C, 2])
        aexp = k.sb("aexp", [C, 2])
        ds = k.sb("ds", [C, 2])
        p1 = k.ps("setup_p1", [C, 512])
        p2 = k.ps("setup_p2", [C, 512])
        p3 = k.ps("setup_p3", [C + 1, 512])
        loaded, summed, folded, stored, powed, crow_ready, row_in = (
            k.sem(f"setup_{n}") for n in ("loaded", "summed", "folded", "stored", "powed", "crow", "rowin"))
        loads = [
            (wq_t[:], d["wq_t"]), (wk_t[:], d["wk_t_bk"]), (wv_t[:], d["wv_t"]), (bq[:], d["bq"]),
            (bvl[:], d["bv_lb"]), (bp[:], d["bp"]), (w["wp1"][0:C, :], d["wp"]), (w["ident"][:], d["ident"]),
            (w["group"][:], d["group"]), (w["centre"][:], d["centre"]), (w["mean"][:], d["mean"]),
            (xp[:], d["xp_dt"]), (dtw[:], d["dtw_t"]), (xpt[:], d["xp_t"]), (alog[:], d["alog_t"]), (ds[:], d["ds_t"]),
            (w["wd"][C:C + 1, :, :], d["dtb"]), (w["inw"][:], d["in_w_t"]), (w["wo"][:], d["wo_t"]),
            (w["onwb"][:], d["onwb"]), (w["scale"][:], d["scale_w"]),
            (w["lepe"][:], d["lepe_w"].partition_broadcast(128)),
        ]
        with nc.Block() as block:
            @block.sync
            def _(sp):
                for to, src in loads:
                    sp.dma_start(to, src).then_inc(loaded, 16)
                sp.wait_ge(crow_ready, 1)
                sp.dma_start(w["wp1"][C:C + 1, :], crow[:]).then_inc(row_in, 16)
                sp.wait_ge(row_in, 16)

            @block.vector
            def _(dve):
                dve.wait_ge(loaded, 16 * len(loads))
                nc.vector.tensor_tensor(bsum[:], bvl[:, 0:1], bvl[:, 1:2], ALU.add).then_inc(summed, 1)
                nc.vector.tensor_tensor(w["dsum"][:], ds[:, 0:1], ds[:, 1:2], ALU.add)
                for s in range(2):
                    for r in range(2):
                        nc.vector.tensor_copy(w["bc"][:, s, r, :],
                                              xpt[:, s * NX + R + r:s * NX + R + r + 1].to_broadcast([C, C]))
                dve.wait_ge(folded, 1)
                nc.vector.tensor_copy(w["g"][:], p1[:, 0:C + 1])
                nc.vector.tensor_copy(w["wvp"][:], p1[:, 128:128 + C])
                nc.vector.tensor_copy(w["wd"][0:C, 0, :], p1[:, 256:256 + C])
                nc.vector.tensor_copy(w["wd"][0:C, 1, :], p1[:, 384:384 + C])
                nc.vector.tensor_copy(w["gb"][:], p3[:, 0:1])
                nc.vector.tensor_tensor(crow[:], p2[0:1, 0:C], bp[:], ALU.add).then_inc(crow_ready, 1)
                dve.wait_ge(powed, 1)
                nc.vector.tensor_scalar(w["nega"][:], aexp[:], -1.0, None, ALU.mult).then_inc(stored, 1)

            @block.scalar
            def _(act):
                act.wait_ge(loaded, 16 * len(loads))
                nc.scalar.activation(aexp[:], alog[:], ACT.Exp).then_inc(powed, 1)

            @block.tensor
            def _(pe):
                pe.wait_ge(loaded, 16 * len(loads))
                mm = lambda o, a, b: nc.tensor.matmul(o, a, b, start=True, stop=True)
                mm(p1[:, 0:C + 1], wq_t[:], wk_t[:])
                mm(p1[:, 128:128 + C], wv_t[:], w["wp1"][0:C, :])
                mm(p1[:, 256:256 + C], xp[:, 0, :], dtw[:, 0, :])
                mm(p1[:, 384:384 + C], xp[:, 1, :], dtw[:, 1, :])
                mm(p3[:, 0:1], wk_t[:], bq[:])
                pe.wait_ge(summed, 1)
                mm(p2[0:1, 0:C], bsum[:], w["wp1"][0:C, :]).then_inc(folded, 1)


def image_stats(core, w, stats, pooled, wconv):
    nc, d = core.nc, core.d
    x = d["x"].rearrange("b c (g r) w -> c b g (r w)", r=GS)
    CG = 4
    SLOTS = 4
    with core.stage() as k:
        xin = k.sb("a_x", [C, SLOTS, RT])
        x_in = [k.sem(f"a_x_in{s}") for s in range(SLOTS)]
        x_free = k.sem("a_x_free")
        shifts = k.sb("a_shifts", [128, 9, 128])
        taps = k.sb("a_taps", [128, 2, CG, 128])
        pw = [k.ps(f"a_pw{i}", [128, CG * 128]) for i in range(2)]
        shifts_in, scaled, multiplied, copied = (k.sem("a_" + n) for n in ("shifts_in", "scaled", "multiplied",
                                                                        "copied"))
        with nc.Block() as block:
            @block.scalar
            def _(act):
                act.sem_inc(copied, 2)
                with act.Fori(0, C // (2 * CG)) as i:
                    for g in range(2):
                        for t in range(9):
                            n = g * 9 + t
                            act.wait_ge(multiplied, i * 18 + (n + 1))
                            for c in range(CG):
                                ins = nc.scalar.activation(
                                    taps[:, n % 2, c, :], w["ident"][:], ACT.Copy,
                                    scale=w["lepe"][:, bass.ds(i * (2 * CG * 9) + ((g * CG + c) * 9 + t), 1)])
                            ins.then_inc(scaled, 1)
                        act.wait_ge(multiplied, i * 18 + (g * 9 + 11))
                        nc.scalar.copy(wconv[:, bass.ds(i * (2 * CG * 128) + g * CG * 128, CG * 128)], pw[g][:]
                                       ).then_inc(copied, 1)

            @block.tensor
            def _(pe):
                pe.sem_inc(multiplied, 2)
                pe.wait_ge(shifts_in, 16)
                with pe.Fori(0, C // (2 * CG)) as i:
                    for g in range(2):
                        pe.wait_ge(copied, i * 2 + (g + 1))
                        for t in range(9):
                            n = g * 9 + t
                            pe.wait_ge(scaled, i * 18 + (n + 1))
                            nc.tensor.matmul(pw[g][:], shifts[:, 8 - t, :],
                                             taps[:, n % 2, :, :].rearrange("p c m -> p (c m)"),
                                             start=(t == 0), stop=(t == 8)).then_inc(multiplied, 1)

            @block.sync
            def _(sp):
                sp.dma_start(shifts[:], d["shifts"]).then_inc(shifts_in, 16)
                with sp.Fori(0, B) as b:
                    with sp.Fori(0, GH // SLOTS) as g:
                        for s in range(SLOTS):
                            sp.wait_ge(x_free, b * GH + g * SLOTS + (s + 1))
                            sp.dma_start(xin[:, s, :], x[:, b, g * SLOTS + s, :]).then_inc(x_in[s], 16)

            @block.vector
            def _(dve):
                dve.sem_inc(x_free, SLOTS)
                with dve.Fori(0, NT // SLOTS) as g:
                    for s in range(SLOTS):
                        dve.wait_ge(x_in[s], g * 16 + 16)
                        for q in range(RT // 512):
                            nc.vector.bn_stats(
                                stats[:, bass.ds(g * (SLOTS * 24) + (s * 24 + q * 6), 6)],
                                xin[:, s, q * 512:(q + 1) * 512])
                        nc.vector.tensor_reduce(
                            pooled[:, bass.ds(g * (SLOTS * GW) + s * GW, GW)],
                            xin[:, s, :].rearrange("c (r w k) -> c w r k", r=GS, k=GS),
                            AX.XY, ALU.max).then_inc(x_free, 1)


def group_coefficients(core, w, name, stats, gscale, gbias):
    nc = core.nc
    with core.stage() as k:
        mv = k.sb(name + "mv", [C, B, 2])
        s2 = k.sb(name + "s2", [C, 2, B])
        gs = k.sb(name + "gs", [C, 2, B])
        var = k.sb(name + "var", [C, B])
        std = k.sb(name + "std", [C, B])
        pg = k.ps(name + "pg", [C, 512])
        step, grouped, rooted = k.sem(name + "step"), k.sem(name + "grouped"), k.sem(name + "rooted")
        per = NT // B * 24
        with nc.Block() as block:
            @block.vector
            def _(dve):
                for b in range(B):
                    last = nc.vector.bn_aggr(mv[:, b, :], stats[:, b * per:(b + 1) * per])
                last.then_inc(step, 1)
                dve.wait_ge(step, 1)
                nc.vector.tensor_tensor(var[:], mv[:, :, 0], mv[:, :, 0], ALU.mult)
                nc.vector.tensor_copy(s2[:, 0, :], mv[:, :, 0]).then_inc(step, 1)
                dve.wait_ge(step, 2)
                nc.vector.tensor_tensor(s2[:, 1, :], var[:], mv[:, :, 1], ALU.add).then_inc(step, 1)
                dve.wait_ge(grouped, 1)
                nc.vector.tensor_copy(gs[:], pg[:, 0:2 * B].rearrange("c (a b) -> c a b", a=2)).then_inc(step, 1)
                dve.wait_ge(step, 4)
                nc.vector.tensor_tensor(var[:], gs[:, 0, :], gs[:, 0, :], ALU.mult).then_inc(step, 1)
                dve.wait_ge(step, 5)
                nc.vector.tensor_tensor(std[:], gs[:, 1, :], var[:], ALU.subtract).then_inc(step, 1)
                dve.wait_ge(step, 6)
                nc.vector.tensor_scalar(var[:], std[:], GEPS, None, ALU.add).then_inc(step, 1)
                dve.wait_ge(rooted, 1)
                nc.vector.reciprocal(gscale[:], std[:]).then_inc(step, 1)
                dve.wait_ge(step, 8)
                nc.vector.tensor_tensor(std[:], gscale[:], gscale[:], ALU.mult).then_inc(step, 1)
                dve.wait_ge(step, 9)
                nc.vector.scalar_tensor_tensor(mv[:, :, 0], std[:], -0.5, var[:], ALU.mult, ALU.mult).then_inc(step, 1)
                dve.wait_ge(step, 10)
                nc.vector.scalar_tensor_tensor(gscale[:], mv[:, :, 0], 1.5, gscale[:], ALU.add, ALU.mult
                                               ).then_inc(step, 1)
                dve.wait_ge(step, 11)
                nc.vector.scalar_tensor_tensor(gbias[:], gs[:, 0, :], -1.0, gscale[:], ALU.mult, ALU.mult)

            @block.tensor
            def _(pe):
                pe.wait_ge(step, 3)
                nc.tensor.matmul(pg[:, 0:2 * B], w["group"][:], s2[:].rearrange("c a b -> c (a b)"),
                                 start=True, stop=True).then_inc(grouped, 1)

            @block.scalar
            def _(act):
                act.wait_ge(step, 7)
                nc.scalar.activation(std[:], var[:], ACT.Sqrt).then_inc(rooted, 1)


def top_windows(core, pooled, gscale, gbias, nbr_w, nbr_i):
    nc = core.nc
    T = NW // 128
    HALF = 1024
    with core.stage() as k:
        score = k.sb("score", [128, 2, NW])
        own = k.sb("own", [C, 2, 128])
        top = k.sb("top", [128, 2, 8])
        place = k.sb("place", [128, 2, 8], U32)
        tops = k.sb("tops", [128, T, 8])
        places = k.sb("places", [128, T, 8], U32)
        diff = k.sb("diff", [128, T, TOPK])
        ex = k.sb("ex", [128, T, TOPK])
        tot = k.sb("tot", [128, T])
        rtot = k.sb("rtot", [128, T])
        ps = [k.ps(f"sim{i}", [128, HALF]) for i in range(4)]
        normed, own_ready, sim, copied, step, kept, exped, fin = (
            k.sem("b_" + n) for n in ("normed", "own_ready", "sim", "copied", "step", "kept", "exped", "fin"))
        Q = NW // HALF
        with nc.Block() as block:
            @block.gpsimd
            def _(pool):
                pool.wait_ge(normed, 1)
                with pool.Fori(0, T // 2) as i:
                    for u in range(2):
                        pool.wait_ge(sim, (i * 2 + u) * Q)
                        nc.gpsimd.tensor_copy(own[:, u, :], pooled[:, bass.ds((i * 2 + u) * 128, 128)]
                                              ).then_inc(own_ready, 1)

            @block.tensor
            def _(pe):
                pe.sem_inc(sim, Q)
                pe.wait_ge(normed, 1)
                with pe.Fori(0, T // 2) as i:
                    for u in range(2):
                        pe.wait_ge(own_ready, i * 2 + (u + 1))
                        for q in range(Q):
                            pe.wait_ge(copied, (i * 2 + u) * Q + q)
                            for h in range(2):
                                mm = nc.tensor.matmul(ps[q][:, h * 512:(h + 1) * 512], own[:, u, :],
                                                      pooled[:, q * HALF + h * 512:q * HALF + (h + 1) * 512],
                                                      start=True, stop=True)
                            mm.then_inc(sim, 1)

            @block.scalar
            def _(act):
                act.sem_inc(copied, Q - 1)
                act.sem_inc(kept, 2)
                with act.Fori(0, T // 2) as i:
                    for u in range(2):
                        act.wait_ge(kept, i * 2 + (u + 1))
                        for q in range(Q):
                            act.wait_ge(sim, (i * 2 + u) * Q + (q + 1 + Q))
                            nc.scalar.copy(score[:, u, q * HALF:(q + 1) * HALF], ps[q][:]).then_inc(copied, 1)
                act.wait_ge(step, 1)
                nc.scalar.activation(ex[:], diff[:], ACT.Exp).then_inc(exped, 1)

            @block.vector
            def _(dve):
                for b in range(B):
                    sl = pooled[:, b * GH * GW:(b + 1) * GH * GW]
                    last = nc.vector.tensor_scalar(sl, sl, gscale[:, b:b + 1], gbias[:, b:b + 1],
                                                   ALU.mult, ALU.add)
                last.then_inc(normed, 1)
                with dve.Fori(0, T // 2) as i:
                    for u in range(2):
                        dve.wait_ge(copied, (i * 2 + u) * Q + (2 * Q - 1))
                        core.apart(dve)
                        nc.vector.max(top[:, u, :], score[:, u, :]).then_inc(fin, 1)
                        dve.wait_ge(fin, (i * 2 + u) * 2 + 1)
                        core.apart(dve)
                        nc.vector.max_index(place[:, u, :], top[:, u, :], score[:, u, :]).then_inc(fin, 1)
                        dve.wait_ge(fin, (i * 2 + u) * 2 + 2)
                        nc.vector.tensor_copy(tops[:, i * 2 + u, :], top[:, u, :])
                        nc.vector.tensor_copy(places[:, i * 2 + u, :], place[:, u, :]).then_inc(kept, 1)
                dve.wait_ge(kept, T + 2)
                nc.vector.tensor_tensor(diff[:], tops[:, :, 0:TOPK], tops[:, :, 0:1].to_broadcast([128, T, TOPK]),
                                        ALU.subtract).then_inc(step, 1)
                nc.vector.tensor_copy(nbr_i[:], places[:, :, 0:TOPK])
                dve.wait_ge(exped, 1)
                nc.vector.tensor_reduce(tot[:], ex[:], AX.X, ALU.add).then_inc(step, 1)
                dve.wait_ge(step, 2)
                nc.vector.reciprocal(rtot[:], tot[:]).then_inc(step, 1)
                dve.wait_ge(step, 3)
                nc.vector.tensor_tensor(nbr_w[:], ex[:], rtot[:].unsqueeze(2).to_broadcast([128, T, TOPK]), ALU.mult)


def window_convs(core, w, wconv, gscale, gbias):
    nc, d = core.nc, core.d
    x = d["x"].rearrange("b c (g r) w -> c b g (r w)", r=GS)
    part = d["part"]
    xg = d["xg"].rearrange("(t n) (c s) -> c t n s", n=GW, c=C)
    Q = 8
    M = GH // Q
    NS = 4
    TG = Q * PAIRS // 4
    GPR = TG // Q
    MG = C // 8
    with core.stage() as k:
        xr = k.sb("l_xr", [C, Q, RT])
        xn = k.sb("l_xn", [C, NS, GW, P])
        xt = k.sb("l_xt", [128, Q * PAIRS, C])
        lc = k.sb("l_lc", [C + 1, 2, 512])
        coef = k.sb("l_coef", [C, 2])
        pt = [k.ps(f"l_pt{i}", [128, 512]) for i in range(2)]
        pm = [k.ps(f"l_pm{i}", [128, 8, Q * PAIRS]) for i in range(2)]
        pw = [k.ps(f"l_pw{i}", [C, 8, GS, GS]) for i in range(2)]
        x_in = [k.sem(f"l_x_in{q}") for q in range(Q)]
        part_out = [k.sem(f"l_part_out{q}") for q in range(Q)]
        xg_out = [k.sem(f"l_xg_out{s}") for s in range(NS)]
        (coef_set, xn_ready, turned, turned_dve, turned_act, conved, conved_dve, conved_act, back, back_out,
         projected, added, ones, freed) = (
            k.sem("l_" + n) for n in ("coef_set", "xn_ready", "turned", "turned_dve", "turned_act", "conved",
                                      "conved_dve", "conved_act", "back", "back_out", "projected", "added",
                                      "ones", "freed"))

        def turn_out(copy, g):
            return copy(xt[:, g * 4:(g + 1) * 4, :], pt[g % 2][:, 0:4 * C].rearrange("p (n c) -> p n c", n=4))

        def conv_out(copy, g):
            return copy(xt[:, :, g * 8:(g + 1) * 8].rearrange("p n c -> p c n"), pm[g % 2][:])

        with nc.Block() as block:
            @block.sync
            def _(sp):
                with sp.Fori(0, B) as b:
                    with sp.Fori(0, M) as m:
                        for q in range(Q):
                            sp.wait_ge(freed, (b * M + m) * Q + (q + 1))
                            sp.dma_start(xr[:, q, :], x[:, b, m * Q + q, :]).then_inc(x_in[q], 16)

            @block.scalar
            def _(act):
                act.sem_inc(back_out, 2)
                act.sem_inc(conved_act, 1)
                for s in range(NS):
                    act.sem_inc(xg_out[s], 16)
                with act.Fori(0, B) as b:
                    nc.scalar.copy(coef[:, 0:1], gscale[:, bass.ds(b, 1)])
                    nc.scalar.copy(coef[:, 1:2], gbias[:, bass.ds(b, 1)]).then_inc(coef_set, 1)
                    act.wait_ge(coef_set, b + 1)
                    with act.Fori(0, M) as m:
                        j = b * M + m
                        for q in range(Q + 1):
                            if q < Q:
                                act.wait_ge(x_in[q], j * 16 + 16)
                                act.wait_ge(xg_out[q % NS], j * (Q // NS * 16) + (q // NS * 16 + 16))
                                if q >= NS:
                                    act.wait_ge(turned, j * TG + (q - NS + 1) * GPR)
                                nc.scalar.activation(
                                    xn[:, q % NS, :, :].rearrange("c n (r k) -> c n r k", r=GS),
                                    xr[:, q, :].rearrange("c (r n k) -> c n r k", r=GS, k=GS), ACT.Identity,
                                    scale=coef[:, 0:1], bias=coef[:, 1:2]).then_inc(xn_ready, 1)
                            if q:
                                act.wait_ge(xn_ready, j * Q + q)
                                nc.scalar.dma_start(xg[:, j * Q + (q - 1), :, :], xn[:, (q - 1) % NS, :, :]
                                                    ).then_inc(xg_out[(q - 1) % NS], 16)
                                for g in range((q - 1) * GPR + 1, q * GPR, 2):
                                    act.wait_ge(turned, j * TG + (g + 1))
                                    turn_out(nc.scalar.copy, g).then_inc(turned_act, 1)
                        for g in range(1, MG, 2):
                            act.wait_ge(conved, j * MG + (g + 1))
                            conv_out(nc.scalar.copy, g).then_inc(conved_act, 1)
                        for g in range(TG):
                            act.wait_ge(back, j * TG + (g + 1))
                            if g == 0:
                                act.wait_ge(ones, 1)
                            nc.scalar.copy(lc[0:C, g % 2, :], pt[g % 2][0:C, :]).then_inc(back_out, 1)
                for s in range(NS):
                    act.wait_ge(xg_out[s], B * M * (Q // NS) * 16 + 16)

            @block.vector
            def _(dve):
                dve.sem_inc(conved_dve, 1)
                dve.sem_inc(added, 2)
                nc.vector.memset(lc[C:C + 1, :, :], 1.0).then_inc(ones, 1)
                with dve.Fori(0, B * M) as j:
                    for g in range(0, TG, 2):
                        dve.wait_ge(turned, j * TG + (g + 1))
                        turn_out(nc.vector.tensor_copy, g).then_inc(turned_dve, 1)
                    for g in range(0, MG, 2):
                        dve.wait_ge(conved, j * MG + (g + 1))
                        conv_out(nc.vector.tensor_copy, g).then_inc(conved_dve, 1)
                    for g in range(TG):
                        q, s = g // GPR, g % GPR
                        dve.wait_ge(projected, j * TG + (g + 1))
                        res = xr[:, q, :].rearrange("c (r n k) -> c n r k", r=GS, k=GS)[:, s * 8:(s + 1) * 8]
                        nc.vector.tensor_tensor(res, pw[g % 2][:], res, ALU.add).then_inc(added, 1)

            @block.gpsimd
            def _(pool):
                pool.sem_inc(freed, Q)
                with pool.Fori(0, B * M) as j:
                    for q in range(Q + 1):
                        if q < Q:
                            pool.wait_ge(added, j * TG + ((q + 1) * GPR + 2))
                            core.apart(pool)
                            pool.dma_start(part[:, j * Q + q, :], xr[:, q, :]).then_inc(part_out[q], 16)
                        if q:
                            pool.wait_ge(part_out[q - 1], j * 16 + 16)
                            pool.sem_inc(freed, 1)

            @block.tensor
            def _(pe):
                def project(j, g):
                    pe.wait_ge(back_out, j * TG + (g + 3))
                    pe.wait_ge(added, j * TG + (g + 1))
                    nc.tensor.matmul(pw[g % 2][:].rearrange("c n r k -> c (n r k)"), w["wp1"][:], lc[:, g % 2, :],
                                     start=True, stop=True).then_inc(projected, 1)

                pe.wait_ge(ones, 1)
                with pe.Fori(0, B * M) as j:
                    for g in range(TG):
                        if g < 2:
                            pe.wait_ge(back_out, j * TG + (g + 1))
                        else:
                            pe.wait_ge(turned_act if g % 2 else turned_dve, j * (TG // 2) + g // 2)
                        if g % GPR == 0:
                            pe.wait_ge(xn_ready, j * Q + (g // GPR + 1))
                        for i in range(4):
                            pair = (g % GPR) * 4 + i
                            mm = nc.tensor.transpose(
                                pt[g % 2][:, i * C:(i + 1) * C],
                                xn[:, g // GPR % NS, 2 * pair:2 * pair + 2, :].rearrange("c n s -> c (n s)"),
                                w["ident"][0:C, 0:C])
                        mm.then_inc(turned, 1)
                    pe.wait_ge(turned_dve, j * (TG // 2) + TG // 2)
                    pe.wait_ge(turned_act, j * (TG // 2) + TG // 2)
                    for g in range(MG):
                        pe.wait_ge(conved_act if g % 2 else conved_dve, j * (MG // 2) + (g // 2 + 1))
                        for i in range(8):
                            c = g * 8 + i
                            mm = nc.tensor.matmul(pm[g % 2][:, i, :], wconv[:, c * 128:(c + 1) * 128], xt[:, :, c],
                                                  start=True, stop=True)
                        mm.then_inc(conved, 1)
                    pe.wait_ge(conved_dve, j * (MG // 2) + (MG // 2 + 1))
                    pe.wait_ge(conved_act, j * (MG // 2) + (MG // 2 + 1))
                    for g in range(TG):
                        pe.wait_ge(back_out, j * TG + (g + 1))
                        for i in range(4):
                            mm = nc.tensor.transpose(pt[g % 2][0:C, i * 128:(i + 1) * 128], xt[:, g * 4 + i, :],
                                                     w["ident"][:])
                        mm.then_inc(back, 1)
                        if g:
                            project(j, g - 1)
                    project(j, TG - 1)


def attend(core, w, stats, nbr_w, nbr_i, gscale, gbias):
    nc, d = core.nc, core.d
    UW = 16
    UT = UW * P
    N = NW // UW
    UPR = GW // UW
    SLOTS = 4
    BODY = SLOTS * UPR
    T = NW // 128
    AHEAD = 2
    QUARTERS = 4
    ROW = C * P // QUARTERS
    assert BODY * UW == 128 and BODY == 2 * QUARTERS
    near = d["xg"].rearrange("n (h v) -> (n h) v", h=QUARTERS)
    ctx_out = d["ctx"].rearrange("(t n) (h v) -> n t h v", n=128, h=QUARTERS)
    x = d["x"].rearrange("b c (g r) w -> c b g (r w)", r=GS)
    cg = d["ctx"].rearrange("(t n) (c s) -> c t n s", n=GW, c=C)
    part, x1 = d["part"], d["x1"]
    with core.stage() as k:
        xw = k.sb("d_xw", [C, SLOTS, RT])
        cx = k.sb("d_cx", [C + 1, SLOTS, GW, P])
        pr = k.sb("d_pr", [C, SLOTS, RT])
        tq = k.sb("d_tq", [C + 1, 2, UT])
        mx = k.sb("d_mx", [128, 2, 8])
        sm = k.sb("d_sm", [128, 2, 8])
        rs = k.sb("d_rs", [128, 2, 8])
        ex = k.sb("d_ex", [128, 2, 8, P])
        pn = k.sb("d_pn", [128, 2, 8, P])
        vt = k.sb("d_vt", [128, 2, 8, C])
        at = k.sb("d_at", [128, 2, UW, P])
        rows_near = k.sb("d_rows_near", [128, 2, TOPK, ROW])
        every = k.sb("d_every", [128, T, QUARTERS, TOPK], U32)
        idx = k.sb("d_idx", [128, 2, TOPK], U32)
        p_t = k.ps("d_p_t", [C + 1, UT])
        p_s = [k.ps(f"d_p_s{i}", [128, 8, P]) for i in range(2)]
        p_v = k.ps("d_p_v", [128, 512])
        p_a = k.ps("d_p_a", [128, 4, 128])
        p_o = k.ps("d_p_o", [C, UW, GS, GS])
        xw_in, cx_in, pr_in, x1_out = ([k.sem(f"d_{n}{s}") for s in range(SLOTS)]
                                       for n in ("xw_in", "cx_in", "pr_in", "x1_out"))
        (ones, queries, queries_out, scores, maxed, centred, exped, softmaxed, p_ready, values, values_out,
         turned, turned_out, attended, added, x1_ready) = (
            k.sem("d_" + n) for n in ("ones", "queries", "queries_out", "scores", "maxed", "centred", "exped",
                                      "softmaxed", "p_ready", "values", "values_out", "turned", "turned_out",
                                      "attended", "added", "x1_ready"))

        scales = k.sb("d_scales", [C, T])
        biases = k.sb("d_biases", [C + 1, T])
        gcur = k.sb("d_gcur", [C, C + 1])
        gbcur = k.sb("d_gbcur", [C + 1, 1])
        folded, spread, cur_set = (k.sem("d_" + n) for n in ("folded", "spread", "cur_set"))
        every_set, idx_set, summed = (k.sem("d_" + n) for n in ("every_set", "idx_set", "summed"))
        got, ctx_done = ([k.sem(f"d_{n}{s}") for s in range(2)] for n in ("got", "ctx_done"))

        def mixes(n, i):
            return not isinstance(n, int) or 0 <= n < N - AHEAD * BODY

        def wait(eng, sem, value):
            if not isinstance(value, int) or value > 0:
                eng.wait_ge(sem, value)

        def units(step):
            def over(eng):
                for j in range(-2, BODY):
                    step(j, j % BODY, j // BODY, lambda m: m >= 0)
                with eng.Fori(1, T - AHEAD) as i:
                    for k in range(BODY):
                        step(i * BODY + k, k, i, lambda m: True)
                for j in range(N - AHEAD * BODY, N + 3):
                    step(j, j % BODY, j // BODY, lambda m: m < N)
            return over

        def landed(i, k):
            return (i + k // BODY) * 16 + 16

        def slot(k):
            return k % BODY // UPR

        with nc.Block() as block:
            @block.sync
            def _(sp):
                def load_x(b, g, s):
                    sp.dma_start(xw[:, s, :], x[:, b, g, :]).then_inc(xw_in[s], 16)

                def await_ctx(t):
                    for q in range(2):
                        sp.wait_ge(ctx_done[q], t * (QUARTERS // 2 * 16) + (QUARTERS // 2 * 16 + 16))

                def load_ctx(r, s):
                    sp.dma_start(cx[0:C, s, :, :], cg[:, r, :, :]).then_inc(cx_in[s], 16)

                def load_part(r, s):
                    sp.dma_start(pr[:, s, :], part[:, r, :]).then_inc(pr_in[s], 16)

                def store(i, s):
                    r = i * SLOTS + s
                    sp.wait_ge(x1_ready, r * UPR + UPR)
                    sp.dma_start(x1[:, r, :], pr[:, s, :]).then_inc(x1_out[s], 16)

                def turn_over(b, m, t):
                    await_ctx(t)
                    for s in range(SLOTS):
                        r = t * SLOTS + s
                        sp.wait_ge(queries, r * UPR - (SLOTS - 1) * UPR)
                        load_x(b, m * SLOTS + s, s)
                        sp.wait_ge(values, r * (2 * UPR) - (SLOTS - 1) * (2 * UPR))
                        load_ctx(r, s)
                        store(t - 1, s)
                        sp.wait_ge(x1_out[s], t * 16)
                        load_part(r, s)

                for s in range(SLOTS):
                    load_x(0, s, s)
                    load_part(s, s)
                await_ctx(0)
                for s in range(SLOTS):
                    load_ctx(s, s)
                per = T // B
                with sp.Fori(1, per) as m:
                    turn_over(0, m, m)
                with sp.Fori(1, B) as b:
                    with sp.Fori(0, per) as m:
                        turn_over(b, m, b * per + m)
                for s in range(SLOTS):
                    store(NT // SLOTS - 1, s)
                for s in range(SLOTS):
                    sp.wait_ge(x1_out[s], NT // SLOTS * 16)

            @block.tensor
            def _(pe):
                def make_queries(n, k, i):
                    if k % UPR == 0:
                        pe.wait_ge(xw_in[slot(k)], landed(i, k))
                    if k % BODY == 0:
                        pe.wait_ge(cur_set, i + k // BODY + 1)
                    wait(pe, queries_out, n)
                    for h in range(2):
                        lo = (k % UPR) * UW + h * 8
                        row = xw[:, slot(k), :].rearrange("c (r n k) -> c n r k", r=GS, k=GS)
                        mm = nc.tensor.matmul(p_t[:, h * 512:(h + 1) * 512], gcur[:], row[:, lo:lo + 8],
                                              start=True, stop=True)
                    mm.then_inc(queries, 1)

                def make_values(n, k, h):
                    wait(pe, values_out, n * 2 + h)
                    for j in range(4):
                        lo = (k % UPR) * UW + (h * 4 + j) * 2
                        mm = nc.tensor.matmul(p_v[:, j * C:(j + 1) * C],
                                              cx[0:C, slot(k), lo:lo + 2, :].rearrange("c n s -> c (n s)"),
                                              w["wvp"][:], start=True, stop=True)
                    mm.then_inc(values, 1)

                def score(n, k, i):
                    if k % UPR == 0:
                        pe.wait_ge(cx_in[slot(k)], landed(i, k))
                    pe.wait_ge(queries_out, n + 1)
                    wait(pe, centred, n - 1)
                    for v in range(UW):
                        half, col = v // 2 % 2, 2 * (v // 4) + v % 2
                        mm = nc.tensor.matmul(p_s[k % 2][half * P:(half + 1) * P, col, :],
                                              tq[:, k % 2, v * P:(v + 1) * P],
                                              cx[:, slot(k), (k % UPR) * UW + v, :], start=True, stop=True)
                    mm.then_inc(scores, 1)

                def turn(n, k):
                    pe.wait_ge(p_ready, n + 1)
                    wait(pe, turned_out, n)
                    for j in range(4):
                        mm = nc.tensor.transpose(p_a[:, j, :],
                                                 pn[:, k % 2, 2 * j:2 * j + 2, :].rearrange("p n s -> p (n s)"),
                                                 w["ident"][:])
                    mm.then_inc(turned, 1)

                def apply(n, k):
                    pe.wait_ge(turned_out, n + 1)
                    pe.wait_ge(values_out, n * 2 + 2)
                    wait(pe, added, n)
                    for j in range(UW // 2):
                        mm = nc.tensor.matmul(
                            p_o[:, 2 * j:2 * j + 2, :, :].rearrange("c n r k -> c (n r k)"), vt[:, k % 2, j, :],
                            at[:, k % 2, 2 * j:2 * j + 2, :].rearrange("p n s -> p (n s)"), start=True, stop=True)
                    mm.then_inc(attended, 1)

                def step(n, k, i, live):
                    if live(n + 2):
                        make_queries(n + 2, k + 2, i)
                    if live(n):
                        make_values(n, k, 0)
                    if live(n + 1):
                        score(n + 1, k + 1, i)
                    if live(n):
                        make_values(n, k, 1)
                        turn(n, k)
                    if live(n - 1):
                        apply(n - 1, k - 1)

                nc.tensor.matmul(p_t[:, 0:B], w["g"][:], gbias[:], start=True, stop=True).then_inc(folded, 1)
                pe.wait_ge(spread, 1)
                pe.wait_ge(ones, 1)
                units(step)(pe)

            @block.scalar
            def _(act):
                nc.scalar.preload_act_table(ACT.Exp)

                def set_current(t):
                    nc.scalar.copy(gbcur[:], biases[:, bass.ds(t, 1)] if not isinstance(t, int) else
                                   biases[:, t:t + 1])
                    nc.scalar.activation(gcur[:], w["g"][:], ACT.Copy,
                                         scale=scales[:, bass.ds(t, 1)] if not isinstance(t, int) else
                                         scales[:, t:t + 1]).then_inc(cur_set, 1)
                    act.wait_ge(cur_set, t + 1)

                for s in range(2):
                    act.sem_inc(ctx_done[s], 16)

                def store_ctx(t, h):
                    act.wait_ge(summed, t * (QUARTERS * TOPK) + (h + 1) * TOPK)
                    core.apart(act)
                    nc.scalar.dma_start(ctx_out[:, t, h, :], rows_near[:, h % 2, 0, :]).then_inc(ctx_done[h % 2], 16)

                for t in range(AHEAD):
                    for h in range(QUARTERS):
                        store_ctx(t, h)
                act.wait_ge(ones, 1)
                act.wait_ge(spread, 1)
                set_current(0)

                def step(n, k, i, live):
                    if live(n + 2):
                        act.wait_ge(queries, n + 3)
                        nc.scalar.activation(tq[:, k % 2, :], p_t[:], ACT.Identity, bias=gbcur[:, 0:1]
                                             ).then_inc(queries_out, 1)
                    for h in range(2):
                        if live(n):
                            act.wait_ge(values, n * 2 + (h + 1))
                            nc.scalar.copy(vt[:, k % 2, h * 4:(h + 1) * 4, :],
                                           p_v[:, 0:4 * C].rearrange("p (n c) -> p n c", n=4)).then_inc(values_out, 1)
                    if live(n):
                        act.wait_ge(turned, n + 1)
                        for h in range(2):
                            ins = nc.scalar.copy(at[h * P:(h + 1) * P, k % 2, h::2, :],
                                                 p_a[h * P:(h + 1) * P, :, :].rearrange("p i (n s) -> p (i n) s", n=2))
                        ins.then_inc(turned_out, 1)
                    if live(n + 1):
                        act.wait_ge(centred, n + 2)
                        e = ex[:, (k + 1) % 2, :, :]
                        nc.scalar.activation(e, e, ACT.Exp, scale=SCALE).then_inc(exped, 1)
                    if mixes(n, i) and k % 2:
                        store_ctx(i + AHEAD, k // 2)
                    if k == BODY - 3 and (not isinstance(n, int) or 0 <= n < N - BODY):
                        set_current(i + 1)

                units(step)(act)

            @block.vector
            def _(dve):
                nc.vector.memset(at[:], 0.0)
                nc.vector.memset(cx[C:C + 1, :, :, :], 1.0).then_inc(ones, 1)
                for h in range(QUARTERS):
                    ins = nc.vector.tensor_scalar(every[:, :, h, :], nbr_i[:], float(QUARTERS), float(h),
                                                  ALU.mult, ALU.add)
                ins.then_inc(every_set, 1)
                dve.wait_ge(folded, 1)
                for b in range(B):
                    per = slice(b * (T // B), (b + 1) * (T // B))
                    nc.vector.tensor_copy(scales[:, per], gscale[:, b:b + 1].to_broadcast([C, T // B]))
                    ins = nc.vector.tensor_scalar(biases[:, per], p_t[:, b:b + 1].to_broadcast([C + 1, T // B]),
                                                  w["gb"][:, 0:1], None, ALU.add)
                ins.then_inc(spread, 1)

                def mix(t, h, j):
                    s, wj = h % 2, nbr_w[:, t, j:j + 1]
                    to = rows_near[:, s, 0, :]
                    if j == 0:
                        dve.wait_ge(got[s], t * (QUARTERS // 2 * 16 * TOPK) + (h // 2 + 1) * 16 * TOPK)
                        ins = nc.vector.tensor_scalar(to, to, wj, None, ALU.mult)
                    else:
                        dve.wait_ge(summed, t * (QUARTERS * TOPK) + (h * TOPK + j))
                        ins = nc.vector.scalar_tensor_tensor(to, rows_near[:, s, j, :], wj, to, ALU.mult, ALU.add)
                    ins.then_inc(summed, 1)

                for t in range(AHEAD):
                    for h in range(QUARTERS):
                        for j in range(TOPK):
                            mix(t, h, j)

                def step(n, k, i, live):
                    m, s = n + 1, (k + 1) % 2
                    if mixes(n, i):
                        mix(i + AHEAD, k // 2, 2 if k % 2 else 0)
                    if live(m):
                        dve.wait_ge(scores, m + 1)
                        nc.vector.tensor_reduce(mx[:, s, :], p_s[s][:], AX.X, ALU.max).then_inc(maxed, 1)
                        dve.wait_ge(maxed, m + 1)
                        nc.vector.tensor_tensor(ex[:, s, :, :], p_s[s][:],
                                                mx[:, s, :].unsqueeze(2).to_broadcast([128, 8, P]),
                                                ALU.subtract).then_inc(centred, 1)
                    if live(n - 2):
                        o, q = n - 2, k - 2
                        half = q % UPR
                        if half == 0:
                            dve.wait_ge(pr_in[slot(q)], landed(i, q))
                        dve.wait_ge(attended, o + 1)
                        rows = pr[:, slot(q), :].rearrange("c (r w) -> c r w", r=GS)
                        res = rows[:, :, half * 128:half * 128 + 128].rearrange("c r (n k) -> c n r k", k=GS)
                        nc.vector.tensor_tensor(res, p_o[:], res, ALU.add).then_inc(added, 1)
                        dve.wait_ge(added, o + 1)
                        for h in range(2):
                            st = stats[:, bass.ds(o * 12 + h * 6, 6)] if not isinstance(o, int) else \
                                stats[:, o * 12 + h * 6:o * 12 + h * 6 + 6]
                            ins = nc.vector.bn_stats(st, rows[:, h * 4:h * 4 + 4, half * 128:half * 128 + 128])
                        ins.then_inc(x1_ready, 1)
                    if mixes(n, i) and k % 2 == 0:
                        mix(i + AHEAD, k // 2, 1)
                    if live(m):
                        dve.wait_ge(exped, m + 1)
                        nc.vector.tensor_reduce(sm[:, s, :], ex[:, s, :, :], AX.X, ALU.add).then_inc(softmaxed, 1)
                        dve.wait_ge(softmaxed, m * 2 + 1)
                        nc.vector.reciprocal(rs[:, s, :], sm[:, s, :]).then_inc(softmaxed, 1)
                        dve.wait_ge(softmaxed, m * 2 + 2)
                        nc.vector.tensor_tensor(pn[:, s, :, :], ex[:, s, :, :],
                                                rs[:, s, :].unsqueeze(2).to_broadcast([128, 8, P]),
                                                ALU.mult).then_inc(p_ready, 1)

                units(step)(dve)

            @block.gpsimd
            def _(pool):
                pool.wait_ge(every_set, 1)
                with pool.Fori(0, T) as t:
                    for h in range(QUARTERS):
                        s = h % 2
                        pool.wait_ge(ctx_done[s], t * (QUARTERS // 2 * 16) + (h // 2 * 16 + 16))
                        nc.gpsimd.tensor_copy(idx[:, s, :], every[:, t, h, :]).then_inc(idx_set, 1)
                        pool.wait_ge(idx_set, t * QUARTERS + (h + 1))
                        core.apart(pool)
                        for j in range(TOPK):
                            pool.indirect_dma_start(rows_near[:, s, j, :], None, near[:],
                                                    bass.IndirectOffsetOnAxis(idx[:, s, j:j + 1], 0)
                                                    ).then_inc(got[s], 16)


HALF = 1024
TILE = 2 * HALF
NTILE = B * L // TILE


def tokens(ap):
    if len(ap.shape) == 3:
        ap = ap.rearrange("c a b -> c (a b)")
    return ap.rearrange("c (t n) -> c t n", n=TILE)


def image_units(n, body, step, start=lambda b: None, ahead=2, behind=0):
    def over(eng):
        with eng.Fori(0, B) as b:
            start(b)
            for j in range(-ahead, body):
                step(b * n + j, j % body, b, j // body, lambda o, j=j: j + o >= 0)
            with eng.Fori(1, n // body - 1) as i:
                for j in range(body):
                    step(b * n + i * body + j, j, b, i, lambda o: True)
            for j in range(n - body, n + behind):
                step(b * n + j, j % body, b, j // body, lambda o, j=j: 0 <= j + o < n)
    return over


def project_in(core, w, gscale, gbias):
    nc, d = core.nc, core.d
    x1, xc, zs = tokens(d["x1"]), tokens(d["xc"]), tokens(d["zs"])
    PER = NTILE // B
    with core.stage() as k:
        xi = k.sb("p_xi", [C, 4, TILE])
        xo = k.sb("p_xo", [C, 2, TILE])
        zo = k.sb("p_zo", [C, 2, TILE])
        wcur = k.sb("p_wcur", [C, 2 * C])
        bias = k.sb("p_bias", [C, 2, B])
        bcur = k.sb("p_bcur", [C, 2])
        px = [k.ps(f"p_px{i}", [C, HALF]) for i in range(2)]
        pz = [k.ps(f"p_pz{i}", [C, HALF]) for i in range(2)]
        x_in = [k.sem(f"p_x_in{s}") for s in range(4)]
        xc_out, zs_out = ([k.sem(f"p_{n}{s}") for s in range(2)] for n in ("xc_out", "zs_out"))
        biased, bias_set, w_set, b_set, made, xc_ready, zs_ready = (
            k.sem("p_" + n) for n in ("biased", "bias_set", "w_set", "b_set", "made", "xc_ready", "zs_ready"))
        with nc.Block() as block:
            @block.sync
            def _(sp):
                with sp.Fori(0, NTILE // 4) as i:
                    for s in range(4):
                        sp.wait_ge(made, i * 8 + (2 * s + 2))
                        sp.dma_start(xi[:, s, :], x1[:, i * 4 + s, :]).then_inc(x_in[s], 16)

            @block.tensor
            def _(pe):
                pe.sem_inc(made, 8)
                for h in range(2):
                    mm = nc.tensor.matmul(px[0][:, h * B:(h + 1) * B], w["inw"][:, h * C:(h + 1) * C], gbias[:],
                                          start=True, stop=True)
                mm.then_inc(biased, 1)
                pe.wait_ge(bias_set, 1)
                with pe.Fori(0, B) as b:
                    pe.wait_ge(w_set, b + 1)
                    core.apart(pe)
                    with pe.Fori(0, PER // 4) as i:
                        for s in range(4):
                            pe.wait_ge(x_in[s], b * (PER // 4 * 16) + i * 16 + 16)
                            for h in range(2):
                                n = b * (2 * PER) + i * 8 + (2 * s + h)
                                pe.wait_ge(xc_ready, n + 1)
                                pe.wait_ge(zs_ready, n + 1)
                                for p, lo in ((px, 0), (pz, C)):
                                    for q in range(2):
                                        mm = nc.tensor.matmul(
                                            p[h][:, q * 512:(q + 1) * 512], wcur[:, lo:lo + C],
                                            xi[:, s, h * HALF + q * 512:h * HALF + (q + 1) * 512],
                                            start=True, stop=True)
                                mm.then_inc(made, 1)

            @block.vector
            def _(dve):
                dve.sem_inc(xc_ready, 2)
                dve.wait_ge(biased, 1)
                nc.vector.tensor_copy(bias[:], px[0][:, 0:2 * B].rearrange("c (h b) -> c h b", h=2)
                                      ).then_inc(bias_set, 1)
                dve.wait_ge(bias_set, 1)
                with dve.Fori(0, B) as b:
                    dve.wait_ge(made, b * (2 * PER) + 8)
                    nc.vector.tensor_scalar(wcur[:], w["inw"][:], gscale[:, bass.ds(b, 1)], None, ALU.mult
                                            ).then_inc(w_set, 1)
                    dve.wait_ge(zs_ready, b * (2 * PER) + 2)
                    dve.wait_ge(xc_ready, b * (2 * PER) + 2)
                    nc.vector.tensor_copy(bcur[:], bias[:, :, b]).then_inc(b_set, 1)
                    dve.wait_ge(b_set, b + 1)
                    core.apart(dve)
                    with dve.Fori(0, PER // 2) as i:
                        for s in range(2):
                            dve.wait_ge(xc_out[s], b * (PER // 2 * 16) + i * 16)
                            for h in range(2):
                                dve.wait_ge(made, b * (2 * PER) + i * 4 + (2 * s + h + 9))
                                nc.vector.tensor_scalar(xo[:, s, h * HALF:(h + 1) * HALF], px[h][:],
                                                        bcur[:, 0:1], None, ALU.add).then_inc(xc_ready, 1)

            @block.scalar
            def _(act):
                nc.scalar.preload_act_table(ACT.Silu)
                act.sem_inc(zs_ready, 2)
                with act.Fori(0, B) as b:
                    act.wait_ge(b_set, b + 1)
                    with act.Fori(0, PER // 2) as i:
                        for s in range(2):
                            act.wait_ge(zs_out[s], b * (PER // 2 * 16) + i * 16)
                            for h in range(2):
                                act.wait_ge(made, b * (2 * PER) + i * 4 + (2 * s + h + 9))
                                nc.scalar.activation(zo[:, s, h * HALF:(h + 1) * HALF], pz[h][:], ACT.Silu,
                                                     bias=bcur[:, 1:2]).then_inc(zs_ready, 1)

            @block.gpsimd
            def _(pool):
                with pool.Fori(0, NTILE // 2) as i:
                    for s in range(2):
                        for ready, outs, to, src in ((xc_ready, xc_out, xc, xo), (zs_ready, zs_out, zs, zo)):
                            pool.wait_ge(ready, i * 4 + (2 * s + 4))
                            core.apart(pool)
                            pool.dma_start(to[:, i * 2 + s, :], src[:, s, :]).then_inc(outs[s], 16)
                for s in range(2):
                    pool.wait_ge(xc_out[s], NTILE // 2 * 16)
                    pool.wait_ge(zs_out[s], NTILE // 2 * 16)


def image_convs(core, w):
    nc, d = core.nc, core.d
    halves = d["xc"].rearrange("c (b t p) w -> c p t b w", b=B, p=128)
    xc = d["xc"].rearrange("c (b h) w -> c b h w", b=B)
    u = d["u"].rearrange("c (b h) w -> c b h w", b=B)
    T = H // 128
    GROUPS = T * B // 2
    NS = C // SEAM
    KS, MS = SEAM * B * 4, SEAM * B * 2
    with core.stage() as k:
        rows = k.sb("v_rows", [128, 3, 128])
        taps = k.sb("v_taps", [128, C * 9])
        cb = k.sb("v_cb", [128, C])
        xi = k.sb("v_xi", [128, 3, T, B, W + 2])
        band = k.sb("v_band", [128, 2, 3, 128])
        cbc = k.sb("v_cbc", [128, 2])
        uo = k.sb("v_uo", [128, 2, T, B, W])
        seams = k.sb("v_seams", [KS, 3, MS])
        seam_taps = k.sb("v_seam_taps", [KS, NS, 9])
        seam_cb = k.sb("v_seam_cb", [MS, NS])
        seam_band = k.sb("v_seam_band", [KS, NS, 3, MS])
        seam_x = k.sb("v_seam_x", [KS, NS, W + 2])
        seam_u = k.sb("v_seam_u", [MS, NS, W])
        pc = [k.ps(f"v_pc{i}", [128, 2, W]) for i in range(2 * GROUPS)]
        consts, zeroed, built, banded, made, acted, seam_in, seam_built, seam_made, seam_acted, seam_out = (
            k.sem("v_" + n) for n in ("consts", "zeroed", "built", "banded", "made", "acted", "seam_in",
                                      "seam_built", "seam_made", "seam_acted", "seam_out"))
        freed = k.sem("v_freed")
        x_in = [k.sem(f"v_x_in{s}") for s in range(3)]
        u_out = [k.sem(f"v_u_out{s}") for s in range(2)]
        STEPS = 6
        with nc.Block() as block:
            @block.sync
            def _(sp):
                loads = [(rows[:], d["rows"]), (taps[:], d["conv_w"].partition_broadcast(128)),
                         (cb[:], d["conv_b"].partition_broadcast(128)), (seams[:], d["seams"]),
                         (seam_taps[:], d["seam_taps"]), (seam_cb[:], d["seam_cb"])]
                for to, src in loads:
                    sp.dma_start(to, src).then_inc(consts, 16)
                sp.wait_ge(zeroed, 1)
                with sp.Fori(0, C // STEPS) as i:
                    for j in range(STEPS):
                        sp.wait_ge(made, i * (STEPS * GROUPS) + (j + 1) * GROUPS)
                        for t in range(T):
                            sp.dma_start(xi[:, j % 3, t, :, 1:W + 1], halves[i * STEPS + j, :, t, :, :]
                                         ).then_inc(x_in[j % 3], 16)
                for g in range(NS):
                    for c in range(SEAM):
                        sp.dma_start(seam_x[c * B * 4:(c + 1) * B * 4, g, 1:W + 1],
                                     xc[g * SEAM + c, :, H // 2 - 2:H // 2 + 2, :]).then_inc(seam_in, 16)
                for g in range(NS):
                    sp.wait_ge(seam_acted, g + 1)
                    for c in range(SEAM):
                        sp.dma_start(u[g * SEAM + c, :, H // 2 - 1:H // 2 + 1, :],
                                     seam_u[c * B * 2:(c + 1) * B * 2, g, :]).then_inc(seam_out, 16)
                sp.wait_ge(seam_out, 16 * C)

            @block.vector
            def _(dve):
                nc.vector.memset(seam_x[:], 0.0)
                nc.vector.memset(xi[:], 0.0).then_inc(zeroed, 1)
                dve.wait_ge(consts, 96)
                with dve.Fori(0, C // 2) as i:
                    for s in range(2):
                        dve.wait_ge(made, i * (2 * GROUPS) + (s + 2) * GROUPS)
                        dve.wait_ge(acted, i * (2 * GROUPS) + (s + 1) * GROUPS)
                        nc.vector.tensor_copy(cbc[:, s:s + 1], cb[:, bass.ds(i * 2 + s, 1)])
                        for dy in range(3):
                            if dy:
                                dve.wait_ge(built, (i * 2 + s) * 2 + dy)
                            for dx in range(3):
                                tap = taps[:, bass.ds(i * 18 + (s * 9 + dy * 3 + dx), 1)]
                                to = band[:, s, dx, :]
                                if dy == 0:
                                    ins = nc.vector.tensor_scalar(to, rows[:, dy, :], tap, None, ALU.mult)
                                else:
                                    ins = nc.vector.scalar_tensor_tensor(to, rows[:, dy, :], tap, to,
                                                                         ALU.mult, ALU.add)
                            ins.then_inc(banded if dy == 2 else built, 1)
                for dy in range(3):
                    if dy:
                        dve.wait_ge(seam_built, dy)
                    for g in range(NS):
                        for dx in range(3):
                            tap = seam_taps[:, g, dy * 3 + dx:dy * 3 + dx + 1]
                            to = seam_band[:, g, dx, :]
                            if dy == 0:
                                ins = nc.vector.tensor_scalar(to, seams[:, dy, :], tap, None, ALU.mult)
                            else:
                                ins = nc.vector.scalar_tensor_tensor(to, seams[:, dy, :], tap, to,
                                                                     ALU.mult, ALU.add)
                    ins.then_inc(seam_built, 1)

            @block.tensor
            def _(pe):
                pe.sem_inc(made, 3 * GROUPS)
                with pe.Fori(0, C // STEPS) as i:
                    for j in range(STEPS):
                        pe.wait_ge(banded, i * STEPS + (j + 1))
                        pe.wait_ge(x_in[j % 3], (i * 2 + (j // 3 + 1)) * (16 * T))
                        for g in range(GROUPS):
                            pe.wait_ge(acted, i * (STEPS * GROUPS) + (j * GROUPS + g + 1))
                            t, b = g // 2, g % 2 * 2
                            for dx in range(3):
                                mm = nc.tensor.matmul(pc[j % 2 * GROUPS + g][:], band[:, j % 2, dx, :],
                                                      xi[:, j % 3, t, b:b + 2, dx:dx + W],
                                                      start=(dx == 0), stop=(dx == 2))
                            mm.then_inc(made, 1)
                pe.wait_ge(seam_built, 3)
                pe.wait_ge(seam_in, 16 * C)
                pe.wait_ge(acted, (C + 2) * GROUPS)
                for g in range(NS):
                    if g >= 2 * GROUPS:
                        pe.wait_ge(seam_acted, g - 2 * GROUPS + 1)
                    for dx in range(3):
                        mm = nc.tensor.matmul(pc[g % (2 * GROUPS)][0:MS, 0, :], seam_band[:, g, dx, :],
                                              seam_x[:, g, dx:dx + W], start=(dx == 0), stop=(dx == 2))
                    mm.then_inc(seam_made, 1)

            @block.scalar
            def _(act):
                nc.scalar.preload_act_table(ACT.Silu)
                act.sem_inc(acted, 2 * GROUPS)
                with act.Fori(0, C // 2) as i:
                    for s in range(2):
                        act.wait_ge(freed, i * 2 + (s + 1))
                        for g in range(GROUPS):
                            act.wait_ge(made, i * (2 * GROUPS) + ((s + 3) * GROUPS + g + 1))
                            nc.scalar.activation(uo[:, s, g // 2, g % 2 * 2:g % 2 * 2 + 2, :],
                                                 pc[s * GROUPS + g][:],
                                                 ACT.Silu, bias=cbc[:, s:s + 1]).then_inc(acted, 1)
                for g in range(NS):
                    act.wait_ge(seam_made, g + 1)
                    nc.scalar.activation(seam_u[:, g, :], pc[g % (2 * GROUPS)][0:MS, 0, :], ACT.Silu,
                                         bias=seam_cb[:, g:g + 1]).then_inc(seam_acted, 1)

            @block.gpsimd
            def _(pool):
                pool.sem_inc(freed, 2)
                with pool.Fori(0, C // 2) as i:
                    for s in range(2):
                        pool.wait_ge(acted, i * (2 * GROUPS) + (s + 3) * GROUPS)
                        for t in range(T):
                            row = t * 128 + t
                            pool.dma_start(u[i * 2 + s, :, row:row + 127, :].rearrange("b p w -> p b w"),
                                           uo[t:t + 127, s, t, :, :]).then_inc(u_out[s], 16)
                        pool.wait_ge(u_out[s], i * (16 * T) + 16 * T)
                        pool.sem_inc(freed, 1)
                for s in range(2):
                    pool.wait_ge(u_out[s], C // 2 * 16 * T)


def scan_pass(core, w, way):
    nc, d = core.nc, core.d
    u, yf, y = tokens(d["u"]), tokens(d["yf"]), tokens(d["y"])
    PER = NTILE // B
    N = 2 * PER
    SLOTS = 4
    BODY = 2 * SLOTS
    DEEP = 4
    n_ = f"s{way}_"
    with core.stage() as k:
        ui = k.sb(n_ + "ui", [C + 1, SLOTS, TILE])
        fi = k.sb(n_ + "fi", [C, SLOTS, TILE]) if way else None
        yo = k.sb(n_ + "yo", [C, 2, TILE])
        ex = k.sb(n_ + "ex", [C, 2, HALF])
        dl = k.sb(n_ + "dl", [C, 2, HALF])
        da = k.sb(n_ + "da", [C, DEEP, HALF])
        db = k.sb(n_ + "db", [C, DEEP, HALF])
        hs = k.sb(n_ + "hs", [C, 2, HALF])
        us = k.sb(n_ + "us", [C, DEEP, HALF]) if way else None
        p_d = [k.ps(f"{n_}p_d{i}", [C, HALF]) for i in range(2)]
        p_b = k.ps(n_ + "p_b", [C, HALF])
        p_c = k.ps(n_ + "p_c", [C, HALF])
        u_in, f_in = ([k.sem(f"{n_}{n}{s}") for s in range(SLOTS)] for n in ("u_in", "f_in"))
        y_out = [k.sem(f"{n_}y_out{s}") for s in range(2)]
        (ones, raw, b_made, c_made, sized, exped, logged, delta, decays, gained, bu, scanned, y_ready, skip, skipped,
         cleared, seen) = (
            k.sem(n_ + n) for n in ("ones", "raw", "b_made", "c_made", "sized", "exped", "logged", "delta", "decays", "gained",
                                    "bu", "scanned", "y_ready", "skip", "skipped", "cleared", "seen"))

        def units(step, start=lambda b: None):
            return image_units(N, BODY, step, start, ahead=3)

        def landed(b, i, k):
            return b * (PER // SLOTS * 16) + (i + k // BODY) * 16 + 16

        def half(k, n=HALF):
            h = k % 2 if way == 0 else 1 - k % 2
            return slice(h * n, (h + 1) * n)

        def slot(k):
            return k % BODY // 2

        def place(t):
            return t if way == 0 else NTILE - 1 - t

        with nc.Block() as block:
            @block.sync
            def _(sp):
                def load(t, s):
                    sp.dma_start(ui[0:C, s, :], u[:, place(t), :]).then_inc(u_in[s], 16)
                    if way:
                        sp.dma_start(fi[:, s, :], yf[:, place(t), :]).then_inc(f_in[s], 16)

                def store(t, s):
                    sp.wait_ge(y_ready, t * 2 + 3)
                    core.apart(sp)
                    sp.dma_start((yf if way == 0 else y)[:, place(t), :], yo[:, s % 2, :]).then_inc(y_out[s % 2], 16)

                for s in range(2):
                    sp.sem_inc(y_out[s], 16)
                for s in range(SLOTS):
                    load(s, s)
                with sp.Fori(0, NTILE // SLOTS - 1) as i:
                    for s in range(SLOTS):
                        t = i * SLOTS + s
                        store(t, s)
                        load(t + SLOTS, s)
                for s in range(SLOTS):
                    store(NTILE - SLOTS + s, s)
                for s in range(2):
                    sp.wait_ge(y_out[s], NTILE // 2 * 16 + 16)

            @block.tensor
            def _(pe):
                def product(p, lhs, k, rows):
                    for q in range(2):
                        lo = half(k).start + q * 512
                        mm = nc.tensor.matmul(p[:, q * 512:(q + 1) * 512], lhs, ui[0:rows, slot(k), lo:lo + 512],
                                              start=True, stop=True)
                    return mm

                def step(m, k, b, i, live):
                    if live(0):
                        pe.wait_ge(bu, m + 1)
                        product(p_b, w["bc"][:, way, 0, :], k, C).then_inc(b_made, 1)
                    if live(3):
                        kk = k + 3
                        if kk % 2 == 0:
                            pe.wait_ge(u_in[slot(kk)], landed(b, i, kk))
                        pe.wait_ge(delta, m + 4)
                        product(p_d[kk % 2], w["wd"][:, way, :], kk, C + 1).then_inc(raw, 1)
                    if live(0):
                        if way:
                            pe.wait_ge(seen, m + 1)
                        else:
                            pe.wait_ge(y_ready, m + 1)
                        product(p_c, w["bc"][:, way, 1, :], k, C).then_inc(c_made, 1)

                pe.wait_ge(ones, 1)
                units(step)(pe)

            @block.scalar
            def _(act):
                nc.scalar.preload_act_table_set("natural_log_exp_and_others")

                def step(m, k, b, i, live):
                    kk = k + 2
                    e = ex[:, (k + 3) % 2, :]
                    if live(3):
                        act.wait_ge(raw, m + 4)
                        nc.scalar.activation(e, p_d[(k + 3) % 2][:], ACT.Abs).then_inc(sized, 1)
                    if live(2):
                        act.wait_ge(delta, m + 5)
                        nc.scalar.activation(da[:, kk % DEEP, :], dl[:, kk % 2, :], ACT.Exp,
                                             scale=w["nega"][:, way:way + 1]).then_inc(decays, 1)
                    if live(3):
                        act.wait_ge(sized, m + 4)
                        nc.scalar.activation(e, e, ACT.Exp, scale=-1.0).then_inc(exped, 1)
                    if live(2) and way:
                        nc.scalar.activation(us[:, kk % DEEP, :], ui[0:C, slot(kk), half(kk)], ACT.Identity,
                                             scale=w["dsum"][:, 0:1]).then_inc(skip, 1)
                    if live(3):
                        act.wait_ge(exped, m + 4)
                        nc.scalar.activation(e, e, ACT.Ln, bias=1.0).then_inc(logged, 1)

                units(step)(act)

            @block.gpsimd
            def _(pool):
                def step(m, k, b, i, live):
                    if live(2):
                        kk = k + 2
                        pool.wait_ge(delta, m + 5)
                        nc.gpsimd.tensor_tensor(db[:, kk % DEEP, :], dl[:, kk % 2, :], ui[0:C, slot(kk), half(kk)],
                                                ALU.mult).then_inc(gained, 1)
                        if way:
                            pool.wait_ge(skip, m + 3)
                            if kk % 2 == 0:
                                pool.wait_ge(f_in[slot(kk)], landed(b, i, kk))
                            us_ = us[:, kk % DEEP, :]
                            nc.gpsimd.tensor_tensor(us_, us_, fi[:, slot(kk), half(kk)], ALU.add
                                                    ).then_inc(skipped, 1)

                units(step)(pool)

            @block.vector
            def _(dve):
                dve.sem_inc(delta, 2)
                dve.sem_inc(y_ready, 1)
                dve.sem_inc(bu, 1)
                dve.sem_inc(seen, 1)
                nc.vector.memset(ui[C:C + 1, :, :], 1.0).then_inc(ones, 1)

                def start(b):
                    last = HALF - 1 if way == 0 else 0
                    dve.wait_ge(y_ready, b * N + 1)
                    nc.vector.memset(hs[:, 1, last:last + 1], 0.0).then_inc(cleared, 1)
                    dve.wait_ge(cleared, b + 1)

                def step(m, k, b, i, live):
                    if live(0):
                        d = db[:, k % DEEP, :]
                        dve.wait_ge(gained, m + 1)
                        dve.wait_ge(b_made, m + 1)
                        nc.vector.tensor_tensor(d, d, p_b[:], ALU.mult).then_inc(bu, 1)
                        dve.wait_ge(decays, m + 1)
                    if live(2):
                        kk = k % 2
                        dve.wait_ge(logged, m + 3)
                        nc.vector.scalar_tensor_tensor(dl[:, kk, :], p_d[kk][:], 0.0, ex[:, kk, :],
                                                       ALU.max, ALU.add).then_inc(delta, 1)
                    if live(0):
                        dve.wait_ge(bu, m + 2)
                        r = slice(None) if way == 0 else slice(None, None, -1)
                        before = hs[:, (k + 1) % 2, HALF - 1:HALF] if way == 0 else hs[:, (k + 1) % 2, 0:1]
                        nc.vector.tensor_tensor_scan(hs[:, k % 2, r], da[:, k % DEEP, r], db[:, k % DEEP, r], before,
                                                     ALU.mult, ALU.add).then_inc(scanned, 1)
                        dve.wait_ge(scanned, m + 1)
                        dve.wait_ge(c_made, m + 1)
                        if k % 2 == 0:
                            dve.wait_ge(y_out[k // 2 % 2], b * (PER // 2 * 16) + i * (SLOTS // 2 * 16)
                                        + (k // 4 * 16 + 16))
                        to = yo[:, k // 2 % 2, half(k)]
                        nc.vector.tensor_tensor(to, hs[:, k % 2, :], p_c[:], ALU.mult).then_inc(
                            seen if way else y_ready, 1)
                        if way:
                            dve.wait_ge(seen, m + 2)
                            dve.wait_ge(skipped, m + 1)
                            nc.vector.tensor_tensor(to, to, us[:, k % DEEP, :], ALU.add).then_inc(y_ready, 1)

                units(step, start)(dve)


def norm_gate_out(core, w):
    nc, d = core.nc, core.d
    x1, y, zs = tokens(d["x1"]), tokens(d["y"]), tokens(d["zs"])
    out = d["out"].rearrange("b c h w -> c b (h w)").rearrange("c b (t n) -> c b t n", n=TILE)
    PER = NTILE // B
    SLOTS = 4
    BODY = 2 * SLOTS
    N = 2 * PER
    with core.stage() as k:
        yi, xi, zi = (k.sb("o_" + n, [C, SLOTS, TILE]) for n in ("yi", "xi", "zi"))
        sq, rs, tn, gt = (k.sb("o_" + n, [C, 2, HALF]) for n in ("sq", "rs", "tn", "gt"))
        eps = k.sb("o_eps", [C, 1])
        p_y = [k.ps(f"o_p_y{i}", [C, HALF]) for i in range(2)]
        p_v = k.ps("o_p_v", [C, HALF])
        p_o = k.ps("o_p_o", [C, HALF])
        y_in, x_in, z_in, out_done = ([k.sem(f"o_{n}{s}") for s in range(SLOTS)]
                                      for n in ("y_in", "x_in", "z_in", "out_done"))
        (eps_set, centred, squared, vared, logged, rooted, normed, affine, gated, projected, finished) = (
            k.sem("o_" + n) for n in ("eps_set", "centred", "squared", "vared", "logged", "rooted", "normed",
                                      "affine", "gated", "projected", "finished"))

        def landed(b, i, k):
            return b * (PER // SLOTS * 16) + (i + k // BODY) * 16 + 16

        def slot(k):
            return k % BODY // 2

        def half(k):
            return slice(k % 2 * HALF, (k % 2 + 1) * HALF)

        with nc.Block() as block:
            @block.sync
            def _(sp):
                def load(t, s):
                    sp.dma_start(yi[:, s, :], y[:, t, :]).then_inc(y_in[s], 16)
                    sp.dma_start(zi[:, s, :], zs[:, t, :]).then_inc(z_in[s], 16)
                    sp.dma_start(xi[:, s, :], x1[:, t, :]).then_inc(x_in[s], 16)

                def tiles(b, i, more):
                    for s in range(SLOTS):
                        t = b * PER + i * SLOTS + s
                        sp.wait_ge(finished, t * 2 + 3)
                        core.apart(sp)
                        sp.dma_start(out[:, b, i * SLOTS + s, :], xi[:, s, :]).then_inc(out_done[s], 16)
                        if more or s == 0:
                            last = (s - 1) % SLOTS
                            sp.wait_ge(out_done[last], b * (PER // SLOTS * 16) + i * 16 + (32 if s else 16))
                            load(t + SLOTS - 1, last)

                for s in range(SLOTS):
                    sp.sem_inc(out_done[s], 16)
                for s in range(SLOTS - 1):
                    load(s, s)
                with sp.Fori(0, B - 1) as b:
                    with sp.Fori(0, PER // SLOTS) as i:
                        tiles(b, i, True)
                with sp.Fori(0, PER // SLOTS - 1) as i:
                    tiles(B - 1, i, True)
                tiles(B - 1, PER // SLOTS - 1, False)
                for s in range(SLOTS):
                    sp.wait_ge(out_done[s], NTILE // SLOTS * 16 + 16)

            @block.tensor
            def _(pe):
                pe.sem_inc(projected, 1)

                def product(p, lhs, rhs, done):
                    for q in range(2):
                        mm = nc.tensor.matmul(p[:, q * 512:(q + 1) * 512], lhs, rhs[:, q * 512:(q + 1) * 512],
                                              start=True, stop=True)
                    mm.then_inc(done, 1)

                def step(m, k, b, i, live):
                    if live(2):
                        kk = k + 2
                        if kk % 2 == 0:
                            pe.wait_ge(y_in[slot(kk)], landed(b, i, kk))
                        pe.wait_ge(normed, m + 3)
                        product(p_y[kk % 2], w["centre"][:], yi[:, slot(kk), half(kk)], centred)
                    if live(0):
                        pe.wait_ge(gated, m + 2)
                        pe.wait_ge(finished, m + 1)
                        product(p_o, w["wo"][:], gt[:, k % 2, :], projected)
                    if live(2):
                        pe.wait_ge(squared, m + 3)
                        pe.wait_ge(logged, m + 2)
                        product(p_v, w["mean"][:], sq[:, k % 2, :], vared)

                image_units(N, BODY, step)(pe)

            @block.scalar
            def _(act):
                nc.scalar.preload_act_table_set("natural_log_exp_and_others")
                act.wait_ge(eps_set, 1)

                def step(m, k, b, i, live):
                    r = rs[:, (k + 1) % 2, :]
                    if live(1):
                        act.wait_ge(vared, m + 2)
                        nc.scalar.activation(r, p_v[:], ACT.Ln, bias=eps[:, 0:1]).then_inc(logged, 1)
                    if live(2):
                        act.wait_ge(centred, m + 3)
                        nc.scalar.activation(sq[:, k % 2, :], p_y[k % 2][:], ACT.Square).then_inc(squared, 1)
                    if live(1):
                        act.wait_ge(logged, m + 2)
                        nc.scalar.activation(r, r, ACT.Exp, scale=-0.5).then_inc(rooted, 1)

                image_units(N, BODY, step)(act)

            @block.vector
            def _(dve):
                dve.sem_inc(normed, 2)
                dve.sem_inc(finished, 1)
                nc.vector.memset(eps[:], GEPS).then_inc(eps_set, 1)

                def step(m, k, b, i, live):
                    if live(-1):
                        kk = (k - 1) % BODY
                        dve.wait_ge(x_in[slot(kk)], landed(b, i, k - 1))
                        dve.wait_ge(projected, m + 1)
                        x = xi[:, slot(kk), half(kk)]
                        nc.vector.scalar_tensor_tensor(x, p_o[:], w["scale"][:, 0:1], x, ALU.mult, ALU.add
                                                       ).then_inc(finished, 1)
                    if live(1):
                        kk = (k + 1) % 2
                        dve.wait_ge(rooted, m + 2)
                        dve.wait_ge(gated, m + 1)
                        nc.vector.tensor_tensor(tn[:, kk, :], p_y[kk][:], rs[:, kk, :], ALU.mult).then_inc(normed, 1)
                        dve.wait_ge(normed, m + 4)
                        nc.vector.tensor_scalar(tn[:, kk, :], tn[:, kk, :], w["onwb"][:, 0:1], w["onwb"][:, 1:2],
                                                ALU.mult, ALU.add).then_inc(affine, 1)

                image_units(N, BODY, step, behind=1)(dve)

            @block.gpsimd
            def _(pool):
                pool.sem_inc(gated, 1)

                def step(m, k, b, i, live):
                    if live(1):
                        kk = k + 1
                        if kk % 2 == 0:
                            pool.wait_ge(z_in[slot(kk)], landed(b, i, kk))
                        pool.wait_ge(affine, m + 2)
                        pool.wait_ge(projected, m + 1)
                        nc.gpsimd.tensor_tensor(gt[:, kk % 2, :], tn[:, kk % 2, :], zi[:, slot(kk), half(kk)],
                                                ALU.mult).then_inc(gated, 1)

                image_units(N, BODY, step)(pool)


def program(nc, dram, upto=99):
    with ExitStack() as ctx:
        core = Core(nc, ctx, dram)
        w = {n: core.sb("w_" + n, s) for n, s in dict(
            ident=[128, 128], group=[C, C], centre=[C, C], mean=[C, C], g=[C, C + 1], gb=[C + 1, 1],
            wvp=[C, C], wp1=[C + 1, C], lepe=[128, C * 9], wd=[C + 1, 2, C], bc=[C, 2, 2, C],
            nega=[C, 2], dsum=[C, 1], inw=[C, 2 * C], wo=[C, C], onwb=[C, 2], scale=[C, 1]).items()}
        gscale, gbias = core.sb("gscale", [C, B]), core.sb("gbias", [C, B])
        nbr_w = core.sb("nbr_w", [128, NW // 128, TOPK])
        nbr_i = core.sb("nbr_i", [128, NW // 128, TOPK], U32)
        setup_weights(core, w)
        with ExitStack() as early:
            wconv = early.enter_context(nc.sbuf_tensor("wconv", [128, C * 128], F32))
            with ExitStack() as pool:
                stats = pool.enter_context(nc.sbuf_tensor("stats", [C, NT * 24], F32))
                pooled = pool.enter_context(nc.sbuf_tensor("pooled", [C, NW], F32))
                image_stats(core, w, stats, pooled, wconv)
                group_coefficients(core, w, "g0", stats, gscale, gbias)
                top_windows(core, pooled, gscale, gbias, nbr_w, nbr_i)
            if upto < 2:
                return
            window_convs(core, w, wconv, gscale, gbias)
        if upto < 3:
            return
        with ExitStack() as pool:
            stats = pool.enter_context(nc.sbuf_tensor("stats1", [C, NT * 24], F32))
            attend(core, w, stats, nbr_w, nbr_i, gscale, gbias)
            group_coefficients(core, w, "g1", stats, gscale, gbias)
        if upto < 4:
            return
        project_in(core, w, gscale, gbias)
        if upto < 5:
            return
        image_convs(core, w)
        if upto < 6:
            return
        scan_pass(core, w, 0)
        if upto < 7:
            return
        scan_pass(core, w, 1)
        if upto < 8:
            return
        norm_gate_out(core, w)


def declare(nc, d):
    for name, shape in dict(xg=(NW, C * P), ctx=(NW, C * P), part=(C, NT, RT), x1=(C, NT, RT), xc=(C, B * H, W),
                            u=(C, B * H, W), yf=(C, B * L), y=(C, B * L), zs=(C, B * L)).items():
        d[name] = nc.dram_tensor("mid_" + name, shape, F32, kind="Internal").ap()


def arrays(i):
    f = lambda a: np.ascontiguousarray(a)
    col = lambda a: f(np.asarray(a).reshape(-1, 1))
    a = {k: np.asarray(v) for k, v in i.items()}
    xp = a["L1_conv_x_proj_w"]
    out = dict(
        x=f(a["x"]), wq_t=f(a["L0_conv_Wq"].T),
        wk_t_bk=f(np.concatenate([a["L0_conv_Wk"].T, a["L0_conv_bk"][:, None]], axis=1)),
        bq=col(a["L0_conv_bq"]), wv_t=f(a["L0_conv_Wv"].T),
        bv_lb=f(np.stack([a["L0_conv_bv"], a["L0_conv_lepe_b"]], axis=1)),
        wp=f(a["L0_conv_Wp"]), bp=f(a["L0_conv_bp"].reshape(1, C)), lepe_w=f(a["L0_conv_lepe_w"].reshape(C * 9)),
        xp_dt=f(xp[:, 0:R].transpose(1, 0, 2)), dtw_t=f(a["L1_conv_dt_proj_w"].transpose(2, 0, 1)),
        xp_t=f(xp.transpose(2, 0, 1).reshape(C, 2 * NX)), alog_t=f(a["L1_conv_A_logs"].reshape(2, C).T),
        ds_t=f(a["L1_conv_Ds"].reshape(2, C).T), dtb=f(a["L1_conv_dt_proj_b"].reshape(1, 2, C)),
        in_w_t=f(a["L1_conv_in_proj_w"].T), wo_t=f(a["L1_conv_out_proj_w"].T),
        onwb=f(np.stack([a["L1_conv_out_norm_w"], a["L1_conv_out_norm_b"]], axis=1)),
        scale_w=col(a["L1_conv_scale_w"]), conv_w=f(a["L1_conv_conv_w"].reshape(C * 9)), conv_b=f(a["L1_conv_conv_b"]))
    cw, cbias = a["L1_conv_conv_w"].reshape(C // SEAM, SEAM, 9), a["L1_conv_conv_b"].reshape(C // SEAM, SEAM)
    out.update(seam_taps=f(np.repeat(cw.transpose(1, 0, 2), B * 4, axis=0)),
               seam_cb=f(np.repeat(cbias.T, B * 2, axis=0)))
    out.update(unit_constants())
    return {"in_" + n: v for n, v in out.items()}


def kernel(**inputs):
    import concourse.bacc as bacc
    from concourse.bass_utils import run_bass_kernel_spmd

    nc = bacc.Bacc("TRN2", target_bir_lowering=False, num_devices=1)
    sent = arrays(inputs)
    dram = {n[3:]: nc.dram_tensor(n, a.shape, mybir.dt.from_np(a.dtype), kind="ExternalInput").ap()
            for n, a in sent.items()}
    dram["out"] = nc.dram_tensor("out", (B, C, H, W), F32, kind="ExternalOutput").ap()
    declare(nc, dram)
    program(nc, dram)
    return run_bass_kernel_spmd(nc, [sent], core_ids=[0]).results[0]["out"]
```
